# Optimizing a Trainium2 kernel written in Bass

```python
import numpy as np
import jax
import jax.numpy as jnp

def _softmax(x, axis=-1):
    return jax.nn.softmax(x, axis=axis)

def _gelu(x):
    return jax.nn.gelu(x, approximate=True)

def _silu(x):
    return jax.nn.silu(x)

def _sigmoid(x):
    return jax.nn.sigmoid(x)

def _layernorm(x, axis=-1, eps=1e-05):
    m = jnp.mean(x, axis=axis, keepdims=True)
    v = jnp.var(x, axis=axis, keepdims=True)
    return (x - m) / jnp.sqrt(v + eps)

def _scatter_add(tgt, idx, src, axis=0):
    return tgt.at[idx].add(src)

def _segment_sum(src, seg, n):
    return jax.ops.segment_sum(src, seg, n)
kernel_name = 'mk_xattn_ffn_d4_seqx_r8_7108c0'

def setup_inputs(seed: int=0):
    np.random.seed(seed)
    _w = jnp.asarray

    def _rec_inputs():
        import jax
        import jax.numpy as jnp
        _rk = jax.random.key(seed)
        x = 7.22e-05 + 1 * jax.random.normal(jax.random.fold_in(_rk, 1), (4, 512, 128), jnp.float32)
        _lenS = 512 - jax.random.randint(jax.random.fold_in(_rk, 7), (4,), 0, max(1, 512 // 4) + 1, jnp.int32)
        _lenS2 = 77 - jax.random.randint(jax.random.fold_in(_rk, 8), (4,), 0, max(1, 77 // 4) + 1, jnp.int32)
        _ctx_1024P = jax.random.normal(jax.random.fold_in(_rk, 11), (4, 16, 128), jnp.float32)
        _ctx_1024c = jax.random.dirichlet(jax.random.fold_in(_rk, 511), 0.3 * jnp.ones((16,), jnp.float32), (4, 77))
        _ctx_1024t = jnp.einsum('bsk,bkd->bsd', _ctx_1024c, _ctx_1024P)
        _ctx_1024t = _ctx_1024t * jax.lax.rsqrt(jnp.mean(jnp.square(_ctx_1024t)) + 1e-12) * 0.953939
        ctx_1024 = -1.39393e-06 + 0.999914 * (_ctx_1024t + 0.3 * jax.random.normal(jax.random.fold_in(_rk, 611), (4, 77, 128), jnp.float32))
        _validS = jnp.arange(512)[None, :] < _lenS[:, None]
        _validS2 = jnp.arange(77)[None, :] < _lenS2[:, None]
        _causal = jnp.tril(jnp.ones((512, 512), dtype=bool))
        mask_BxS2_bk0 = jnp.logical_not(jnp.broadcast_to(_validS2[:, :], (4, 77)))
        return (x, ctx_1024, mask_BxS2_bk0)
    x, ctx_1024, mask_BxS2_bk0 = _rec_inputs()

    def _L0_xattn_setup():
        import jax, jax.numpy as jnp
        import numpy as np
        HEADS = 16
        DIM_HEAD = 64
        QUERY_DIM = 128
        CONTEXT_DIM = 128
        D_ATTN = HEADS * DIM_HEAD
        SCALE = DIM_HEAD ** (-0.5)
        key = jax.random.key(seed)
        ks = jax.random.split(key, 7)
        B, N, M = (4, 256, 128)
        x = jax.random.normal(ks[0], (B, N, QUERY_DIM), dtype=jnp.float32)
        context = jax.random.normal(ks[1], (B, M, CONTEXT_DIM), dtype=jnp.float32)
        s = 0.02
        Wq = jax.random.normal(ks[2], (QUERY_DIM, D_ATTN), dtype=jnp.float32) * s
        Wk = jax.random.normal(ks[3], (CONTEXT_DIM, D_ATTN), dtype=jnp.float32) * s
        Wv = jax.random.normal(ks[4], (CONTEXT_DIM, D_ATTN), dtype=jnp.float32) * s
        Wo = jax.random.normal(ks[5], (D_ATTN, QUERY_DIM), dtype=jnp.float32) * s
        bo = jax.random.normal(ks[6], (QUERY_DIM,), dtype=jnp.float32) * s
        return {'x': x, 'context': context, 'Wq': Wq, 'Wk': Wk, 'Wv': Wv, 'Wo': Wo, 'bo': bo}
    _L0_xattn_all = _L0_xattn_setup()
    _L0_xattn_in = {k: v for k, v in _L0_xattn_all.items() if k in ('Wq', 'Wk', 'Wv', 'Wo', 'bo')}
    del _L0_xattn_all

    def _L0_ffn_setup():
        import jax, jax.numpy as jnp
        import numpy as np
        B, S, H, I, E, K = (4, 256, 128, 128, 8, 2)
        LIMIT = 7.0
        ALPHA = 1.702
        EPS = 1e-05
        key = jax.random.key(seed)
        ks = jax.random.split(key, 5)
        x = jax.random.normal(ks[0], (B, S, H), dtype=jnp.float32)
        norm_weight = jnp.ones((H,), dtype=jnp.float32)
        gate_weight = (jax.random.normal(ks[1], (E, H), dtype=jnp.float32) / np.sqrt(H)).astype(jnp.bfloat16)
        gate_bias = jnp.zeros((E,), dtype=jnp.bfloat16)
        mlp1_weight = (jax.random.normal(ks[2], (E, 2 * I, H), dtype=jnp.float32) / np.sqrt(H)).astype(jnp.bfloat16)
        mlp1_bias = jnp.zeros((E, 2 * I), dtype=jnp.bfloat16)
        mlp2_weight = (jax.random.normal(ks[3], (E, H, I), dtype=jnp.float32) / np.sqrt(I)).astype(jnp.bfloat16)
        mlp2_bias = jnp.zeros((E, H), dtype=jnp.bfloat16)
        return {'x': x, 'norm_weight': norm_weight, 'gate_weight': gate_weight, 'gate_bias': gate_bias, 'mlp1_weight': mlp1_weight, 'mlp1_bias': mlp1_bias, 'mlp2_weight': mlp2_weight, 'mlp2_bias': mlp2_bias}
    _L0_ffn_all = _L0_ffn_setup()
    _L0_ffn_in = {k: v for k, v in _L0_ffn_all.items() if k in ('norm_weight', 'gate_weight', 'gate_bias', 'mlp1_weight', 'mlp1_bias', 'mlp2_weight', 'mlp2_bias')}
    del _L0_ffn_all

    def _L1_xattn_setup():
        import jax, jax.numpy as jnp
        import numpy as np
        D_MODEL = 128
        NUM_HEADS = 16
        DEPTH = D_MODEL // NUM_HEADS

        def _split_heads(x):
            B, S, _ = x.shape
            return x.reshape(B, S, NUM_HEADS, DEPTH).transpose(0, 2, 1, 3)
        key = jax.random.key(seed)
        ks = jax.random.split(key, 11)
        B, S = (4, 256)
        scale = 1.0 / np.sqrt(D_MODEL)
        inp = {'v': jax.random.normal(ks[0], (B, S, D_MODEL), jnp.float32), 'k': jax.random.normal(ks[1], (B, S, D_MODEL), jnp.float32), 'q': jax.random.normal(ks[2], (B, S, D_MODEL), jnp.float32), 'wq_w': jax.random.normal(ks[3], (D_MODEL, D_MODEL), jnp.float32) * scale, 'wq_b': jnp.zeros((D_MODEL,), jnp.float32), 'wk_w': jax.random.normal(ks[4], (D_MODEL, D_MODEL), jnp.float32) * scale, 'wk_b': jnp.zeros((D_MODEL,), jnp.float32), 'wv_w': jax.random.normal(ks[5], (D_MODEL, D_MODEL), jnp.float32) * scale, 'wv_b': jnp.zeros((D_MODEL,), jnp.float32), 'dense_w': jax.random.normal(ks[6], (D_MODEL, D_MODEL), jnp.float32) * scale, 'dense_b': jnp.zeros((D_MODEL,), jnp.float32)}
        return inp
    _L1_xattn_all = _L1_xattn_setup()
    _L1_xattn_in = {k: v for k, v in _L1_xattn_all.items() if k in ('wq_w', 'wq_b', 'wk_w', 'wk_b', 'wv_w', 'wv_b', 'dense_w', 'dense_b')}
    del _L1_xattn_all

    def _L1_ffn_setup():
        import math
        import jax, jax.numpy as jnp
        import numpy as np
        B, S, D, F, E = (8, 256, 128, 512, 8)
        CAPACITY_FACTOR = 1.0
        key = jax.random.key(seed)
        k1, k2, k3, k4 = jax.random.split(key, 4)
        x = jax.random.normal(k1, (B, S, D), dtype=jnp.float32)
        Wr = jax.random.normal(k2, (D, E), dtype=jnp.float32) * (1.0 / math.sqrt(D))
        W1 = jax.random.normal(k3, (E, D, F), dtype=jnp.float32) * (1.0 / math.sqrt(D))
        W2 = jax.random.normal(k4, (E, F, D), dtype=jnp.float32) * (1.0 / math.sqrt(F))
        return {'x': x, 'Wr': Wr, 'W1': W1, 'W2': W2}
    _L1_ffn_all = _L1_ffn_setup()
    _L1_ffn_in = {k: v for k, v in _L1_ffn_all.items() if k in ('Wr', 'W1', 'W2')}
    del _L1_ffn_all

    def _L2_xattn_setup():
        import jax, jax.numpy as jnp
        import numpy as np
        D1, D2, D3 = (128, 128, 128)
        key = jax.random.key(seed)
        k1, k2, kw, kb = jax.random.split(key, 4)
        x1 = jax.random.normal(k1, (8, 256, D1), dtype=jnp.float32)
        x2 = jax.random.normal(k2, (8, 256, D2), dtype=jnp.float32)
        bound = 1.0 / np.sqrt(D1 + D2)
        W = jax.random.uniform(kw, (D3, D1 + D2), minval=-bound, maxval=bound, dtype=jnp.float32)
        b = jax.random.uniform(kb, (D3,), minval=-bound, maxval=bound, dtype=jnp.float32)
        return {'x1': x1, 'x2': x2, 'W': W, 'b': b}
    _L2_xattn_all = _L2_xattn_setup()
    _L2_xattn_in = {k: v for k, v in _L2_xattn_all.items() if k in ('W', 'b')}
    del _L2_xattn_all

    def _L2_ffn_setup():
        import jax, jax.numpy as jnp
        import numpy as np
        HIDDEN = 128
        NUM_EXPERTS = 8
        TOP_K = 2
        B, S = (2, 256)
        key = jax.random.key(seed)
        k1, k2, k3, k4, k5 = jax.random.split(key, 5)
        d, dff, E = (HIDDEN, 4 * HIDDEN, NUM_EXPERTS)
        x = jax.random.normal(k1, (B, S, d), dtype=jnp.float32)
        W1 = jax.random.normal(k2, (E, d, dff), dtype=jnp.float32) * (1.0 / np.sqrt(d))
        b1 = jax.random.normal(k3, (E, dff), dtype=jnp.float32) * 0.01
        W2 = jax.random.normal(k4, (E, dff, d), dtype=jnp.float32) * (1.0 / np.sqrt(dff))
        b2 = jax.random.normal(k5, (E, d), dtype=jnp.float32) * 0.01
        return {'x': x, 'W1': W1, 'b1': b1, 'W2': W2, 'b2': b2}
    _L2_ffn_all = _L2_ffn_setup()
    _L2_ffn_in = {k: v for k, v in _L2_ffn_all.items() if k in ('W1', 'b1', 'W2', 'b2')}
    del _L2_ffn_all

    def _L3_xattn_setup():
        import jax, jax.numpy as jnp
        import numpy as np
        B, L1, L2, H = (16, 256, 256, 128)
        key = jax.random.key(seed)
        kx, ky, km, kw, kb = jax.random.split(key, 5)
        x = jax.random.normal(kx, (B, L1, H), dtype=jnp.float32)
        y = jax.random.normal(ky, (B, L2, H), dtype=jnp.float32)
        y_mask = jax.random.randint(km, (B, L2), 0, 8) == 0
        stdv = 1.0 / np.sqrt(H)
        W = jax.random.uniform(kw, (H, H), minval=-stdv, maxval=stdv, dtype=jnp.float32)
        b = jax.random.uniform(kb, (H,), minval=-stdv, maxval=stdv, dtype=jnp.float32)
        return {'x': x, 'y': y, 'y_mask': y_mask, 'W': W, 'b': b}
    _L3_xattn_all = _L3_xattn_setup()
    _L3_xattn_in = {k: v for k, v in _L3_xattn_all.items() if k in ('W', 'b')}
    del _L3_xattn_all

    def _L3_ffn_setup():
        import jax, jax.numpy as jnp
        import numpy as np
        DIM = 128
        HIDDEN = 128
        NUM_EXPERTS = 8
        TOP_K = 2
        key = jax.random.key(seed)
        ks = jax.random.split(key, 8)
        std = 0.02
        x = jax.random.normal(ks[0], (2, 128, DIM), dtype=jnp.float32)
        gate_w = jax.random.normal(ks[1], (NUM_EXPERTS, DIM), dtype=jnp.float32) * std
        w1 = jax.random.normal(ks[2], (NUM_EXPERTS, DIM, HIDDEN), dtype=jnp.float32) * std
        w2 = jax.random.normal(ks[3], (NUM_EXPERTS, HIDDEN, DIM), dtype=jnp.float32) * std
        w3 = jax.random.normal(ks[4], (NUM_EXPERTS, DIM, HIDDEN), dtype=jnp.float32) * std
        w1s = jax.random.normal(ks[5], (1, DIM, HIDDEN), dtype=jnp.float32) * std
        w2s = jax.random.normal(ks[6], (1, HIDDEN, DIM), dtype=jnp.float32) * std
        w3s = jax.random.normal(ks[7], (1, DIM, HIDDEN), dtype=jnp.float32) * std
        return {'x': x, 'gate_w': gate_w, 'w1': w1, 'w2': w2, 'w3': w3, 'w1s': w1s, 'w2s': w2s, 'w3s': w3s}
    _L3_ffn_all = _L3_ffn_setup()
    _L3_ffn_in = {k: v for k, v in _L3_ffn_all.items() if k in ('gate_w', 'w1', 'w2', 'w3', 'w1s', 'w2s', 'w3s')}
    del _L3_ffn_all
    return {'x': x, 'ctx_1024': ctx_1024, 'mask_BxS2_bk0': mask_BxS2_bk0, 'L0_xattn_Wq': _L0_xattn_in['Wq'], 'L0_xattn_Wk': _L0_xattn_in['Wk'], 'L0_xattn_Wv': _L0_xattn_in['Wv'], 'L0_xattn_Wo': _L0_xattn_in['Wo'], 'L0_xattn_bo': _L0_xattn_in['bo'], 'L0_ffn_norm_weight': _L0_ffn_in['norm_weight'], 'L0_ffn_gate_weight': _L0_ffn_in['gate_weight'], 'L0_ffn_gate_bias': _L0_ffn_in['gate_bias'], 'L0_ffn_mlp1_weight': _L0_ffn_in['mlp1_weight'], 'L0_ffn_mlp1_bias': _L0_ffn_in['mlp1_bias'], 'L0_ffn_mlp2_weight': _L0_ffn_in['mlp2_weight'], 'L0_ffn_mlp2_bias': _L0_ffn_in['mlp2_bias'], 'L1_xattn_wq_w': _L1_xattn_in['wq_w'], 'L1_xattn_wq_b': _L1_xattn_in['wq_b'], 'L1_xattn_wk_w': _L1_xattn_in['wk_w'], 'L1_xattn_wk_b': _L1_xattn_in['wk_b'], 'L1_xattn_wv_w': _L1_xattn_in['wv_w'], 'L1_xattn_wv_b': _L1_xattn_in['wv_b'], 'L1_xattn_dense_w': _L1_xattn_in['dense_w'], 'L1_xattn_dense_b': _L1_xattn_in['dense_b'], 'L1_ffn_Wr': _L1_ffn_in['Wr'], 'L1_ffn_W1': _L1_ffn_in['W1'], 'L1_ffn_W2': _L1_ffn_in['W2'], 'L2_xattn_W': _L2_xattn_in['W'], 'L2_xattn_b': _L2_xattn_in['b'], 'L2_ffn_W1': _L2_ffn_in['W1'], 'L2_ffn_b1': _L2_ffn_in['b1'], 'L2_ffn_W2': _L2_ffn_in['W2'], 'L2_ffn_b2': _L2_ffn_in['b2'], 'L3_xattn_W': _L3_xattn_in['W'], 'L3_xattn_b': _L3_xattn_in['b'], 'L3_ffn_gate_w': _L3_ffn_in['gate_w'], 'L3_ffn_w1': _L3_ffn_in['w1'], 'L3_ffn_w2': _L3_ffn_in['w2'], 'L3_ffn_w3': _L3_ffn_in['w3'], 'L3_ffn_w1s': _L3_ffn_in['w1s'], 'L3_ffn_w2s': _L3_ffn_in['w2s'], 'L3_ffn_w3s': _L3_ffn_in['w3s']}

def reference(x, ctx_1024, mask_BxS2_bk0, L0_xattn_Wq, L0_xattn_Wk, L0_xattn_Wv, L0_xattn_Wo, L0_xattn_bo, L0_ffn_norm_weight, L0_ffn_gate_weight, L0_ffn_gate_bias, L0_ffn_mlp1_weight, L0_ffn_mlp1_bias, L0_ffn_mlp2_weight, L0_ffn_mlp2_bias, L1_xattn_wq_w, L1_xattn_wq_b, L1_xattn_wk_w, L1_xattn_wk_b, L1_xattn_wv_w, L1_xattn_wv_b, L1_xattn_dense_w, L1_xattn_dense_b, L1_ffn_Wr, L1_ffn_W1, L1_ffn_W2, L2_xattn_W, L2_xattn_b, L2_ffn_W1, L2_ffn_b1, L2_ffn_W2, L2_ffn_b2, L3_xattn_W, L3_xattn_b, L3_ffn_gate_w, L3_ffn_w1, L3_ffn_w2, L3_ffn_w3, L3_ffn_w1s, L3_ffn_w2s, L3_ffn_w3s):
    import jax
    import jax.numpy as jnp

    def _L0_xattn_ref(x, context, Wq, Wk, Wv, Wo, bo):
        import jax, jax.numpy as jnp
        import numpy as np
        HEADS = 16
        DIM_HEAD = 64
        QUERY_DIM = 128
        CONTEXT_DIM = 128
        D_ATTN = HEADS * DIM_HEAD
        SCALE = DIM_HEAD ** (-0.5)
        B, N, _ = x.shape
        M = context.shape[1]
        Q = (x @ Wq).reshape(B, N, HEADS, DIM_HEAD)
        K = (context @ Wk).reshape(B, M, HEADS, DIM_HEAD)
        V = (context @ Wv).reshape(B, M, HEADS, DIM_HEAD)
        scores = jnp.einsum('bqhd,bmhd->bqhm', Q, K) * SCALE
        attn = jax.nn.softmax(scores, axis=-1)
        out = jnp.einsum('bqhm,bmhd->bqhd', attn, V)
        out = out.reshape(B, N, D_ATTN)
        return out @ Wo + bo

    def _L0_ffn_ref(x, norm_weight, gate_weight, gate_bias, mlp1_weight, mlp1_bias, mlp2_weight, mlp2_bias):
        import jax, jax.numpy as jnp
        import numpy as np
        B, S, H, I, E, K = (4, 256, 128, 128, 8, 2)
        LIMIT = 7.0
        ALPHA = 1.702
        EPS = 1e-05
        xc = x.astype(jnp.bfloat16)
        xf = xc.astype(jnp.float32)
        rms = jnp.mean(xf * xf, axis=-1, keepdims=True)
        normed = (xf * jax.lax.rsqrt(rms + EPS) * norm_weight).astype(jnp.bfloat16)
        nf = normed.astype(jnp.float32)
        logits = (jnp.einsum('bsh,eh->bse', nf, gate_weight.astype(jnp.float32)) + gate_bias.astype(jnp.float32)).astype(jnp.bfloat16).astype(jnp.float32)
        scores, idx = jax.lax.top_k(logits, K)
        w = jax.nn.softmax(scores, axis=-1)
        combine = jnp.sum(jax.nn.one_hot(idx, E, dtype=jnp.float32) * w[..., None], axis=-2)
        p1 = jnp.einsum('bsh,eoh->bseo', nf, mlp1_weight.astype(jnp.float32)) + mlp1_bias.astype(jnp.float32)
        g = jnp.minimum(p1[..., 0::2], LIMIT)
        lin = jnp.clip(p1[..., 1::2], -LIMIT, LIMIT)
        act = g * jax.nn.sigmoid(ALPHA * g) * (lin + 1.0)
        p2 = jnp.einsum('bsei,ehi->bseh', act, mlp2_weight.astype(jnp.float32)) + mlp2_bias.astype(jnp.float32)
        combined = jnp.einsum('bseh,bse->bsh', p2, combine)
        out = (xc + combined.astype(jnp.bfloat16)).astype(x.dtype)
        return out

    def _L1_xattn_ref(v, k, q, wq_w, wq_b, wk_w, wk_b, wv_w, wv_b, dense_w, dense_b):
        import jax, jax.numpy as jnp
        import numpy as np
        D_MODEL = 128
        NUM_HEADS = 16
        DEPTH = D_MODEL // NUM_HEADS

        def _split_heads(x):
            B, S, _ = x.shape
            return x.reshape(B, S, NUM_HEADS, DEPTH).transpose(0, 2, 1, 3)
        B, S, _ = q.shape
        qh = _split_heads(q @ wq_w.T + wq_b)
        kh = _split_heads(k @ wk_w.T + wk_b)
        vh = _split_heads(v @ wv_w.T + wv_b)
        scale = 1.0 / jnp.sqrt(jnp.float32(DEPTH))
        logits = jnp.einsum('bhqd,bhkd->bhqk', qh, kh) * scale
        attn = jax.nn.softmax(logits, axis=-1)
        out = jnp.einsum('bhqk,bhkd->bhqd', attn, vh)
        out = out.transpose(0, 2, 1, 3).reshape(B, S, D_MODEL)
        return out @ dense_w.T + dense_b

    def _L1_ffn_ref(x, Wr, W1, W2):
        import math
        import jax, jax.numpy as jnp
        import numpy as np
        B, S, D, F, E = (8, 256, 128, 512, 8)
        CAPACITY_FACTOR = 1.0
        b, s, d = x.shape
        t = b * s
        cap = max(math.ceil(t * CAPACITY_FACTOR / E), 1)
        xf = x.reshape(t, d)
        probs = jax.nn.softmax(xf.astype(jnp.float32) @ Wr, axis=-1)
        eidx = jnp.argmax(probs, axis=-1)
        p_tok = jnp.take_along_axis(probs, eidx[:, None], axis=1)[:, 0]
        onehot = jax.nn.one_hot(eidx, E, dtype=jnp.int32)
        rank_all = jnp.cumsum(onehot, axis=0) - onehot
        rank = jnp.take_along_axis(rank_all, eidx[:, None], axis=1)[:, 0]
        keep = rank < cap
        slot = jnp.where(keep, rank, cap)
        dispatch = jnp.zeros((E, cap + 1), dtype=jnp.int32).at[eidx, slot].set(jnp.arange(t, dtype=jnp.int32))
        valid = jnp.zeros((E, cap + 1), dtype=bool).at[eidx, slot].set(keep)
        dispatch = dispatch[:, :cap]
        valid = valid[:, :cap]
        xe = xf[dispatch]
        h = jnp.maximum(jnp.einsum('ecd,edf->ecf', xe, W1), 0.0)
        ye = jnp.einsum('ecf,efd->ecd', h, W2)
        pe = p_tok[dispatch]
        ye = ye * (pe * valid.astype(ye.dtype))[:, :, None]
        y = jnp.zeros((t, d), dtype=x.dtype).at[dispatch.reshape(-1)].add(ye.reshape(E * cap, d).astype(x.dtype))
        return y.reshape(b, s, d)

    def _L2_xattn_ref(x1, x2, W, b):
        import jax, jax.numpy as jnp
        import numpy as np
        D1, D2, D3 = (128, 128, 128)
        d1 = x1.shape[-1]
        W1 = W[:, :d1]
        W2 = W[:, d1:]
        part1 = jnp.einsum('bld,ed->ble', x1, W1)
        part2 = jnp.einsum('bld,ed->be', x2, W2) / x2.shape[1]
        return part1 + part2[:, None, :] + b

    def _L2_ffn_ref(x, W1, b1, W2, b2):
        import jax, jax.numpy as jnp
        import numpy as np
        HIDDEN = 128
        NUM_EXPERTS = 8
        TOP_K = 2
        B, S = (2, 256)
        Bm, Sm, d = x.shape
        E = W1.shape[0]
        x_flat = x.reshape(-1, d)
        h = jnp.mod(x_flat[:, :TOP_K].sum(axis=1).astype(jnp.int32), E)
        sel = jnp.stack([h, jnp.mod(h + 1, E)], axis=1)

        def step(acc, params):
            e, W1e, b1e, W2e, b2e = params
            w = jnp.any(sel == e, axis=1).astype(x.dtype) / TOP_K
            y = jnp.maximum(x_flat @ W1e + b1e, 0.0) @ W2e + b2e
            return (acc + w[:, None] * y, None)
        init = jnp.zeros_like(x_flat)
        out_flat, _ = jax.lax.scan(step, init, (jnp.arange(E), W1, b1, W2, b2))
        return out_flat.reshape(Bm, Sm, d)

    def _L3_xattn_ref(x, y, y_mask, W, b):
        import jax, jax.numpy as jnp
        import numpy as np
        B, L1, L2, H = (16, 256, 256, 128)
        x_proj = jax.nn.relu(jnp.einsum('bih,oh->bio', x, W) + b)
        y_proj = jax.nn.relu(jnp.einsum('bjh,oh->bjo', y, W) + b)
        scores = jnp.einsum('bih,bjh->bij', x_proj, y_proj)
        scores = jnp.where(y_mask[:, None, :], -jnp.inf, scores)
        alpha = jax.nn.softmax(scores, axis=-1)
        matched_seq = jnp.einsum('bij,bjh->bih', alpha, y)
        return matched_seq

    def _L3_ffn_ref(x, gate_w, w1, w2, w3, w1s, w2s, w3s):
        import jax, jax.numpy as jnp
        import numpy as np
        DIM = 128
        HIDDEN = 128
        NUM_EXPERTS = 8
        TOP_K = 2
        bs, slen, dim = x.shape
        xt = x.reshape(bs * slen, dim)
        logits = xt @ gate_w.T
        scores = jax.nn.softmax(logits.astype(jnp.float32), axis=1).astype(x.dtype)
        top_scores, sel = jax.lax.top_k(scores, TOP_K)
        sel_flat = sel.reshape(-1)
        order = jnp.argsort(sel_flat, stable=True)
        top_scores_sorted = top_scores.reshape(-1)[order]
        token_idx = order // TOP_K
        eid = sel_flat[order]
        routed_in = xt[token_idx] * top_scores_sorted[:, None]
        out_routed = jnp.zeros_like(routed_in)
        for e in range(NUM_EXPERTS):
            m = (eid == e)[:, None]
            xe = jnp.where(m, routed_in, 0.0)
            h = jax.nn.silu(xe @ w1[e]) * (xe @ w3[e])
            out_routed = out_routed + jnp.where(m, h @ w2[e], 0.0)
        hs = jax.nn.silu(xt @ w1s[0]) * (xt @ w3s[0])
        out = hs @ w2s[0]
        out = out.at[token_idx].add(out_routed)
        return out.reshape(bs, slen, dim)
    x = x + _L0_xattn_ref(_layernorm(x, axis=-1), ctx_1024, L0_xattn_Wq, L0_xattn_Wk, L0_xattn_Wv, L0_xattn_Wo, L0_xattn_bo)
    x = x + _L0_ffn_ref(_layernorm(x, axis=-1), L0_ffn_norm_weight, L0_ffn_gate_weight, L0_ffn_gate_bias, L0_ffn_mlp1_weight, L0_ffn_mlp1_bias, L0_ffn_mlp2_weight, L0_ffn_mlp2_bias)
    x = x + _L1_xattn_ref(ctx_1024, ctx_1024, _layernorm(x, axis=-1), L1_xattn_wq_w, L1_xattn_wq_b, L1_xattn_wk_w, L1_xattn_wk_b, L1_xattn_wv_w, L1_xattn_wv_b, L1_xattn_dense_w, L1_xattn_dense_b)
    x = x + _L1_ffn_ref(_layernorm(x, axis=-1), L1_ffn_Wr, L1_ffn_W1, L1_ffn_W2)
    x = x + _L2_xattn_ref(_layernorm(x, axis=-1), ctx_1024, L2_xattn_W, L2_xattn_b)
    x = x + _L2_ffn_ref(_layernorm(x, axis=-1), L2_ffn_W1, L2_ffn_b1, L2_ffn_W2, L2_ffn_b2)
    x = x + _L3_xattn_ref(_layernorm(x, axis=-1), ctx_1024, mask_BxS2_bk0, L3_xattn_W, L3_xattn_b)
    x = x + _L3_ffn_ref(_layernorm(x, axis=-1), L3_ffn_gate_w, L3_ffn_w1, L3_ffn_w2, L3_ffn_w3, L3_ffn_w1s, L3_ffn_w2s, L3_ffn_w3s)
    return x

_drawn_inputs = setup_inputs


def setup_inputs(seed=0):
    import zlib

    import numpy as np

    out = dict(_drawn_inputs(seed))
    spreads = {'L0_ffn_norm_weight': (1.0, 0.2),
     'L0_ffn_gate_bias': (0.0, 0.1),
     'L0_ffn_mlp1_bias': (0.0, 0.1),
     'L0_ffn_mlp2_bias': (0.0, 0.1),
     'L1_xattn_wq_b': (0.0, 0.1),
     'L1_xattn_wk_b': (0.0, 0.8),
     'L1_xattn_wv_b': (0.0, 0.1),
     'L1_xattn_dense_b': (0.0, 0.1)}
    factors = {'L0_xattn_Wq': 5.088,
     'L0_xattn_Wk': 5.32,
     'L2_xattn_b': 3.084,
     'L2_ffn_b1': 8.0,
     'L2_ffn_b2': 8.0,
     'L3_ffn_gate_w': 8.0,
     'L3_ffn_w1': 8.0,
     'L3_ffn_w2': 8.0,
     'L3_ffn_w3': 8.0,
     'L3_ffn_w1s': 8.0,
     'L3_ffn_w2s': 8.0,
     'L3_ffn_w3s': 8.0}
    for name, (base, spread) in spreads.items():
        noise = np.random.default_rng([zlib.crc32(name.encode()), seed]).standard_normal(out[name].shape)
        drawn = base * np.exp(spread * noise) if base else spread * noise
        out[name] = jnp.asarray(drawn.astype(out[name].dtype))
    for name, factor in factors.items():
        out[name] = (out[name] * factor).astype(out[name].dtype)
    return out
```

```python
import numpy as np
import concourse.bass as bass
from concourse import mybir
from contextlib import ExitStack

F32 = mybir.dt.float32
BF16 = mybir.dt.bfloat16
U8 = mybir.dt.uint8
U32 = mybir.dt.uint32
I32 = mybir.dt.int32
ALU = mybir.AluOpType
ACT = mybir.ActivationFunctionType
AXX = mybir.AxisListType.X

P = 128
B, SEQ, D = 4, 512, 128
G, J = B, SEQ // P
T = G * J
M = 77
H = 16
DH0, DH1 = 64, D // H
HM = H * M
NK = -(-HM // P)
CH = [min(P, HM - P * k) for k in range(NK)]
HEADS = [(0, 5), (5, 10), (10, 16)]
E = 8
F = 512
FC = F // P
CAP = T * P // E
LN_EPS = 1e-5
LIMIT, ALPHA = 7.0, 1.702
MASKED = -1e30
NU = 5 * J

STAGES = ["a0", "f0", "a1", "f1", "a2", "f2", "a3", "f3"]
HEADED = ["a0", "a1"]
SIGNALS = {k: [(s, G) for s in STAGES] for k in ("st", "mv", "ve", "rstd", "ln", "xt", "xte")}
SIGNALS |= {k: [(s, 3 * T) for s in HEADED] + [("a3", G)] for k in ("sc", "sub", "pt")}
SIGNALS |= {k: [(s, T) for s in HEADED] + [("a2", G), ("a3", G)] for k in ("out",)}
SIGNALS |= {k: [(s, T) for s in HEADED] for k in ("sm", "rs", "p")}
SIGNALS |= {"mx": [(s, 3 * T) for s in HEADED], "exp": [("a0", T), ("a1", T), ("a3", G)],
            "pte": [("a0", 4 * T), ("a1", 4 * T), ("a3", G)], "xb": [("a0", G), ("a1", G), ("a2", G)],
            "x": [("a0", T), ("f0", G), ("a1", T), ("a2", G), ("a3", T), ("f3", T)],
            "q": [("a1", G), ("a3", G)], "qe": [("a1", G), ("a3", G)],
            "lg": [("f0", G), ("f1", G), ("f3", G)], "lge": [("f0", G), ("f1", G), ("f3", G)],
            "gap": [("f0", G), ("f1", G), ("a3", G), ("f3", G)], "gexp": [("f0", G), ("f1", G), ("f3", G)],
            "acc": [("f0", E * G), ("f1", E * G), ("f2", E * G)],
            "h": [("f1", E * FC * G), ("f2", E * FC * G)],
            "dn": [("f0", E * G), ("f1", E * FC * G), ("f2", E * FC * G), ("f3", NU * G)],
            "up": [("f0", E * G), ("f1", E * FC * G), ("f2", E * FC * G), ("f3", NU * G)]}
SIGNALS |= {k: [("f0", G), ("f2", G)] for k in ("cs", "ct", "cte", "b2", "b2e")}


HORD = [0, 2, 4, 6, 1, 3, 5, 7, 8, 10, 12, 14, 9, 11, 13, 15]


FROM_ONE = ["acc", "dn", "h", "lg", "lge", "cte", "b2", "b2e", "f0_act", "f0_gb", "f0_lb", "f0_sg", "f0_gl",
            "f1_rk", "f1_rke", "f3_prod", "f3_hte", "f3_ht"]


class Steps:

    def __init__(self, eng, sem, base=0):
        self.eng, self.sem, self.base, self.n = eng, sem, base, 0

    def __call__(self, ins):
        self.n += 1
        ins.then_inc(self.sem, 1)
        self.eng.wait_ge(self.sem, self.base + self.n)


def build(nc, A, out):
    ctx = ExitStack()
    with ctx:
        def sb(name, shape, dt=F32):
            return ctx.enter_context(nc.sbuf_tensor(name, shape, dt))

        sems = {}

        def sem(name):
            stage, _, signal = name.partition("_")
            if stage in STAGES and signal in SIGNALS:
                name = signal
            if name not in sems:
                sems[name] = ctx.enter_context(nc.semaphore(name))
            return sems[name]

        def at(name, n):
            stage, _, signal = name.partition("_")
            base = 1 if name in FROM_ONE or (stage in STAGES and signal in FROM_ONE) else 0
            for s, count in SIGNALS.get(signal, ()) if stage in STAGES else ():
                if s == stage:
                    return sem(name), n + base
                base += count
            assert stage not in STAGES or signal not in SIGNALS, name
            return sem(name), n + base

        X = sb("X", [P, T, D])
        xn = sb("xn", [P, J, D])
        xnT = sb("xnT", [P, G, SEQ])
        grpT = sb("grpT", [P, J, P])
        queT = sb("queT", [P, J, P])
        ident = sb("ident", [P, P])
        identb = sb("identb", [P, P], BF16)
        ctxr = sb("ctxr", [M, B, D])
        ctxT = sb("ctxT", [P, B * M])
        prb = sb("prb", [P, 4, HM])
        prT = sb("prT", [P, 2, NK * P])
        R1 = sb("R1", [P, B * HM + B * NK * P])
        R2 = sb("R2", [P, B * HM + B * NK * P])
        R3 = sb("R3", [P, 2 * E * F])
        keys0 = R1[:, 0:B * HM].rearrange("p (b n) -> p b n", b=B)
        vals0 = R1[:, B * HM:].rearrange("p (b k n) -> p b k n", b=B, k=NK)
        keys1 = R2[:, 0:B * HM].rearrange("p (b n) -> p b n", b=B)
        vals1 = R2[:, B * HM:].rearrange("p (b k n) -> p b k n", b=B, k=NK)
        w1_l1 = R3[:, 0:E * F].rearrange("p (e n) -> p e n", e=E)
        w2_l1 = R3[:, E * F:].rearrange("p (e c n) -> p e c n", e=E, c=FC)
        w1_l2 = R1[:, 0:E * F].rearrange("p (e n) -> p e n", e=E)
        w2_l2 = R1[:, B * HM:B * HM + E * F].rearrange("p (e c n) -> p e c n", e=E, c=FC)
        w13_l3 = R2[:, 0:9 * 256].rearrange("p (e n) -> p e n", e=9)
        w2_l3 = R2[:, 9 * 256:9 * 384].rearrange("p (e n) -> p e n", e=9)
        wq = R3[:, 0:1024]
        wk = R3[:, 1024:2048]
        wv = R3[:, 2048:3072]
        wo = R3[:, 3072:4096].rearrange("p (c n) -> p c n", c=8)
        wqT = R3[:, 4096:5120].rearrange("p (c n) -> p c n", c=8)
        kT = R3[:, 5120:5120 + 8 * B * M].rearrange("p (c n) -> p c n", c=8)
        vT = prT[:, :, :].rearrange("p a n -> p (a n)")[:, 0:8 * B * M].rearrange("p (c n) -> p c n", c=8)
        vstage = R2[0:M, 0:B * H * D].rearrange("p (b h n) -> p b h n", b=B, h=H)
        prbf = prb[:, :, :].rearrange("p a n -> p (a n)")
        kvT1 = prbf[:, 0:2 * B * M].rearrange("p (a n) -> p a n", a=2)
        vblk = prbf[:, 640:640 + 2 * HM].rearrange("p (a n) -> p a n", a=2)
        csB = prbf[:, 3200:3200 + B * P].rearrange("p (b n) -> p b n", b=B)
        acc = prbf[:, 0:T * D].rearrange("p (t n) -> p t n", t=T)
        hid = prbf[:, 2048:2048 + 4 * SEQ].rearrange("p (a n) -> p a n", a=4)
        mlpg = prT[:, 0, 0:2 * SEQ].rearrange("p (a n) -> p a n", a=2)
        mlpl = prT[:, 1, 0:2 * SEQ].rearrange("p (a n) -> p a n", a=2)

        w4r = sb("w4r", [P, 4, D])
        w4T = sb("w4T", [P, 4, D])
        w3r = sb("w3r", [P, 3, D])
        w3T = sb("w3T", [P, 3, D])
        gw3r = sb("gw3r", [E, D])
        gw3T = sb("gw3T", [P, E])
        wr1 = sb("wr1", [P, E])
        gw0r = sb("gw0r", [E, D], BF16)
        gw0T = sb("gw0T", [P, E], BF16)
        m1r = prT[:, 1, 0:1024].bitcast(BF16).rearrange("p (e n) -> p e n", e=E)
        m1T = sb("m1T", [P, E * 2, P], BF16)
        m2r = prT[:, 0, 0:512].bitcast(BF16).rearrange("p (e n) -> p e n", e=E)
        m2T = sb("m2T", [P, E, P])
        m1br = sb("m1br", [E, 2 * P], BF16)
        m1bT = sb("m1bT", [P, 2, E])
        m2b = sb("m2b", [E, D], BF16)
        m2bf = sb("m2bf", [E, D])
        b1r = sb("b1r", [E * FC, P])
        b1T = sb("b1T", [P, E * FC])
        b2r = sb("b2r", [E, D])
        nwB = sb("nwB", [P, D])
        gbB = sb("gbB", [P, E], BF16)
        boB = sb("boB", [P, 3, D])
        cols = sb("cols", [P, 4])
        rowc = sb("rowc", [P, B, D])
        ypT = sb("ypT", [P, B * M])
        maskw = sb("maskw", [P, M], I32)
        maskf = sb("maskf", [P, B, M])
        blk = sb("blk", [P, H])
        lower = sb("lower", [P, P], BF16)
        onesb = sb("onesb", [P, P], BF16)
        iota = sb("iota", [P, E])
        nhalf = sb("nhalf", [P, J])
        pad = sb("pad", [P, 1])
        st = sb("st", [P, J, 6])
        mv = sb("mv", [P, J, 2])
        ve = sb("ve", [P, J])
        rstd = sb("rstd", [P, J])
        mx = sb("mx", [P, 2, H])
        sm = sb("sm", [P, 2, H])
        rs = sb("rs", [P, 2, H])
        csum = sb("csum", [P, B])
        C9 = sb("C9", [P, J, E + 1])
        C = sb("C", [P, T, E])
        cT = sb("cT", [E, J, P])
        lg = sb("lg", [P, J, E])
        lgb = sb("lgb", [P, J, E], BF16)
        m8 = sb("m8", [P, J, E])
        i8 = sb("i8", [P, J, E], U32)
        i8f = sb("i8f", [P, J, E])
        gs = sb("gs", [P, 8, J])
        gi = sb("gi", [P, J], I32)
        eq = sb("eq", [P, 2, J, E])
        oneh = sb("oneh", [P, J, E], BF16)
        seen = sb("seen", [P, J, E], BF16)
        seenf = sb("seenf", [P, E])
        nT = sb("nT", [P, G, SEQ], BF16)
        nTg = sb("nTg", [P, J, P], BF16)
        nrm = sb("nrm", [P, J, D], BF16)
        xc = sb("xc", [P, T, D], BF16)
        xcg = sb("xcg", [P, J, D], BF16)
        accb = sb("accb", [P, J, D], BF16)
        vwd = nc.dram_tensor("vwd", [B, M, H, D], F32, kind="Internal").ap()

        bank = [ctx.enter_context(nc.psum_tensor(f"bank{i}", [P, 512], F32)) for i in range(8)]

        def b4(i):
            return bank[i][:, :].rearrange("p (j n) -> p j n", j=4)

        def bb(i):
            return bank[i][:, :].bitcast(BF16).rearrange("p (j n) -> p j n", j=8)

        block = ctx.enter_context(nc.Block())

        J_CTX, J_WQ, J_K, J_A, J_V, J_VW = 0, 1, 3, 11, 27, 35
        J_W4 = J_VW + 16
        J_K1, J_V1 = J_W4 + 1, J_W4 + 2
        J_VB = J_V1 + 1
        J_W3 = J_VB + 3 * B
        J_SM = J_W3 + 1
        J_M1 = J_SM + 1
        J_M2 = J_M1 + 2
        J_SMB = J_M2 + 1
        J_ROW = J_SMB + 1
        J_YP = J_ROW + 1
        J_END = J_YP + 1

        @block.sync
        def _(sp):
            sp.dma_start(ctxr[:, :, :], A["ctx_1024"].rearrange("b m d -> m b d")).then_inc(sem("ld_ctx"), 16)
            sp.dma_start(wq, A["L0_xattn_Wq"]).then_inc(sem("ld_wq"), 16)
            sp.dma_start(wk, A["L0_xattn_Wk"]).then_inc(sem("ld_wk"), 16)
            sp.dma_start(X[:, :, :], A["x"].rearrange("b (j p) d -> p (b j) d", p=P)).then_inc(sem("ld_x"), 16)
            sp.dma_start(wv, A["L0_xattn_Wv"]).then_inc(sem("ld_wv"), 16)
            sp.dma_start(wo, A["L0_xattn_Wo"].rearrange("(c p) n -> p c n", p=P)).then_inc(sem("ld_wo"), 16)
            for n, w in enumerate(["wq_w", "wk_w", "wv_w", "dense_w"]):
                sp.dma_start(w4r[:, n, :], A["L1_xattn_" + w]).then_inc(sem("ld_w4"), 16)
            for n, w in enumerate(["L1_xattn_wq_b", "L1_xattn_wk_b", "L1_xattn_wv_b", "L3_xattn_b"]):
                sp.dma_start(cols[:, n:n + 1], A[w].rearrange("(p a) -> p a", a=1)).then_inc(sem("ld_cols"), 16)
            for n, w in enumerate(["L0_xattn_bo", "L1_xattn_dense_b", "L2_xattn_b"]):
                sp.dma_start(boB[:, n, :], A[w].rearrange("(a n) -> a n", a=1).partition_broadcast(P)
                             ).then_inc(sem("ld_bo"), 16)
            sp.dma_start(w3r[:, 0:2, :], A["L2_xattn_W"].rearrange("p (a n) -> p a n", a=2)).then_inc(sem("ld_w3"), 16)
            sp.dma_start(w3r[:, 2, :], A["L3_xattn_W"]).then_inc(sem("ld_w3"), 16)
            sp.dma_start(gw3r[:, :], A["L3_ffn_gate_w"]).then_inc(sem("ld_small"), 16)
            sp.dma_start(b1r[:, :], A["L2_ffn_b1"].rearrange("e (c p) -> (e c) p", p=P)).then_inc(sem("ld_small"), 16)
            sp.dma_start(gw0r[:, :], A["L0_ffn_gate_weight"]).then_inc(sem("ld_small"), 16)
            sp.dma_start(m1br[:, :], A["L0_ffn_mlp1_bias"]).then_inc(sem("ld_small"), 16)
            sp.dma_start(m2b[:, :], A["L0_ffn_mlp2_bias"]).then_inc(sem("ld_later"), 16)
            sp.dma_start(b2r[:, :], A["L2_ffn_b2"]).then_inc(sem("ld_later"), 16)
            sp.dma_start(wr1[:, :], A["L1_ffn_Wr"]).then_inc(sem("ld_later"), 16)
            sp.dma_start(nwB[:, :], A["L0_ffn_norm_weight"].rearrange("(a n) -> a n", a=1).partition_broadcast(P)
                         ).then_inc(sem("ld_later"), 16)
            sp.dma_start(gbB[:, :], A["L0_ffn_gate_bias"].rearrange("(a n) -> a n", a=1).partition_broadcast(P)
                         ).then_inc(sem("ld_later"), 16)
            sp.dma_start(maskw[:, :], A["mask_BxS2_bk0"].rearrange("(a n) -> a n", a=1).partition_broadcast(P)
                         ).then_inc(sem("ld_later"), 16)
            for b in range(B):
                sp.wait_ge(*at("prep_ev", J_VW + 4 * (b + 1)))
                sp.dma_start(vwd[b, :, :, :], vstage[:, b, :, :]).then_inc(sem("vw_out"), 16)
            sp.wait_ge(*at("vw_out", 16 * B))
            for b in range(B):
                for h in range(H):
                    r = h * M
                    while r < (h + 1) * M:
                        n = min((h + 1) * M, (r // P + 1) * P) - r
                        sp.dma_start(vals0[r % P:r % P + n, b, r // P, :], vwd[b, r - h * M:r - h * M + n, h, :]
                                     ).then_inc(sem("vw_in"), 16)
                        r += n
            sp.wait_ge(*at("prep_mm", J_VW + 16))
            sp.dma_start(m1r, A["L0_ffn_mlp1_weight"].rearrange("e (i two) h -> i e (two h)", two=2)
                         ).then_inc(sem("ld_m"), 16)
            sp.dma_start(m2r, A["L0_ffn_mlp2_weight"].rearrange("e h i -> h e i")).then_inc(sem("ld_m"), 16)
            sp.dma_start(w1_l1, A["L1_ffn_W1"].rearrange("e d f -> d e f")).then_inc(sem("ld_w1_l1"), 16)
            sp.dma_start(w2_l1, A["L1_ffn_W2"].rearrange("e (c p) n -> p e c n", p=P)).then_inc(sem("ld_w2_l1"), 16)
            sp.wait_ge(*at("a0_out", T))
            sp.dma_start(w1_l2, A["L2_ffn_W1"].rearrange("e d f -> d e f")).then_inc(sem("ld_w1_l2"), 16)
            sp.dma_start(w2_l2, A["L2_ffn_W2"].rearrange("e (c p) n -> p e c n", p=P)).then_inc(sem("ld_w2_l2"), 16)
            sp.wait_ge(*at("a1_out", T))
            for n, (w1, w3, w2) in enumerate([("w1", "w3", "w2"), ("w1s", "w3s", "w2s")]):
                e0, ne = (0, E) if n == 0 else (E, 1)
                sp.dma_start(w13_l3[:, e0:e0 + ne, 0:P], A["L3_ffn_" + w1].rearrange("e d n -> d e n")
                             ).then_inc(sem("ld_w_l3"), 16)
                sp.dma_start(w13_l3[:, e0:e0 + ne, P:2 * P], A["L3_ffn_" + w3].rearrange("e d n -> d e n")
                             ).then_inc(sem("ld_w_l3"), 16)
                sp.dma_start(w2_l3[:, e0:e0 + ne, :], A["L3_ffn_" + w2].rearrange("e d n -> d e n")
                             ).then_inc(sem("ld_w_l3"), 16)
            with sp.Fori(0, G) as g:
                sp.wait_ge(*at("f3_x", J * (g + 1)))
                sp.dma_start(out.rearrange("b (j p) d -> p b j d", p=P)[:, g, :, :], X[:, :, :].rearrange(
                    "p (b j) d -> p b j d", b=B)[:, g, :, :]).then_inc(sem("stored"), 16)
            sp.wait_ge(*at("stored", 16 * G))

        NPIECE = sum((((h + 1) * M - 1) // P) - (h * M // P) + 1 for h in range(H)) * B

        @block.gpsimd
        def _(pool):
            for name in FROM_ONE:
                pool.sem_inc(sem(name), 1)
            c = Steps(pool, sem("consts"))
            c(pool.memset(ident[:, :], 0.0))
            c(pool.affine_select(out=ident[:, :], in_=ident[:, :], compare_op=ALU.not_equal, fill=1.0,
                                 base=0, pattern=[[-1, P]], channel_multiplier=1))
            c(pool.tensor_copy(identb[:, :], ident[:, :]))
            c(pool.memset(nhalf[:, :], -0.5))
            c(pool.memset(blk[:, :], 1.0))
            c(pool.affine_select(out=blk[:, :], in_=blk[:, :], compare_op=ALU.is_ge, fill=0.0,
                                 base=0, pattern=[[-DH1, H]], channel_multiplier=1))
            c(pool.affine_select(out=blk[:, :], in_=blk[:, :], compare_op=ALU.is_ge, fill=0.0,
                                 base=DH1 - 1, pattern=[[DH1, H]], channel_multiplier=-1))
            c(pool.memset(onesb[:, :], 1.0))
            c(pool.affine_select(out=lower[:, :], in_=onesb[:, :], compare_op=ALU.is_gt, fill=0.0,
                                 base=0, pattern=[[1, P]], channel_multiplier=-1))
            c(pool.iota(i8[:, 0, :].bitcast(I32), pattern=[[1, E]], base=0, channel_multiplier=0))
            c(pool.tensor_copy(iota[:, :], i8[:, 0, :].bitcast(I32)))
            pool.wait_ge(*at("ld_later", 96))
            c(pool.tensor_copy(m2bf[:, :], m2b[:, :]))
            c(pool.tensor_copy(maskf[:, :, :].rearrange("p b m -> p (b m)"), maskw[:, :].bitcast(U8)))
            assert c.n == 13

            def pow_rstd(name, g):
                pool.wait_ge(*at(name + "_ve", g + 1))
                pool.tensor_tensor(rstd[:, :], ve[:, :], nhalf[:, :], ALU.pow).then_inc(sem(name + "_rstd"), 1)

            def attention(name, bias):
                def scale(g, j):
                    t = J * g + j
                    pool.wait_ge(*at(name + "_rs", t + 1))
                    pool.tensor_tensor(prb[:, j, :].rearrange("p (h m) -> p h m", h=H),
                                       prb[:, j, :].rearrange("p (h m) -> p h m", h=H),
                                       rs[:, j % 2, :].unsqueeze(2).to_broadcast([P, H, M]),
                                       ALU.mult).then_inc(sem(name + "_p"), 1)

                def group(g, first):
                    pow_rstd(name, g)
                    pool.wait_ge(*at(name + "_ln", g + 1))
                    pool.tensor_tensor(X4(g), X4(g), boB[:, bias, :].unsqueeze(1).to_broadcast([P, J, D]),
                                       ALU.add).then_inc(sem(name + "_xb"), 1)
                    for j in range(J):
                        if not (first and j == 0):
                            scale(*((g, j - 1) if j else (g - 1, J - 1)))

                group(0, True)
                with pool.Fori(1, G) as g:
                    group(g, False)
                scale(G - 1, J - 1)

            def X4(g):
                return X[:, :, :].rearrange("p (g j) d -> p g (j d)", g=G)[:, g, :].rearrange(
                    "p (j d) -> p j d", j=J)

            pool.wait_ge(*at("ld_bo", 48))
            attention("a0", 0)
            with pool.Fori(0, G) as g:
                pow_rstd("f0", g)
                pool.wait_ge(*at("f0_ms", g + 1))
                pool.tensor_tensor(gs[:, 1, :], gs[:, 0, :], nhalf[:, :], ALU.pow).then_inc(sem("f0_rms"), 1)
            with pool.Fori(0, G) as g:
                for e in range(E):
                    n = E * g + e
                    pool.wait_ge(*at("f0_gl", n + 1))
                    pool.wait_ge(*at("f0_sg", n + 1))
                    pool.tensor_tensor(hid[:, e % 2, :], hid[:, e % 2, :], hid[:, 2 + e % 2, :],
                                       ALU.mult).then_inc(sem("f0_act"), 1)
            attention("a1", 1)
            with pool.Fori(0, G) as g:
                pow_rstd("f1", g)
            with pool.Fori(0, G) as g:
                pow_rstd("a2", g)
                pool.wait_ge(*at("a2_ln", g + 1))
                pool.tensor_tensor(X4(g), X4(g), rowc[:, g, :].unsqueeze(1).to_broadcast([P, J, D]),
                                   ALU.add).then_inc(sem("a2_xb"), 1)
            with pool.Fori(0, G) as g:
                pow_rstd("f2", g)
            with pool.Fori(0, G) as g:
                pow_rstd("a3", g)
            with pool.Fori(0, G) as g:
                pow_rstd("f3", g)

        @block.tensor
        def _(pe):
            job = [0]

            def begin(n):
                assert n == job[0]
                if n >= 8:
                    pe.wait_ge(*at("prep_ev", n - 7))
                return n % 8

            def end(ins):
                ins.then_inc(sem("prep_mm"), 1)
                job[0] += 1

            def mm(o, l, r, start=True, stop=True):
                return pe.matmul(o, l, r, start=start, stop=stop)

            pe.wait_ge(*at("consts", 13))
            pe.wait_ge(*at("ld_ctx", 16))
            k = begin(J_CTX)
            for b in range(B):
                i = pe.transpose(bank[k][:, b * M:(b + 1) * M], ctxr[:, b, :], ident[0:M, 0:M])
            end(i)
            pe.wait_ge(*at("ld_wq", 16))
            for a in range(2):
                k = begin(J_WQ + a)
                for c in range(4):
                    i = pe.transpose(b4(k)[:, c, :], wq[:, (4 * a + c) * P:(4 * a + c + 1) * P], ident[:, :])
                end(i)
            pe.wait_ge(*at("ld_wk", 16))
            pe.wait_ge(*at("prep_ev", J_CTX + 1))
            for c in range(8):
                k = begin(J_K + c)
                end(mm(bank[k][:, 0:B * M], wk[:, c * P:(c + 1) * P], ctxT[:, :]))
            for h in range(H):
                k = begin(J_A + h)
                o = DH0 * (h % 2)
                pe.wait_ge(*at("prep_ev", J_K + h // 2 + 1))
                end(mm(bank[k][:, 0:B * M], wqT[o:o + DH0, h // 2, :], kT[o:o + DH0, h // 2, :]))
            pe.wait_ge(*at("ld_wv", 16))
            for c in range(8):
                k = begin(J_V + c)
                end(mm(bank[k][:, 0:B * M], wv[:, c * P:(c + 1) * P], ctxT[:, :]))
            pe.wait_ge(*at("ld_wo", 16))
            pe.wait_ge(*at("prep_ev", J_V + 8))
            for b in range(B):
                for q in range(4):
                    k = begin(J_VW + 4 * b + q)
                    for a, h in enumerate(HORD[4 * q:4 * q + 4]):
                        o = DH0 * (h % 2)
                        i = mm(b4(k)[0:M, a, :], vT[o:o + DH0, h // 2, b * M:(b + 1) * M], wo[o:o + DH0, h // 2, :])
                    end(i)
            pe.wait_ge(*at("ld_w4", 64))
            k = begin(J_W4)
            for a in range(4):
                i = pe.transpose(b4(k)[:, a, :], w4r[:, a, :], ident[:, :])
            end(i)
            for a, jn in ((1, J_K1), (2, J_V1)):
                k = begin(jn)
                if a == 1:
                    pe.wait_ge(*at("prep_ev", J_W4 + 1))
                end(mm(bank[k][:, 0:B * M], w4T[:, a, :], ctxT[:, :]))
            for b in range(B):
                pe.wait_ge(*at("vblk", b + 1))
                for q in range(3):
                    k = begin(J_VB + 3 * b + q)
                    for kk in range(4 * q, min(4 * q + 4, NK)):
                        i = mm(b4(k)[0:CH[kk], kk % 4, :], vblk[:, b % 2, kk * P:kk * P + CH[kk]], w4T[:, 3, :])
                    end(i)
            pe.wait_ge(*at("ld_w3", 32))
            k = begin(J_W3)
            for a in range(3):
                i = pe.transpose(b4(k)[:, a, :], w3r[:, a, :], ident[:, :])
            end(i)
            pe.wait_ge(*at("ld_small", 64))
            k = begin(J_SM)
            pe.transpose(bank[k][:, 0:E], gw3r[:, :], ident[0:E, 0:E])
            end(pe.transpose(bank[k][:, E:E + E * FC], b1r[:, :], ident[0:E * FC, 0:E * FC]))
            pe.wait_ge(*at("ld_m", 32))
            for a in range(2):
                k = begin(J_M1 + a)
                for c in range(8):
                    n = 8 * a + c
                    i = pe.transpose(bb(k)[:, c, :], m1r[:, n // 2, (n % 2) * P:(n % 2 + 1) * P], identb[:, :])
                end(i)
            k = begin(J_M2)
            for c in range(E):
                i = pe.transpose(bb(k)[:, c, :], m2r[:, c, :], identb[:, :])
            end(i)
            k = begin(J_SMB)
            pe.transpose(bb(k)[:, 0, 0:E], gw0r[:, :], identb[0:E, 0:E])
            for a in range(2):
                i = pe.transpose(bb(k)[:, 0, E * (a + 1):E * (a + 2)], m1br[:, a:2 * P:2], identb[0:E, 0:E])
            end(i)
            k = begin(J_ROW)
            pe.wait_ge(*at("csum", 2))
            pe.wait_ge(*at("prep_ev", J_W3 + 1))
            for b in range(B):
                i = mm(b4(k)[:, b, :], csB[:, b, :], w3T[:, 1, :])
            end(i)
            k = begin(J_YP)
            end(mm(bank[k][:, 0:B * M], w3T[:, 2, :], ctxT[:, :]))
            pe.wait_ge(*at("prep_ev", J_END))

            def turn(name, g, src=xn, bk=7):
                pe.wait_ge(*at(name + "_ln", g + 1))
                pe.wait_ge(*at(name + "_xte", g))
                for j in range(J):
                    i = pe.transpose(b4(bk)[:, j, :], src[:, j, :], ident[:, :])
                i.then_inc(sem(name + "_xt"), 1)

            def attention(name, keys, vals, q_first):
                src = queT if q_first else grpT

                def scores(g, j, first):
                    t = J * g + j
                    for q, (h0, h1) in enumerate(HEADS):
                        if not (first and j == 0):
                            pe.wait_ge(*at(name + "_sub", 3 * t - 2 + q))
                        mm(bank[q][:, 0:(h1 - h0) * M], src[:, j, :], keys[:, g, h0 * M:h1 * M]
                           ).then_inc(sem(name + "_sc"), 1)

                def values(g, j, first):
                    t = J * g + j
                    pe.wait_ge(*at(name + "_p", t + 1))
                    for q in range(3):
                        if not first:
                            pe.wait_ge(*at(name + "_pte", 4 * t - 3 + (q if q < 2 else 3)))
                        for k in range(4 * q, min(4 * q + 4, NK)):
                            i = pe.transpose(b4(3 + q)[0:CH[k], k % 4, :], prb[:, j, k * P:k * P + CH[k]], ident[:, :])
                        i.then_inc(sem(name + "_pt"), 1)
                    if not first:
                        pe.wait_ge(*at(name + "_x", t))
                    for k in range(NK):
                        if k in (0, 4, 8, 9):
                            pe.wait_ge(*at(name + "_pte", 4 * t + {0: 1, 4: 2, 8: 3, 9: 4}[k]))
                        i = mm(bank[6][:, 0:D], prT[0:CH[k], j % 2, k * P:(k + 1) * P],
                               vals[0:CH[k], g, k, :], k == 0, k == NK - 1)
                    i.then_inc(sem(name + "_out"), 1)

                def group(g, first):
                    turn(name, g)
                    if q_first:
                        pe.wait_ge(*at(name + "_xte", g + 1))
                        mm(bank[7][:, :], w4T[:, 0, :], grpT[:, :, :].rearrange("p j n -> p (j n)")
                           ).then_inc(sem(name + "_q"), 1)
                        pe.wait_ge(*at(name + "_qe", g + 1))
                    else:
                        pe.wait_ge(*at(name + "_xte", g + 1))
                    for j in range(J):
                        scores(g, j, first)
                        if j >= 2:
                            values(g, j - 2, first and j == 2)
                        elif not first:
                            values(g - 1, j + 2, False)

                group(0, True)
                with pe.Fori(1, G) as g:
                    group(g, False)
                values(G - 1, J - 2, False)
                values(G - 1, J - 1, False)

            def bias_rows(name, g, rows):
                pe.wait_ge(*at(name + "_cs", g + 1))
                pe.wait_ge(*at(name + "_cte", g))
                for j in range(J):
                    i = pe.transpose(b4(5)[0:E, j, :], eq[:, 0, j, :], ident[:, :])
                i.then_inc(sem(name + "_ct"), 1)
                pe.wait_ge(*at(name + "_cte", g + 1))
                pe.wait_ge(*at(name + "_b2e", g))
                for j in range(J):
                    i = mm(b4(4)[:, j, :], cT[:, j, :], rows[:, :])
                i.then_inc(sem(name + "_b2"), 1)

            pe.wait_ge(*at("vw_in", 16 * NPIECE))
            attention("a0", keys0, vals0, False)

            pe.wait_ge(*at("a0_x", T))
            with pe.Fori(0, G) as g:
                pe.wait_ge(*at("f0_nrm", g + 1))
                pe.wait_ge(*at("f0_xte", g))
                for j in range(J):
                    i = pe.transpose(bb(7)[:, j, :], nrm[:, j, :], identb[:, :])
                i.then_inc(sem("f0_xt"), 1)
                pe.wait_ge(*at("f0_xte", g + 1))
                pe.wait_ge(*at("f0_lge", g))
                for j in range(J):
                    i = mm(bank[6][:, j * E:(j + 1) * E], nTg[:, j, :], gw0T[:, :])
                i.then_inc(sem("f0_lg"), 1)
                bias_rows("f0", g, m2bf)
            pe.wait_ge(*at("f0_b2e", G))

            def f0_down(g, e):
                n = E * g + e
                pe.wait_ge(*at("f0_act", n + 1))
                if e >= 2:
                    pe.wait_ge(*at("f0_acc", n - 1))
                else:
                    pe.wait_ge(*at("f0_acc", E * g))
                for j in range(J):
                    i = mm(b4(4 + e % 2)[:, j, :], hid[:, e % 2, j * P:(j + 1) * P], m2T[:, e, :])
                i.then_inc(sem("f0_dn"), 1)

            with pe.Fori(0, G) as g:
                for e in range(E):
                    n = E * g + e
                    if e >= 2:
                        pe.wait_ge(*at("f0_gb", n - 1))
                        pe.wait_ge(*at("f0_lb", n - 1))
                    else:
                        pe.wait_ge(*at("f0_gb", E * g))
                        pe.wait_ge(*at("f0_lb", E * g))
                    mm(bank[e % 2][:, :], m1T[:, 2 * e, :], nT[:, g, :])
                    mm(bank[2 + e % 2][:, :], m1T[:, 2 * e + 1, :], nT[:, g, :]).then_inc(sem("f0_up"), 1)
                    if e:
                        f0_down(g, e - 1)
                f0_down(g, E - 1)

            pe.wait_ge(*at("f0_x", G))
            attention("a1", keys1, vals1, True)

            pe.wait_ge(*at("a1_x", T))
            with pe.Fori(0, G) as g:
                turn("f1", g)
                pe.wait_ge(*at("f1_xte", g + 1))
                pe.wait_ge(*at("f1_lge", g))
                for j in range(J):
                    i = mm(bank[6][:, j * E:(j + 1) * E], grpT[:, j, :], wr1[:, :])
                i.then_inc(sem("f1_lg"), 1)
                pe.wait_ge(*at("f1_oneh", g + 1))
                pe.wait_ge(*at("f1_rke", g))
                for j in range(J):
                    o = bank[5][:, j * E:(j + 1) * E]
                    mm(o, lower[:, :], oneh[:, j, :], True, False)
                    i = mm(o, onesb[:, :], seen[:, j, :], False, True)
                i.then_inc(sem("f1_rk"), 1)
            pe.wait_ge(*at("f1_rke", G))

            def moe(name, w1, w2):
                def down(g, u):
                    n = E * FC * g + u
                    e, c = u // FC, u % FC
                    pe.wait_ge(*at(name + "_h", n + 1))
                    if c == 0:
                        pe.wait_ge(*at(name + "_acc", E * g + e - 1 if e >= 2 else E * g))
                    for j in range(J):
                        i = pe.matmul(b4(4 + e % 2)[:, j, :], hid[:, u % 4, j * P:(j + 1) * P], w2[:, e, c, :],
                                      start=(c == 0 and j == 0), stop=(c == FC - 1), skip_group_check=True)
                    i.then_inc(sem(name + "_dn"), 1)

                with pe.Fori(0, G) as g:
                    for u in range(E * FC):
                        n = E * FC * g + u
                        pe.wait_ge(*at(name + "_h", n - 3 if u >= 4 else E * FC * g))
                        mm(bank[u % 4][:, :], w1[:, u // FC, (u % FC) * P:(u % FC + 1) * P], xnT[:, g, :]
                           ).then_inc(sem(name + "_up"), 1)
                        if u:
                            down(g, u - 1)
                    down(g, E * FC - 1)

            pe.wait_ge(*at("ld_w1_l1", 16))
            pe.wait_ge(*at("ld_w2_l1", 16))
            moe("f1", w1_l1, w2_l1)

            pe.wait_ge(*at("f1_acc", G * E))
            with pe.Fori(0, G) as g:
                turn("a2", g)
                pe.wait_ge(*at("a2_xte", g + 1))
                pe.wait_ge(*at("a2_x", g))
                for j in range(J):
                    i = mm(b4(6)[:, j, :], grpT[:, j, :], w3T[:, 0, :])
                i.then_inc(sem("a2_out"), 1)

            pe.wait_ge(*at("a2_x", G))
            with pe.Fori(0, G) as g:
                turn("f2", g)
                bias_rows("f2", g, b2r)
            pe.wait_ge(*at("f2_b2e", G))
            pe.wait_ge(*at("f2_xte", G))
            pe.wait_ge(*at("ld_w1_l2", 16))
            pe.wait_ge(*at("ld_w2_l2", 16))
            moe("f2", w1_l2, w2_l2)

            pe.wait_ge(*at("f2_acc", G * E))
            with pe.Fori(0, G) as g:
                turn("a3", g)
                pe.wait_ge(*at("a3_xte", g + 1))
                mm(bank[6][:, :], w3T[:, 2, :], grpT[:, :, :].rearrange("p j n -> p (j n)")).then_inc(sem("a3_q"), 1)
                pe.wait_ge(*at("a3_qe", g + 1))
                pe.wait_ge(*at("a3_sub", g))
                for j in range(J):
                    i = mm(bank[0][:, j * M:(j + 1) * M], queT[:, j, :],
                           ypT[:, :].rearrange("p (b m) -> p b m", b=B)[:, g, :])
                i.then_inc(sem("a3_sc"), 1)
                pe.wait_ge(*at("a3_exp", g + 1))
                pe.wait_ge(*at("a3_pte", g))
                for j in range(J):
                    i = pe.transpose(b4(1)[0:M, j, :], prb[:, 0, j * M:(j + 1) * M], ident[:, :])
                i.then_inc(sem("a3_pt"), 1)
                pe.wait_ge(*at("a3_pte", g + 1))
                pe.wait_ge(*at("a3_x", J * g))
                for j in range(J):
                    i = mm(b4(2)[:, j, :], prT[0:M, 0, j * P:(j + 1) * P], ctxr[:, g, :])
                i.then_inc(sem("a3_out"), 1)

            pe.wait_ge(*at("a3_x", T))
            pe.wait_ge(*at("ld_w_l3", 16 * 6))
            with pe.Fori(0, G) as g:
                turn("f3", g)
                pe.wait_ge(*at("f3_xte", g + 1))
                pe.wait_ge(*at("f3_lge", g))
                for j in range(J):
                    i = mm(bank[6][:, j * E:(j + 1) * E], grpT[:, j, :], gw3T[:, :])
                i.then_inc(sem("f3_lg"), 1)


                def up(u):
                    j, pr = u // 5, u % 5
                    ne = 2 if pr < 4 else 1
                    n = NU * g + u
                    pe.wait_ge(*at("f3_prod", n - 1 if u >= 2 else NU * g))
                    for a in range(ne):
                        i = pe.matmul(bank[u % 2][:, a * 256:(a + 1) * 256], grpT[:, j, :],
                                      w13_l3[:, 2 * pr + a, :], start=True, stop=True)
                    i.then_inc(sem("f3_up"), 1)

                def back(u):
                    j, pr = u // 5, u % 5
                    ne = 2 if pr < 4 else 1
                    n = NU * g + u
                    pe.wait_ge(*at("f3_prod", n + 1))
                    pe.wait_ge(*at("f3_hte", n - 1 if u >= 2 else NU * g))
                    for a in range(ne):
                        i = pe.transpose(b4(2 + u % 2)[:, a, :], hid[:, u % 2, a * P:(a + 1) * P], ident[:, :])
                    i.then_inc(sem("f3_ht"), 1)

                def down(u):
                    j, pr = u // 5, u % 5
                    ne = 2 if pr < 4 else 1
                    n = NU * g + u
                    pe.wait_ge(*at("f3_hte", n + 1))
                    if pr == 0:
                        pe.wait_ge(*at("f3_x", J * g + j - 1 if j >= 2 else J * g))
                    for a in range(ne):
                        i = mm(bank[4 + j % 2][:, 0:D], hid[:, 2 + u % 2, a * P:(a + 1) * P],
                               w2_l3[:, 2 * pr + a, :], pr == 0 and a == 0, pr == 4)
                    i.then_inc(sem("f3_dn"), 1)

                for u in range(NU + 2):
                    if u < NU:
                        up(u)
                    if 1 <= u <= NU:
                        back(u - 1)
                    if u >= 2:
                        down(u - 2)

        @block.scalar
        def _(act):
            job = [0]

            def ready(n):
                assert n == job[0], (n, job)
                job[0] += 1
                act.wait_ge(*at("prep_mm", n + 1))
                return n % 8

            def ev(o, i, scale=1.0, inc=True):
                x = act.activation(o, i, ACT.Copy, scale=scale)
                if inc:
                    x.then_inc(sem("prep_ev"), 1)

            k = ready(J_CTX)
            ev(ctxT[:, :], bank[k][:, 0:B * M])
            for a in range(2):
                k = ready(J_WQ + a)
                ev(wqT[:, 4 * a:4 * a + 4, :], b4(k))
            for c in range(8):
                k = ready(J_K + c)
                ev(kT[:, c, :], bank[k][:, 0:B * M])
            for h in range(H):
                k = ready(J_A + h)
                ev(keys0[:, :, h * M:(h + 1) * M], bank[k][:, 0:B * M].rearrange("p (b m) -> p b m", b=B), DH0 ** -0.5)
            for c in range(8):
                k = ready(J_V + c)
                ev(vT[:, c, :], bank[k][:, 0:B * M])
            for b in range(B):
                for q in range(4):
                    k = ready(J_VW + 4 * b + q)
                    r = HORD[4 * q]
                    ev(vstage[:, b, r:r + 7:2, :], b4(k)[0:M, :, :])
            k = ready(J_W4)
            ev(w4T[:, :, :], b4(k))
            act.wait_ge(*at("vw_out", 16 * B))
            act.wait_ge(*at("ld_cols", 64))
            k = ready(J_K1)
            act.activation(kvT1[:, 0, :], bank[k][:, 0:B * M], ACT.Identity, bias=cols[:, 1:2]
                           ).then_inc(sem("prep_ev"), 1)
            k = ready(J_V1)
            act.activation(kvT1[:, 1, :], bank[k][:, 0:B * M], ACT.Identity, bias=cols[:, 2:3]
                           ).then_inc(sem("prep_ev"), 1)
            for b in range(B):
                for q in range(3):
                    k = ready(J_VB + 3 * b + q)
                    if q < 2:
                        ev(vals1[:, b, 4 * q:4 * q + 4, :], b4(k))
                    else:
                        ev(vals1[:, b, 8, :], b4(k)[:, 0, :], inc=False)
                        ev(vals1[0:CH[9], b, 9, :], b4(k)[0:CH[9], 1, :])
            k = ready(J_W3)
            ev(w3T[:, :, :], b4(k)[:, 0:3, :])
            k = ready(J_SM)
            ev(gw3T[:, :], bank[k][:, 0:E], inc=False)
            ev(b1T[:, :], bank[k][:, E:E + E * FC])
            for a in range(2):
                k = ready(J_M1 + a)
                ev(m1T[:, 8 * a:8 * a + 8, :], bb(k))
            k = ready(J_M2)
            ev(m2T[:, :, :], bb(k))
            k = ready(J_SMB)
            ev(gw0T[:, :], bb(k)[:, 0, 0:E], inc=False)
            ev(m1bT[:, :, :].rearrange("p a e -> p (a e)"), bb(k)[:, 0, E:3 * E])
            k = ready(J_ROW)
            ev(rowc[:, :, :], b4(k), 1.0 / M)
            k = ready(J_YP)
            act.activation(ypT[:, :], bank[k][:, 0:B * M], ACT.Relu, bias=cols[:, 3:4]).then_inc(sem("prep_ev"), 1)
            act.wait_ge(*at("prep_ev", J_END))

            def turned(name, g, dst, flat=True):
                act.wait_ge(*at(name + "_xt", g + 1))
                act.activation(dst, bank[7][:, :], ACT.Copy).then_inc(sem(name + "_xte"), 1)

            def attention(name, q_first):
                def exps(g, j):
                    t = J * g + j
                    act.wait_ge(*at(name + "_sub", 3 * t + 3))
                    act.activation(prb[:, j, :], prb[:, j, :], ACT.Exp).then_inc(sem(name + "_exp"), 1)

                def evac(g, j, first):
                    t = J * g + j
                    if not first:
                        act.wait_ge(*at(name + "_out", t - 1))
                    for q in range(3):
                        act.wait_ge(*at(name + "_pt", 3 * t + q + 1))
                        if q < 2:
                            act.activation(prT[:, j % 2, 4 * q * P:(4 * q + 4) * P], bank[3 + q][:, :], ACT.Copy
                                           ).then_inc(sem(name + "_pte"), 1)
                        else:
                            act.activation(prT[:, j % 2, 8 * P:9 * P], b4(5)[:, 0, :], ACT.Copy
                                           ).then_inc(sem(name + "_pte"), 1)
                            act.activation(prT[0:CH[9], j % 2, 9 * P:10 * P], b4(5)[0:CH[9], 1, :], ACT.Copy
                                           ).then_inc(sem(name + "_pte"), 1)

                def group(g, first):
                    act.wait_ge(*at(name + ("_q" if q_first else "_sc"), g if q_first else 3 * J * g))
                    turned(name, g, grpT[:, :, :].rearrange("p j n -> p (j n)"))
                    if q_first:
                        act.wait_ge(*at(name + "_q", g + 1))
                        act.wait_ge(*at(name + "_sc", 3 * J * g))
                        act.activation(queT[:, :, :].rearrange("p j n -> p (j n)"), bank[7][:, :], ACT.Identity,
                                       bias=cols[:, 0:1]).then_inc(sem(name + "_qe"), 1)
                    for j in range(J):
                        exps(g, j)
                        if j >= 2:
                            evac(g, j - 2, first)
                        elif not first:
                            evac(g - 1, j + 2, False)

                group(0, True)
                with act.Fori(1, G) as g:
                    group(g, False)
                evac(G - 1, J - 2, False)
                evac(G - 1, J - 1, False)

            attention("a0", False)

            with act.Fori(0, G) as g:
                act.wait_ge(*at("f0_xt", g + 1))
                act.wait_ge(*at("f0_lg", g))
                act.activation(nT[:, g, :], bb(7)[:, 0:4, :].rearrange("p j n -> p (j n)"), ACT.Copy)
                act.activation(nTg[:, :, :], bb(7)[:, 0:4, :], ACT.Copy).then_inc(sem("f0_xte"), 1)
                act.wait_ge(*at("f0_gap", g + 1))
                act.activation(gs[:, 3, :], gs[:, 2, :], ACT.Exp).then_inc(sem("f0_gexp"), 1)
                act.wait_ge(*at("f0_ct", g + 1))
                act.wait_ge(*at("f0_b2", g))
                act.activation(cT[:, :, :], b4(5)[0:E, :, :], ACT.Copy).then_inc(sem("f0_cte"), 1)
            with act.Fori(0, G) as g:
                for e in range(E):
                    n = E * g + e
                    act.wait_ge(*at("f0_gb", n + 1))
                    act.wait_ge(*at("f0_act", n - 1 if e >= 2 else E * g))
                    act.activation(hid[:, 2 + e % 2, :], mlpg[:, e % 2, :], ACT.Sigmoid, scale=ALPHA
                                   ).then_inc(sem("f0_sg"), 1)

            attention("a1", True)

            def gates_exp(name, g):
                act.wait_ge(*at(name + "_gap", g + 1))
                act.activation(lg[:, :, :], lg[:, :, :], ACT.Exp).then_inc(sem(name + "_gexp"), 1)

            with act.Fori(0, G) as g:
                act.wait_ge(*at("f1_xt", g + 1))
                act.wait_ge(*at("f1_lg", g))
                act.activation(xnT[:, g, :], bank[7][:, :], ACT.Copy)
                turned("f1", g, grpT[:, :, :].rearrange("p j n -> p (j n)"))
                gates_exp("f1", g)

            def moe(name, biased):
                with act.Fori(0, G) as g:
                    for u in range(E * FC):
                        n = E * FC * g + u
                        act.wait_ge(*at(name + "_up", n + 1))
                        act.wait_ge(*at(name + "_dn", n - 3 if u >= 4 else E * FC * g))
                        act.activation(hid[:, u % 4, :], bank[u % 4][:, :], ACT.Relu,
                                       bias=b1T[:, u:u + 1] if biased else 0.0).then_inc(sem(name + "_h"), 1)

            moe("f1", False)
            with act.Fori(0, G) as g:
                act.wait_ge(*at("a2_out", g))
                turned("a2", g, grpT[:, :, :].rearrange("p j n -> p (j n)"))
            with act.Fori(0, G) as g:
                turned("f2", g, xnT[:, g, :])
                act.wait_ge(*at("f2_ct", g + 1))
                act.wait_ge(*at("f2_b2", g))
                act.activation(cT[:, :, :], b4(5)[0:E, :, :], ACT.Copy).then_inc(sem("f2_cte"), 1)
            moe("f2", True)
            with act.Fori(0, G) as g:
                act.wait_ge(*at("a3_q", g))
                turned("a3", g, grpT[:, :, :].rearrange("p j n -> p (j n)"))
                act.wait_ge(*at("a3_q", g + 1))
                act.wait_ge(*at("a3_sc", g))
                act.activation(queT[:, :, :].rearrange("p j n -> p (j n)"), bank[6][:, :], ACT.Relu,
                               bias=cols[:, 3:4]).then_inc(sem("a3_qe"), 1)
                act.wait_ge(*at("a3_gap", g + 1))
                act.activation(prb[:, 0, 0:J * M], prb[:, 0, 0:J * M], ACT.Exp).then_inc(sem("a3_exp"), 1)
                act.wait_ge(*at("a3_pt", g + 1))
                act.wait_ge(*at("a3_out", g))
                act.activation(prT[0:M, 0, 0:J * P], bank[1][0:M, :], ACT.Copy).then_inc(sem("a3_pte"), 1)
            with act.Fori(0, G) as g:
                act.wait_ge(*at("f3_up", 5 * J * g))
                turned("f3", g, grpT[:, :, :].rearrange("p j n -> p (j n)"))
                gates_exp("f3", g)
                act.wait_ge(*at("f3_c", g + 1))

                def silu(u):
                    j, pr = u // 5, u % 5
                    ne = 2 if pr < 4 else 1
                    act.wait_ge(*at("f3_up", NU * g + u + 1))
                    act.wait_ge(*at("f3_prod", NU * g + u - 1 if u >= 2 else NU * g))
                    for a in range(ne):
                        i = act.activation(mlpg[:, u % 2, a * P:(a + 1) * P], bank[u % 2][:, a * 256:a * 256 + P],
                                           ACT.Silu, scale=C9[:, j, 2 * pr + a:2 * pr + a + 1])
                    i.then_inc(sem("f3_silu"), 1)

                def hte(u):
                    j, pr = u // 5, u % 5
                    ne = 2 if pr < 4 else 1
                    act.wait_ge(*at("f3_ht", NU * g + u + 1))
                    act.wait_ge(*at("f3_dn", NU * g + u - 1 if u >= 2 else NU * g))
                    act.activation(hid[:, 2 + u % 2, 0:ne * P], bank[2 + u % 2][:, 0:ne * P], ACT.Copy
                                   ).then_inc(sem("f3_hte"), 1)

                for u in range(NU + 1):
                    if u < NU:
                        silu(u)
                    if u:
                        hte(u - 1)

        @block.vector
        def _(dve):
            def bc3(ap, shape, ax):
                return ap.unsqueeze(ax).to_broadcast(shape)

            def take_wait():
                dve.memset(pad[:, :], 0.0)

            def copy_at(o, i):
                return dve.tensor_scalar(o, i, 1.0, None, ALU.mult)

            dve.wait_ge(*at("consts", 13))
            dve.wait_ge(*at("prep_ev", J_CTX + 1))
            dve.tensor_reduce(csum[:, :], ctxT[:, :].rearrange("p (b m) -> p b m", b=B), AXX, ALU.add
                              ).then_inc(sem("csum"), 1)
            dve.wait_ge(*at("csum", 1))
            dve.tensor_copy(csB, bc3(csum[:, :], [P, B, P], 2)).then_inc(sem("csum"), 1)
            dve.wait_ge(*at("prep_ev", J_V1 + 1))
            i = dve.tensor_scalar(kvT1[:, 0, :], kvT1[:, 0, :], DH1 ** -0.5, None, ALU.mult)
            i.then_inc(sem("k1s"), 1)
            dve.wait_ge(*at("k1s", 1))

            def by_head(o, src, b):
                return dve.tensor_tensor(o.rearrange("p (h m) -> p h m", h=H),
                                         bc3(src[:, b * M:(b + 1) * M], [P, H, M], 1),
                                         bc3(blk[:, :], [P, H, M], 2), ALU.mult)

            for b in range(B):
                if b >= 2:
                    dve.wait_ge(*at("prep_mm", J_VB + 3 * (b - 1)))
                by_head(vblk[:, b % 2, :], kvT1[:, 1, :], b).then_inc(sem("vblk"), 1)
            for b in range(B):
                by_head(keys1[:, b, :], kvT1[:, 0, :], b).then_inc(sem("keys1"), 1)
            dve.wait_ge(*at("ld_bo", 48))
            dve.wait_ge(*at("prep_ev", J_END))
            dve.wait_ge(*at("keys1", B))
            dve.tensor_tensor(rowc[:, :, :], rowc[:, :, :], bc3(boB[:, 2, :], [P, B, D], 1), ALU.add
                              ).then_inc(sem("rowc"), 1)
            dve.tensor_scalar(maskf[:, :, :], maskf[:, :, :], MASKED, None, ALU.mult).then_inc(sem("rowc"), 1)
            dve.wait_ge(*at("rowc", 2))

            def norm(name, g, wait_x):
                wait_x(g)
                for j in range(J):
                    i = dve.bn_stats(st[:, j, :], X[:, J * g + j, :])
                i.then_inc(sem(name + "_st"), 1)
                dve.wait_ge(*at(name + "_st", g + 1))
                take_wait()
                for j in range(J):
                    i = dve.bn_aggr(mv[:, j, :], st[:, j, :])
                i.then_inc(sem(name + "_mv"), 1)
                dve.wait_ge(*at(name + "_mv", g + 1))
                dve.tensor_scalar(ve[:, :], mv[:, :, 1], LN_EPS, None, ALU.add).then_inc(sem(name + "_ve"), 1)
                dve.wait_ge(*at(name + "_rstd", g + 1))
                if name != "f0":
                    dve.wait_ge(*at(name + "_xt", g))
                for j in range(J):
                    i = dve.tensor_scalar(xn[:, j, :], X[:, J * g + j, :], mv[:, j, 0:1], rstd[:, j:j + 1],
                                          ALU.subtract, ALU.mult)
                i.then_inc(sem(name + "_ln"), 1)

            def attention(name, wait_x):
                def soft(g, j, first):
                    t = J * g + j
                    for q, (h0, h1) in enumerate(HEADS):
                        dve.wait_ge(*at(name + "_sc", 3 * t + q + 1))
                        dve.tensor_reduce(mx[:, j % 2, h0:h1],
                                          bank[q][:, 0:(h1 - h0) * M].rearrange("p (h m) -> p h m", m=M),
                                          AXX, ALU.max).then_inc(sem(name + "_mx"), 1)
                    if not first:
                        dve.wait_ge(*at(name + "_pt", 3 * (t - 3)))
                    for q, (h0, h1) in enumerate(HEADS):
                        dve.wait_ge(*at(name + "_mx", 3 * t + q + 1))
                        dve.tensor_tensor(prb[:, j, h0 * M:h1 * M].rearrange("p (h m) -> p h m", m=M),
                                          bank[q][:, 0:(h1 - h0) * M].rearrange("p (h m) -> p h m", m=M),
                                          bc3(mx[:, j % 2, h0:h1], [P, h1 - h0, M], 2),
                                          ALU.subtract).then_inc(sem(name + "_sub"), 1)

                def add(g, j):
                    t = J * g + j
                    dve.wait_ge(*at(name + "_out", t + 1))
                    if j == 0:
                        dve.wait_ge(*at(name + "_xb", g + 1))
                    dve.tensor_tensor(X[:, t, :], bank[6][:, 0:D], X[:, t, :], ALU.add).then_inc(sem(name + "_x"), 1)

                def sums(g, j, first):
                    t = J * g + j
                    dve.wait_ge(*at(name + "_exp", t + 1))
                    dve.tensor_reduce(sm[:, j % 2, :], prb[:, j, :].rearrange("p (h m) -> p h m", h=H),
                                      AXX, ALU.add).then_inc(sem(name + "_sm"), 1)
                    dve.wait_ge(*at(name + "_sm", t + 1))
                    if not (first and j < 2):
                        dve.wait_ge(*at(name + "_p", t - 1))
                    dve.reciprocal(rs[:, j % 2, :], sm[:, j % 2, :]).then_inc(sem(name + "_rs"), 1)

                def group(g, first):
                    norm(name, g, wait_x)
                    for j in range(J):
                        soft(g, j, first)
                        if j == 3:
                            add(g, 0)
                        elif not first:
                            add(g - 1, j + 1)
                        if j:
                            sums(g, j - 1, first)
                        elif not first:
                            sums(g - 1, J - 1, False)

                group(0, True)
                with dve.Fori(1, G) as g:
                    group(g, False)
                sums(G - 1, J - 1, False)
                for j in range(1, J):
                    add(G - 1, j)

            dve.wait_ge(*at("ld_x", 16))
            attention("a0", lambda g: None)

            def bias_add(name, g, dst):
                dve.wait_ge(*at(name + "_b2", g + 1))
                if name == "f0":
                    copy_at(dst, b4(4)).then_inc(sem(name + "_b2e"), 1)
                else:
                    dve.tensor_tensor(dst, b4(4), dst, ALU.add).then_inc(sem(name + "_b2e"), 1)

            def grp(tile, g):
                return tile.rearrange("p (g j) d -> p g (j d)", g=G)[:, g, :].rearrange("p (j d) -> p j d", j=J)

            dve.wait_ge(*at("ld_later", 96))
            K = 13
            with dve.Fori(0, G) as g:
                norm("f0", g, lambda g: dve.wait_ge(*at("a0_x", T)))
                dve.wait_ge(*at("f0_ln", g + 1))
                c = Steps(dve, sem("f0_c"), K * g)
                c(dve.tensor_copy(xcg[:, :, :], xn[:, :, :]))
                dve.wait_ge(*at("f0_xt", g))
                for j in range(J):
                    i = dve.tensor_tensor_reduce(nrm[:, j, :], xcg[:, j, :], xcg[:, j, :], 1.0, 0.0,
                                                 ALU.mult, ALU.add, gs[:, 4, j:j + 1])
                c(i)
                c(copy_at(grp(xc[:, :, :], g), xcg[:, :, :]))
                dve.tensor_scalar(gs[:, 0, :], gs[:, 4, :], 1.0 / D, LN_EPS, ALU.mult, ALU.add
                                  ).then_inc(sem("f0_ms"), 1)
                dve.wait_ge(*at("f0_rms", g + 1))
                for j in range(J):
                    i = dve.scalar_tensor_tensor(nrm[:, j, :], xcg[:, j, :], gs[:, 1, j:j + 1], nwB[:, :],
                                                 ALU.mult, ALU.mult)
                i.then_inc(sem("f0_nrm"), 1)
                dve.wait_ge(*at("f0_lg", g + 1))
                c(dve.tensor_tensor(lgb[:, :, :], bank[6][:, 0:J * E].rearrange("p (j e) -> p j e", j=J),
                                    bc3(gbB[:, :], [P, J, E], 1), ALU.add))
                dve.tensor_copy(lg[:, :, :], lgb[:, :, :]).then_inc(sem("f0_lge"), 1)
                dve.wait_ge(*at("f0_lge", g + 1))
                take_wait()
                for j in range(J):
                    i = dve.max(m8[:, j, :], lg[:, j, :])
                c(i)
                dve.tensor_tensor(gs[:, 2, :], m8[:, :, 1], m8[:, :, 0], ALU.subtract).then_inc(sem("f0_gap"), 1)
                take_wait()
                for j in range(J):
                    i = dve.max_index(i8[:, j, :], m8[:, j, :], lg[:, j, :])
                c(i)
                c(dve.tensor_copy(i8f[:, :, :], i8[:, :, :]))
                dve.wait_ge(*at("f0_gexp", g + 1))
                c(dve.tensor_scalar(gs[:, 5, :], gs[:, 3, :], 1.0, None, ALU.add))
                c(dve.reciprocal(gs[:, 6, :], gs[:, 5, :]))
                c(dve.tensor_tensor(gs[:, 7, :], gs[:, 6, :], gs[:, 3, :], ALU.mult))
                for a in range(2):
                    i = dve.tensor_tensor(eq[:, a, :, :], bc3(iota[:, :], [P, J, E], 1),
                                          bc3(i8f[:, :, a], [P, J, E], 2), ALU.is_equal)
                c(i)
                for a in range(2):
                    i = dve.tensor_tensor(eq[:, a, :, :], eq[:, a, :, :], bc3(gs[:, 6 + a, :], [P, J, E], 2), ALU.mult)
                c(i)
                c(dve.tensor_tensor(grp(C[:, :, :], g), eq[:, 0, :, :], eq[:, 1, :, :], ALU.add))
                assert c.n == K
                copy_at(eq[:, 0, :, :], grp(C[:, :, :], g)).then_inc(sem("f0_cs"), 1)
                bias_add("f0", g, grp(acc, g))

            dve.wait_ge(*at("f0_b2e", G))

            def accumulate(name, g, e, n, dst, upto):
                dve.wait_ge(*at(name + "_dn", upto))
                dve.wait_ge(*at(name + "_acc", n))
                for j in range(J):
                    i = dve.scalar_tensor_tensor(dst[:, J * g + j, :], b4(4 + e % 2)[:, j, :], C[:, J * g + j, e:e + 1],
                                                 dst[:, J * g + j, :], ALU.mult, ALU.add)
                i.then_inc(sem(name + "_acc"), 1)

            with dve.Fori(0, G) as g:
                for e in range(E):
                    n = E * g + e
                    s = e % 2
                    dve.wait_ge(*at("f0_up", n + 1))
                    dve.wait_ge(*at("f0_sg", n - 1 if e >= 2 else E * g))
                    dve.wait_ge(*at("f0_gl", n))
                    dve.tensor_scalar(mlpg[:, s, :], bank[s][:, :], m1bT[:, 0, e:e + 1], LIMIT, ALU.add, ALU.min
                                      ).then_inc(sem("f0_gb"), 1)
                    dve.tensor_scalar(mlpl[:, s, :], bank[2 + s][:, :], m1bT[:, 1, e:e + 1], -LIMIT, ALU.add, ALU.max
                                      ).then_inc(sem("f0_lb"), 1)
                    dve.wait_ge(*at("f0_lb", n + 1))
                    dve.tensor_scalar(mlpl[:, s, :], mlpl[:, s, :], LIMIT, 1.0, ALU.min, ALU.add
                                      ).then_inc(sem("f0_l1"), 1)
                    dve.wait_ge(*at("f0_l1", n + 1))
                    dve.wait_ge(*at("f0_dn", n - 1 if e >= 2 else E * g))
                    dve.tensor_tensor(hid[:, s, :], mlpl[:, s, :], mlpg[:, s, :], ALU.mult).then_inc(sem("f0_gl"), 1)
                    if e:
                        accumulate("f0", g, e - 1, n - 1, acc, n)
                accumulate("f0", g, E - 1, E * g + E - 1, acc, E * g + E)
                dve.wait_ge(*at("f0_acc", E * (g + 1)))
                c = Steps(dve, sem("f0_fin"), 2 * g)
                c(copy_at(accb[:, :, :], grp(acc, g)))
                c(dve.tensor_tensor(accb[:, :, :], accb[:, :, :], grp(xc[:, :, :], g), ALU.add))
                dve.tensor_tensor(grp(X[:, :, :], g), accb[:, :, :], grp(X[:, :, :], g), ALU.add
                                  ).then_inc(sem("f0_x"), 1)

            attention("a1", lambda g: dve.wait_ge(*at("f0_x", g + 1)))

            dve.memset(seenf[:, :], 0.0).then_inc(sem("seenf"), 1)
            dve.wait_ge(*at("seenf", 1))
            K1 = 10
            with dve.Fori(0, G) as g:
                norm("f1", g, lambda g: dve.wait_ge(*at("a1_x", T)))
                dve.wait_ge(*at("f1_lg", g + 1))
                c = Steps(dve, sem("f1_c"), K1 * g)
                dve.tensor_copy(lg[:, :, :], bank[6][:, 0:J * E].rearrange("p (j e) -> p j e", j=J)
                                ).then_inc(sem("f1_lge"), 1)
                dve.wait_ge(*at("f1_lge", g + 1))
                take_wait()
                for j in range(J):
                    i = dve.max(m8[:, j, :], lg[:, j, :])
                c(i)
                dve.tensor_tensor(lg[:, :, :], lg[:, :, :], bc3(m8[:, :, 0], [P, J, E], 2), ALU.subtract
                                  ).then_inc(sem("f1_gap"), 1)
                dve.wait_ge(*at("f1_gexp", g + 1))
                c(dve.tensor_reduce(gs[:, 0, :], lg[:, :, :], AXX, ALU.add))
                c(dve.reciprocal(gs[:, 1, :], gs[:, 0, :]))
                c(dve.tensor_tensor(lg[:, :, :], lg[:, :, :], bc3(gs[:, 1, :], [P, J, E], 2), ALU.mult))
                take_wait()
                for j in range(J):
                    i = dve.max(m8[:, j, :], lg[:, j, :])
                c(i)
                take_wait()
                for j in range(J):
                    i = dve.max_index(i8[:, j, :], m8[:, j, :], lg[:, j, :])
                c(i)
                c(dve.tensor_copy(i8f[:, :, 0], i8[:, :, 0]))
                c(dve.tensor_tensor(eq[:, 0, :, :], bc3(iota[:, :], [P, J, E], 1),
                                    bc3(i8f[:, :, 0], [P, J, E], 2), ALU.is_equal))
                dve.wait_ge(*at("f1_rk", g))
                dve.tensor_copy(oneh[:, :, :], eq[:, 0, :, :])
                for j in range(J):
                    dve.tensor_copy(seen[:, j, :], seenf[:, :]).then_inc(sem("f1_seen"), 1)
                    dve.tensor_tensor(seenf[:, :], seenf[:, :], eq[:, 0, j, :], ALU.add).then_inc(sem("f1_seen"), 1)
                    dve.wait_ge(*at("f1_seen", 2 * (J * g + j + 1)))
                c(dve.tensor_copy(eq[:, 1, :, :], eq[:, 0, :, :]))
                dve.tensor_tensor(eq[:, 1, :, :], eq[:, 0, :, :], bc3(m8[:, :, 0], [P, J, E], 2), ALU.mult
                                  ).then_inc(sem("f1_oneh"), 1)
                dve.wait_ge(*at("f1_oneh", g + 1))
                dve.wait_ge(*at("f1_rk", g + 1))
                dve.tensor_scalar(eq[:, 0, :, :], bank[5][:, 0:J * E].rearrange("p (j e) -> p j e", j=J), float(CAP),
                                  None, ALU.is_lt).then_inc(sem("f1_rke"), 1)
                dve.wait_ge(*at("f1_rke", g + 1))
                c(dve.tensor_tensor(grp(C[:, :, :], g), eq[:, 0, :, :], eq[:, 1, :, :], ALU.mult))
                assert c.n == K1

            def moe(name):
                with dve.Fori(0, G) as g:
                    for e in range(E):
                        accumulate(name, g, e, E * g + e, X, E * FC * g + FC * (e + 1))

            moe("f1")
            with dve.Fori(0, G) as g:
                norm("a2", g, lambda g: dve.wait_ge(*at("f1_acc", E * G)))
                dve.wait_ge(*at("a2_out", g + 1))
                dve.wait_ge(*at("a2_xb", g + 1))
                dve.tensor_tensor(grp(X[:, :, :], g), b4(6), grp(X[:, :, :], g), ALU.add).then_inc(sem("a2_x"), 1)
            K2 = 17
            with dve.Fori(0, G) as g:
                norm("f2", g, lambda g: dve.wait_ge(*at("a2_x", g + 1)))
                dve.wait_ge(*at("f2_ln", g + 1))
                c = Steps(dve, sem("f2_c"), K2 * g)
                c(dve.tensor_tensor(gs[:, 0, :], xn[:, :, 0], xn[:, :, 1], ALU.add))
                c(dve.tensor_scalar(gs[:, 1, :], gs[:, 0, :], -1.0, None, ALU.mult))
                c(dve.tensor_tensor(gs[:, 1, :], gs[:, 0, :], gs[:, 1, :], ALU.max))
                c(dve.tensor_copy(gi[:, :], gs[:, 1, :]))
                c(dve.tensor_copy(gs[:, 2, :], gi[:, :]))
                c(dve.tensor_tensor(gs[:, 3, :], gs[:, 2, :], gs[:, 1, :], ALU.is_gt))
                c(dve.tensor_tensor(gs[:, 2, :], gs[:, 2, :], gs[:, 3, :], ALU.subtract))
                c(dve.tensor_scalar(gs[:, 3, :], gs[:, 0, :], 0.0, 2.0, ALU.is_ge, ALU.mult))
                c(dve.tensor_scalar(gs[:, 3, :], gs[:, 3, :], -1.0, None, ALU.add))
                c(dve.tensor_tensor(gs[:, 2, :], gs[:, 2, :], gs[:, 3, :], ALU.mult))
                c(dve.tensor_scalar(gs[:, 2, :], gs[:, 2, :], 3.0 * E, None, ALU.add))
                for k in (4, 2, 1):
                    dve.tensor_scalar(gs[:, 3, :], gs[:, 2, :], float(k * E), -float(k * E), ALU.is_ge, ALU.mult
                                      ).then_inc(sem("f2_m"), 1)
                    dve.wait_ge(*at("f2_m", 3 * g + {4: 1, 2: 2, 1: 3}[k]))
                    c(dve.tensor_tensor(gs[:, 2, :], gs[:, 2, :], gs[:, 3, :], ALU.add))
                c(dve.tensor_scalar(gs[:, 3, :], gs[:, 2, :], E - 1.0, -float(E), ALU.is_equal, ALU.mult))
                c(dve.scalar_tensor_tensor(gs[:, 3, :], gs[:, 2, :], 1.0, gs[:, 3, :], ALU.add, ALU.add))
                for a in range(2):
                    i = dve.tensor_tensor(eq[:, a, :, :], bc3(iota[:, :], [P, J, E], 1),
                                          bc3(gs[:, 2 + a, :], [P, J, E], 2), ALU.is_equal)
                c(i)
                assert c.n == K2
                dve.tensor_tensor(eq[:, 0, :, :], eq[:, 0, :, :], eq[:, 1, :, :], ALU.add).then_inc(sem("f2_e"), 1)
                dve.wait_ge(*at("f2_e", 2 * g + 1))
                dve.tensor_scalar(eq[:, 0, :, :], eq[:, 0, :, :], 0.5, None, ALU.mult).then_inc(sem("f2_e"), 1)
                dve.wait_ge(*at("f2_e", 2 * g + 2))
                copy_at(grp(C[:, :, :], g), eq[:, 0, :, :]).then_inc(sem("f2_cs"), 1)
                bias_add("f2", g, grp(X[:, :, :], g))
            dve.wait_ge(*at("f2_b2e", G))
            moe("f2")

            with dve.Fori(0, G) as g:
                norm("a3", g, lambda g: dve.wait_ge(*at("f2_acc", E * G)))
                dve.wait_ge(*at("a3_sc", g + 1))
                dve.wait_ge(*at("a3_pt", g))
                p3 = prb[:, 0, 0:J * M].rearrange("p (j m) -> p j m", j=J)
                c = Steps(dve, sem("a3_c"), 3 * g)
                dve.tensor_tensor(p3, bank[0][:, 0:J * M].rearrange("p (j m) -> p j m", j=J),
                                  bc3(maskf[:, g, :], [P, J, M], 1), ALU.add).then_inc(sem("a3_sub"), 1)
                dve.wait_ge(*at("a3_sub", g + 1))
                c(dve.tensor_reduce(gs[:, 0, :], p3, AXX, ALU.max))
                dve.tensor_tensor(p3, p3, bc3(gs[:, 0, :], [P, J, M], 2), ALU.subtract).then_inc(sem("a3_gap"), 1)
                dve.wait_ge(*at("a3_exp", g + 1))
                c(dve.tensor_reduce(gs[:, 1, :], p3, AXX, ALU.add))
                c(dve.reciprocal(gs[:, 2, :], gs[:, 1, :]))
                dve.wait_ge(*at("a3_out", g + 1))
                for j in range(J):
                    dve.scalar_tensor_tensor(X[:, J * g + j, :], b4(2)[:, j, :], gs[:, 2, j:j + 1],
                                             X[:, J * g + j, :], ALU.mult, ALU.add).then_inc(sem("a3_x"), 1)

            K3 = 9
            with dve.Fori(0, G) as g:
                norm("f3", g, lambda g: dve.wait_ge(*at("a3_x", T)))
                dve.wait_ge(*at("f3_lg", g + 1))
                c = Steps(dve, sem("f3_ch"), K3 * g)
                dve.tensor_copy(lg[:, :, :], bank[6][:, 0:J * E].rearrange("p (j e) -> p j e", j=J)
                                ).then_inc(sem("f3_lge"), 1)
                dve.wait_ge(*at("f3_lge", g + 1))
                take_wait()
                for j in range(J):
                    i = dve.max(m8[:, j, :], lg[:, j, :])
                c(i)
                dve.tensor_tensor(lg[:, :, :], lg[:, :, :], bc3(m8[:, :, 0], [P, J, E], 2), ALU.subtract
                                  ).then_inc(sem("f3_gap"), 1)
                dve.wait_ge(*at("f3_gexp", g + 1))
                c(dve.tensor_reduce(gs[:, 0, :], lg[:, :, :], AXX, ALU.add))
                c(dve.reciprocal(gs[:, 1, :], gs[:, 0, :]))
                c(dve.tensor_tensor(lg[:, :, :], lg[:, :, :], bc3(gs[:, 1, :], [P, J, E], 2), ALU.mult))
                take_wait()
                for j in range(J):
                    i = dve.max(m8[:, j, :], lg[:, j, :])
                c(i)
                take_wait()
                for j in range(J):
                    i = dve.max_index(i8[:, j, :], m8[:, j, :], lg[:, j, :])
                c(i)
                c(dve.tensor_copy(i8f[:, :, 0:2], i8[:, :, 0:2]))
                for a in range(2):
                    i = dve.tensor_tensor(eq[:, a, :, :], bc3(iota[:, :], [P, J, E], 1),
                                          bc3(i8f[:, :, a], [P, J, E], 2), ALU.is_equal)
                c(i)
                c(dve.tensor_tensor(eq[:, 0, :, :], eq[:, 0, :, :], eq[:, 1, :, :], ALU.add))
                assert c.n == K3
                dve.memset(C9[:, :, E:E + 1], 1.0)
                dve.tensor_tensor(C9[:, :, 0:E], eq[:, 0, :, :], lg[:, :, :], ALU.mult).then_inc(sem("f3_c"), 1)
                dve.wait_ge(*at("f3_c", g + 1))
                for u in range(NU + 3):
                    if u < NU:
                        j, pr = u // 5, u % 5
                        ne = 2 if pr < 4 else 1
                        dve.wait_ge(*at("f3_silu", NU * g + u + 1))
                        dve.wait_ge(*at("f3_ht", NU * g + u - 1 if u >= 2 else NU * g))
                        for a in range(ne):
                            i = dve.scalar_tensor_tensor(hid[:, u % 2, a * P:(a + 1) * P],
                                                         bank[u % 2][:, a * 256 + P:(a + 1) * 256],
                                                         C9[:, j, 2 * pr + a:2 * pr + a + 1],
                                                         mlpg[:, u % 2, a * P:(a + 1) * P], ALU.mult, ALU.mult)
                        i.then_inc(sem("f3_prod"), 1)
                    if u >= 7 and (u - 7) % 5 == 0:
                        j = (u - 7) // 5
                        dve.wait_ge(*at("f3_dn", NU * g + 5 * (j + 1)))
                        t = J * g + j
                        dve.tensor_tensor(X[:, t, :], bank[4 + j % 2][:, 0:D], X[:, t, :], ALU.add
                                          ).then_inc(sem("f3_x"), 1)


_INS = ['x', 'ctx_1024', 'mask_BxS2_bk0', 'L0_xattn_Wq', 'L0_xattn_Wk', 'L0_xattn_Wv', 'L0_xattn_Wo', 'L0_xattn_bo',
        'L0_ffn_norm_weight', 'L0_ffn_gate_weight', 'L0_ffn_gate_bias', 'L0_ffn_mlp1_weight', 'L0_ffn_mlp1_bias',
        'L0_ffn_mlp2_weight', 'L0_ffn_mlp2_bias', 'L1_xattn_wq_w', 'L1_xattn_wq_b', 'L1_xattn_wk_w', 'L1_xattn_wk_b',
        'L1_xattn_wv_w', 'L1_xattn_wv_b', 'L1_xattn_dense_w', 'L1_xattn_dense_b', 'L1_ffn_Wr', 'L1_ffn_W1',
        'L1_ffn_W2', 'L2_xattn_W', 'L2_xattn_b', 'L2_ffn_W1', 'L2_ffn_b1', 'L2_ffn_W2', 'L2_ffn_b2', 'L3_xattn_W',
        'L3_xattn_b', 'L3_ffn_gate_w', 'L3_ffn_w1', 'L3_ffn_w2', 'L3_ffn_w3', 'L3_ffn_w1s', 'L3_ffn_w2s', 'L3_ffn_w3s']


def kernel(**inputs):
    import concourse.bacc as _bacc
    from concourse.bass_utils import run_bass_kernel_spmd as _run

    nc = _bacc.Bacc("TRN2", target_bir_lowering=False, num_devices=1)
    arrays, args = {}, {}
    for name in _INS:
        a = np.ascontiguousarray(inputs[name])
        if a.dtype == np.bool_:
            a = a.reshape(-1).view(np.int32)
        arrays["in_" + name] = a
        args[name] = nc.dram_tensor("in_" + name, a.shape, mybir.dt.from_np(a.dtype), kind="ExternalInput").ap()
    out = nc.dram_tensor("out_0", (B, SEQ, D), F32, kind="ExternalOutput").ap()
    build(nc, args, out)
    r = _run(nc, [arrays], core_ids=[0])
    return r.results[0]["out_0"]
```

```python
import numpy as np
import concourse.bass as bass
from concourse import mybir
from contextlib import ExitStack

F32 = mybir.dt.float32
BF16 = mybir.dt.bfloat16
U8 = mybir.dt.uint8
U32 = mybir.dt.uint32
I32 = mybir.dt.int32
ALU = mybir.AluOpType
ACT = mybir.ActivationFunctionType
AXX = mybir.AxisListType.X

P = 128
B, SEQ, D = 4, 512, 128
G, J = B, SEQ // P
T = G * J
M = 77
H = 16
DH0, DH1 = 64, D // H
HM = H * M
NK = -(-HM // P)
CH = [min(P, HM - P * k) for k in range(NK)]
HEADS = [(0, 5), (5, 10), (10, 16)]
E = 8
F = 512
FC = F // P
CAP = T * P // E
LN_EPS = 1e-5
LIMIT, ALPHA = 7.0, 1.702
MASKED = -1e30
NZERO = T // 4 + 6
NCONST = 20
NBLK = (T * P + E * (P - 1)) // P
NU = 5 * J

STAGES = ["a0", "f0", "a1", "f1", "a2", "f2", "a3", "f3"]
HEADED = ["a0", "a1"]
SIGNALS = {k: [(s, G) for s in STAGES] for k in ("st", "ln")}
SIGNALS |= {k: [(s, G) for s in STAGES if s != "f2"] for k in ("xt", "xte")}
SIGNALS |= {k: [(s, 1) for s in STAGES] for k in ("ve", "rstd")}
SIGNALS |= {"nv": [(s, 2) for s in STAGES]}
SIGNALS |= {k: [(s, 3 * T) for s in HEADED] + [("a3", G)] for k in ("sc", "sub", "pt")}
SIGNALS |= {k: [(s, T) for s in HEADED] + [("a2", G), ("a3", G)] for k in ("out",)}
SIGNALS |= {k: [(s, T) for s in HEADED] for k in ("sm", "rs", "p")}
SIGNALS |= {"mx": [(s, 3 * T) for s in HEADED], "exp": [("a0", T), ("a1", T), ("a3", G)],
            "pte": [("a0", 4 * T), ("a1", 4 * T), ("a3", G)], "xb": [("a0", G), ("a1", G), ("a2", G)],
            "x": [("a0", T), ("f0", G), ("a1", T), ("a2", G), ("a3", T), ("f3", T)],
            "q": [("a1", G), ("a3", G)], "qe": [("a1", G), ("a3", G)],
            "lg": [("f0", 1), ("f1", 1), ("f3", 1)], "lge": [("f0", 1), ("f1", 1), ("f3", 1)],
            "gap": [("f0", 1), ("f1", 1), ("a3", G), ("f3", 1)], "gexp": [("f0", 1), ("f1", 1), ("f3", 1)],
            "acc": [("f0", E * G)],
            "dn": [("f0", E * G), ("f1", E), ("f2", 2 * NBLK), ("f3", NU * G)],
            "up": [("f0", E * G), ("f1", 2 * E), ("f2", 2 * NBLK), ("f3", NU * G)],
            "h": [("f1", 2 * E), ("f2", 2 * NBLK)]}
SIGNALS |= {k: [("f1", E), ("f2", 2 * NBLK)] for k in ("w1", "w2")}
SIGNALS |= {k: [("f1", E), ("f2", NBLK)] for k in ("y",)}
SIGNALS |= {k: [("f1", 16 * E), ("f2", 16 * NBLK)] for k in ("yst",)}
SIGNALS |= {k: [("f1", 16 * T), ("f2", 16 * T)] for k in ("put", "got")}
SIGNALS |= {"idx": [("f1", 1), ("f2", 1)], "rk": [("f1", 1), ("f2", 1)], "pre": [("f1", 1), ("f2", 1)],
            "bt": [("f1", 4), ("f2", 6)], "bte": [("f1", 4), ("f2", 6)], "xs": [("f1", 16), ("f2", 16)],
            "add": [("f1", G), ("f2", G)]}


FROM_ONE = ["acc", "dn", "h", "f0_act", "f0_gb", "f0_lb", "f0_sg", "f0_gl", "f3_prod", "f3_hte", "f3_ht"]


HORD = [0, 2, 4, 6, 1, 3, 5, 7, 8, 10, 12, 14, 9, 11, 13, 15]


def later(n):
    return not isinstance(n, int) or n > 0


class Steps:

    def __init__(self, eng, sem, base=0):
        self.eng, self.sem, self.base, self.n = eng, sem, base, 0

    def __call__(self, ins):
        self.n += 1
        ins.then_inc(self.sem, 1)
        self.eng.wait_ge(self.sem, self.base + self.n)


def build(nc, A, out):
    ctx = ExitStack()
    with ctx:
        def sb(name, shape, dt=F32):
            return ctx.enter_context(nc.sbuf_tensor(name, shape, dt))

        sems = {}

        def sem(name):
            stage, _, signal = name.partition("_")
            if stage in STAGES and signal in SIGNALS:
                name = signal
            if name not in sems:
                sems[name] = ctx.enter_context(nc.semaphore(name))
            return sems[name]

        def at(name, n):
            stage, _, signal = name.partition("_")
            base = 1 if name in FROM_ONE or (stage in STAGES and signal in FROM_ONE) else 0
            for s, count in SIGNALS.get(signal, ()) if stage in STAGES else ():
                if s == stage:
                    return sem(name), n + base
                base += count
            assert stage not in STAGES or signal not in SIGNALS, name
            return sem(name), n + base

        X = sb("X", [P, T, D])
        xn = sb("xn", [P, T, D])
        xnT = sb("xnT", [P, G, SEQ])
        grpque = sb("grpque", [P, 2, J, P])
        grpT = grpque[:, 0, :, :]
        queT = grpque[:, 1, :, :]
        xc = grpque[:, :, :, :].rearrange("p a j n -> p (a j n)").bitcast(BF16).rearrange("p (t d) -> p t d", t=T)
        nrm = xnT[:, 0:2, :].rearrange("p a n -> p (a n)").bitcast(BF16).rearrange("p (t d) -> p t d", t=T)
        nT = xnT[:, 2:4, :].rearrange("p a n -> p (a n)").bitcast(BF16).rearrange("p (g n) -> p g n", g=G)
        ident = sb("ident", [P, P])
        identb = sb("identb", [P, P], BF16)
        ctxr = sb("ctxr", [M, B, D])
        ctxT = sb("ctxT", [P, B * M])
        prb = sb("prb", [P, 4, HM])
        prT = sb("prT", [P, 2, NK * P])
        R1 = sb("R1", [P, B * HM + B * NK * P])
        R2 = sb("R2", [P, B * HM + B * NK * P])
        R3 = sb("R3", [P, 2 * E * F])
        keys0 = R1[:, 0:B * HM].rearrange("p (b n) -> p b n", b=B)
        vals0 = R1[:, B * HM:].rearrange("p (b k n) -> p b k n", b=B, k=NK)
        keys1 = R2[:, 0:B * HM].rearrange("p (b n) -> p b n", b=B)
        vals1 = R2[:, B * HM:].rearrange("p (b k n) -> p b k n", b=B, k=NK)
        w1_l1 = R3[:, 0:E * F].rearrange("p (e n) -> p e n", e=E)
        w2_l1 = R3[:, E * F:].rearrange("p (e c n) -> p e c n", e=E, c=FC)
        w1_l2 = R1[:, 0:E * F].rearrange("p (e n) -> p e n", e=E)
        w2_l2 = R1[:, B * HM:B * HM + E * F].rearrange("p (e c n) -> p e c n", e=E, c=FC)
        w13_l3 = R2[:, 0:9 * 256].rearrange("p (e n) -> p e n", e=9)
        w2_l3 = R2[:, 9 * 256:9 * 384].rearrange("p (e n) -> p e n", e=9)
        wq = R3[:, 0:1024]
        wk = R3[:, 1024:2048]
        wv = R3[:, 2048:3072]
        wo = R3[:, 3072:4096].rearrange("p (c n) -> p c n", c=8)
        wqT = R3[:, 4096:5120].rearrange("p (c n) -> p c n", c=8)
        w4r = R3[:, 7584:8096].rearrange("p (a n) -> p a n", a=4)
        kT = R3[:, 5120:5120 + 8 * B * M].rearrange("p (c n) -> p c n", c=8)
        vT = prT[:, :, :].rearrange("p a n -> p (a n)")[:, 0:8 * B * M].rearrange("p (c n) -> p c n", c=8)
        vstage = R2[0:M, 0:B * H * D].rearrange("p (b h n) -> p b h n", b=B, h=H)
        prbf = prb[:, :, :].rearrange("p a n -> p (a n)")
        kvT1 = prbf[:, 0:2 * B * M].rearrange("p (a n) -> p a n", a=2)
        vblk = prbf[:, 640:640 + 2 * HM].rearrange("p (a n) -> p a n", a=2)
        w3r = prbf[:, 3712:4096].rearrange("p (a n) -> p a n", a=3)
        zero = R1[:, B * HM:B * HM + F]
        csB = prbf[:, 3200:3200 + B * P].rearrange("p (b n) -> p b n", b=B)
        acc = prbf[:, 0:T * D].rearrange("p (t n) -> p t n", t=T)
        hid = prbf[:, 2048:2048 + 4 * SEQ].rearrange("p (a n) -> p a n", a=4)
        mlpg = prT[:, 0, 0:2 * SEQ].rearrange("p (a n) -> p a n", a=2)
        srt1 = R2[:, 3456:3456 + T * D].rearrange("p (k n) -> p k n", k=T)
        res1 = R2[:, 5504:5504 + T * D].rearrange("p (k n) -> p k n", k=T)
        srt2 = R3[:, 0:NBLK * D].rearrange("p (k n) -> p k n", k=NBLK)
        res2 = R3[:, NBLK * D:2 * NBLK * D].rearrange("p (k n) -> p k n", k=NBLK)
        srtT = prbf[:, 0:NBLK * P]
        hid1 = prbf[:, 2048:2048 + 2 * FC * 256].rearrange("p (a c n) -> p a c n", a=2, c=FC)
        hid2 = prbf[:, NBLK * P:NBLK * P + 2 * FC * P].rearrange("p (a c n) -> p a c n", a=2, c=FC)
        back = prbf[:, 0:T * D].rearrange("p (t n) -> p t n", t=T)
        mlpl = prT[:, 1, 0:2 * SEQ].rearrange("p (a n) -> p a n", a=2)

        w4T = sb("w4T", [P, 4, D])
        w3T = sb("w3T", [P, 3, D])
        gw3r = sb("gw3r", [E, D])
        gw3T = sb("gw3T", [P, E])
        wr1 = sb("wr1", [P, E])
        gw0r = sb("gw0r", [E, D], BF16)
        gw0T = sb("gw0T", [P, E], BF16)
        m1r = prT[:, 1, 0:1024].bitcast(BF16).rearrange("p (e n) -> p e n", e=E)
        m1T = sb("m1T", [P, E * 2, P], BF16)
        m2r = prT[:, 0, 0:512].bitcast(BF16).rearrange("p (e n) -> p e n", e=E)
        m2T = sb("m2T", [P, E, P])
        wsel1 = m1T[:, :, :].rearrange("p a n -> p (a n)").bitcast(F32).rearrange("p (a n) -> p a n", a=2)
        wsel2 = m2T[:, :, :].rearrange("p (a c) n -> p a c n", a=2)
        b2pair = R2[:, 7552:7552 + E * D].rearrange("p (e n) -> p e n", e=E)
        m1br = sb("m1br", [E, 2 * P], BF16)
        m1bT = sb("m1bT", [P, 2, E])
        b1r = sb("b1r", [E * FC, P])
        b1T = sb("b1T", [P, E * FC])
        nwB = sb("nwB", [P, D])
        gbB = sb("gbB", [P, E], BF16)
        boB = sb("boB", [P, 3, D])
        cols = sb("cols", [P, 4])
        rowc = sb("rowc", [P, B, D])
        ypT = sb("ypT", [P, B * M])
        maskw = sb("maskw", [P, M], I32)
        maskf = sb("maskf", [P, B, M])
        blk = sb("blk", [P, H])
        lower = sb("lower", [P, P], BF16)
        onesb = sb("onesb", [P, P], BF16)
        iota = sb("iota", [P, E])
        nhalf = sb("nhalf", [P, T])
        pad = sb("pad", [P, 1])
        st = sb("st", [P, T, 6])
        nv = sb("nv", [P, 5, T])
        mean = sb("mean", [P, T])
        ve = sb("ve", [P, T])
        rstd = sb("rstd", [P, T])
        mx = sb("mx", [P, 2, H])
        sm = sb("sm", [P, 2, H])
        rs = sb("rs", [P, 2, H])
        csum = sb("csum", [P, B])
        C9 = sb("C9", [P, T, E + 1])
        C = sb("C", [P, T, E])
        lg = sb("lg", [P, T, E])
        lg2 = sb("lg2", [P, T, E])
        lgb = sb("lgb", [P, T, E], BF16)
        tA = sb("tA", [P, T, E])
        gs = sb("gs", [P, 12, T])
        gi = sb("gi", [P, T], I32)
        oh = sb("oh", [P, 2, T, E])
        ohb = sb("ohb", [P, 2, T, E], BF16)
        pre = sb("pre", [P, 2, E + T, E])
        blkc = sb("blkc", [P, NBLK, E])
        tot = sb("tot", [P, E])
        nblk = sb("nblk", [P, 3, E])
        cmp = sb("cmp", [P, E, 32])
        thr = sb("thr", [P, T])
        kio = sb("kio", [P, 32])
        lowE = sb("lowE", [P, E, E])
        tab = sb("tab", [P, 2, NBLK])
        tabi = sb("tabi", [P, NBLK, 2], I32)
        idx = sb("idx", [P, 2, T], I32)
        tok = sb("tok", [P, T])
        accb = sb("accb", [P, J, D], BF16)
        m2row = sb("m2row", [1, E, D], BF16)
        b2first = sb("b2first", [P, D])
        i32 = sb("i32", [P, 32], I32)
        rows1 = nc.dram_tensor("rows1", [2 * T * P, D], F32, kind="Internal").ap()
        outs1 = nc.dram_tensor("outs1", [T * P, D], F32, kind="Internal").ap()
        rows2 = nc.dram_tensor("rows2", [NBLK * P, D], F32, kind="Internal").ap()
        outs2 = nc.dram_tensor("outs2", [NBLK * P, D], F32, kind="Internal").ap()
        vwd = nc.dram_tensor("vwd", [B, HM, D], F32, kind="Internal").ap()

        bank = [ctx.enter_context(nc.psum_tensor(f"bank{i}", [P, 512], F32)) for i in range(8)]

        def b4(i):
            return bank[i][:, :].rearrange("p (j n) -> p j n", j=4)

        def bb(i):
            return bank[i][:, :].bitcast(BF16).rearrange("p (j n) -> p j n", j=8)

        block = ctx.enter_context(nc.Block())

        J_CTX, J_WQ, J_K, J_A, J_V, J_VW = 0, 1, 3, 11, 27, 35
        J_W4 = J_VW + 16
        J_K1, J_V1 = J_W4 + 1, J_W4 + 2
        J_VB = J_V1 + 1
        J_W3 = J_VB + 3 * B
        J_SM = J_W3 + 1
        J_M1 = J_SM + 1
        J_M2 = J_M1 + 2
        J_SMB = J_M2 + 1
        J_ROW = J_SMB + 1
        J_YP = J_ROW + 1
        J_END = J_YP + 1

        @block.sync
        def _(sp):
            sp.dma_start(ctxr[:, :, :], A["ctx_1024"].rearrange("b m d -> m b d")).then_inc(sem("ld_ctx"), 16)
            sp.dma_start(wq, A["L0_xattn_Wq"]).then_inc(sem("ld_wq"), 16)
            sp.dma_start(wk, A["L0_xattn_Wk"]).then_inc(sem("ld_wk"), 16)
            sp.dma_start(X[:, :, :], A["x"].rearrange("b (j p) d -> p (b j) d", p=P)).then_inc(sem("ld_x"), 16)
            sp.dma_start(wv, A["L0_xattn_Wv"]).then_inc(sem("ld_wv"), 16)
            sp.dma_start(wo, A["L0_xattn_Wo"].rearrange("(c p) n -> p c n", p=P)).then_inc(sem("ld_wo"), 16)
            for n, w in enumerate(["wq_w", "wk_w", "wv_w", "dense_w"]):
                sp.dma_start(w4r[:, n, :], A["L1_xattn_" + w]).then_inc(sem("ld_w4"), 16)
            for n, w in enumerate(["L1_xattn_wq_b", "L1_xattn_wk_b", "L1_xattn_wv_b", "L3_xattn_b"]):
                sp.dma_start(cols[:, n:n + 1], A[w].rearrange("(p a) -> p a", a=1)).then_inc(sem("ld_cols"), 16)
            for n, w in enumerate(["L0_xattn_bo", "L1_xattn_dense_b", "L2_xattn_b"]):
                sp.dma_start(boB[:, n, :], A[w].rearrange("(a n) -> a n", a=1).partition_broadcast(P)
                             ).then_inc(sem("ld_bo"), 16)
            sp.dma_start(w3r[:, 0:2, :], A["L2_xattn_W"].rearrange("p (a n) -> p a n", a=2)).then_inc(sem("ld_w3"), 16)
            sp.dma_start(w3r[:, 2, :], A["L3_xattn_W"]).then_inc(sem("ld_w3"), 16)
            sp.dma_start(gw3r[:, :], A["L3_ffn_gate_w"]).then_inc(sem("ld_small"), 16)
            sp.dma_start(b1r[:, :], A["L2_ffn_b1"].rearrange("e (c p) -> (e c) p", p=P)).then_inc(sem("ld_small"), 16)
            sp.dma_start(gw0r[:, :], A["L0_ffn_gate_weight"]).then_inc(sem("ld_small"), 16)
            sp.dma_start(m1br[:, :], A["L0_ffn_mlp1_bias"]).then_inc(sem("ld_small"), 16)
            sp.dma_start(m2row[:, :, :], A["L0_ffn_mlp2_bias"].rearrange("(a e) d -> a e d", a=1)
                         ).then_inc(sem("ld_later"), 16)
            sp.dma_start(wr1[:, :], A["L1_ffn_Wr"]).then_inc(sem("ld_later"), 16)
            sp.dma_start(nwB[:, :], A["L0_ffn_norm_weight"].rearrange("(a n) -> a n", a=1).partition_broadcast(P)
                         ).then_inc(sem("ld_later"), 16)
            sp.dma_start(gbB[:, :], A["L0_ffn_gate_bias"].rearrange("(a n) -> a n", a=1).partition_broadcast(P)
                         ).then_inc(sem("ld_later"), 16)
            sp.dma_start(maskw[:, :], A["mask_BxS2_bk0"].rearrange("(a n) -> a n", a=1).partition_broadcast(P)
                         ).then_inc(sem("ld_later"), 16)
            sp.wait_ge(*at("consts", 2))
            z = zero[:, :].rearrange("p (k d) -> p k d", d=D)
            for rows, n in ((rows1, T), (rows2, NBLK)):
                for k in range(0, n, 4):
                    m = min(4, n - k)
                    sp.dma_start(rows[k * P:(k + m) * P, :].rearrange("(k p) d -> p k d", p=P), z[:, 0:m, :]
                                 ).then_inc(sem("zeroed"), 16)
            for b in range(B):
                sp.wait_ge(*at("prep_ev", J_VW + 4 * (b + 1)))
                sp.dma_start(vwd[b, :, :].rearrange("(h m) n -> m h n", h=H), vstage[:, b, :, :]
                             ).then_inc(sem("vw_out"), 16)
            sp.wait_ge(*at("vw_out", 16 * B))
            sp.wait_ge(*at("zeroed", 16 * NZERO))
            for b in range(B):
                sp.dma_start(vals0[:, b, 0:NK - 1, :], vwd[b, 0:(NK - 1) * P, :].rearrange("(k p) n -> p k n", p=P)
                             ).then_inc(sem("vw_in"), 16)
                sp.dma_start(vals0[0:CH[-1], b, NK - 1, :], vwd[b, (NK - 1) * P:HM, :]).then_inc(sem("vw_in"), 16)
            sp.wait_ge(*at("prep_mm", J_VW + 16))
            sp.dma_start(m1r, A["L0_ffn_mlp1_weight"].rearrange("e (i two) h -> i e (two h)", two=2)
                         ).then_inc(sem("ld_m"), 16)
            sp.dma_start(m2r, A["L0_ffn_mlp2_weight"].rearrange("e h i -> h e i")).then_inc(sem("ld_m"), 16)
            sp.wait_ge(*at("prep_mm", J_W4 + 1))
            sp.dma_start(w1_l1, A["L1_ffn_W1"].rearrange("e d f -> d e f")).then_inc(sem("ld_w1_l1"), 16)
            sp.dma_start(w2_l1, A["L1_ffn_W2"].rearrange("e (c p) n -> p e c n", p=P)).then_inc(sem("ld_w2_l1"), 16)
            sp.wait_ge(*at("a0_out", T))
            sp.dma_start(w1_l2, A["L2_ffn_W1"].rearrange("e d f -> d e f")).then_inc(sem("ld_w1_l2"), 16)
            sp.dma_start(w2_l2, A["L2_ffn_W2"].rearrange("e (c p) n -> p e c n", p=P)).then_inc(sem("ld_w2_l2"), 16)
            sp.wait_ge(*at("a1_out", T))
            sp.dma_start(b2pair, A["L2_ffn_b2"].rearrange("(a e) d -> a e d", a=1).partition_broadcast(P)
                         ).then_inc(sem("ld_b2"), 16)
            for n, (w1, w3, w2) in enumerate([("w1", "w3", "w2"), ("w1s", "w3s", "w2s")]):
                e0, ne = (0, E) if n == 0 else (E, 1)
                sp.dma_start(w13_l3[:, e0:e0 + ne, 0:P], A["L3_ffn_" + w1].rearrange("e d n -> d e n")
                             ).then_inc(sem("ld_w_l3"), 16)
                sp.dma_start(w13_l3[:, e0:e0 + ne, P:2 * P], A["L3_ffn_" + w3].rearrange("e d n -> d e n")
                             ).then_inc(sem("ld_w_l3"), 16)
                sp.dma_start(w2_l3[:, e0:e0 + ne, :], A["L3_ffn_" + w2].rearrange("e d n -> d e n")
                             ).then_inc(sem("ld_w_l3"), 16)
            def sorted_rows(name, n_it, rows, srt, res, outs, per):
                sp.wait_ge(*at(name + "_put", 16 * T))
                n = n_it * per
                sp.dma_start(srt[:, :, :], rows[0:n * P, :].rearrange("(k p) d -> p k d", p=P)
                             ).then_inc(sem(name + "_xs"), 16)
                with sp.Fori(0, n_it) as k:
                    sp.wait_ge(*at(name + "_y", k + 1))
                    sp.dma_start(outs.rearrange("(k r p) d -> p k r d", p=P, r=per)[:, k, :, :],
                                 res.rearrange("p (k r) d -> p k r d", r=per)[:, k, :, :]
                                 ).then_inc(sem(name + "_yst"), 16)

            sorted_rows("f1", E, rows1, srt1, res1, outs1, 2)
            sorted_rows("f2", NBLK, rows2, srt2, res2, outs2, 1)
            with sp.Fori(0, G) as g:
                sp.wait_ge(*at("f3_x", J * (g + 1)))
                sp.dma_start(out.rearrange("b (j p) d -> p b j d", p=P)[:, g, :, :], X[:, :, :].rearrange(
                    "p (b j) d -> p b j d", b=B)[:, g, :, :]).then_inc(sem("stored"), 16)
            sp.wait_ge(*at("stored", 16 * G))

        @block.gpsimd
        def _(pool):
            for name in FROM_ONE:
                pool.sem_inc(sem(name), 1)
            c = Steps(pool, sem("consts"))
            c(pool.memset(ident[:, :], 0.0))
            c(pool.memset(zero[:, :], 0.0))
            c(pool.affine_select(out=ident[:, :], in_=ident[:, :], compare_op=ALU.not_equal, fill=1.0,
                                 base=0, pattern=[[-1, P]], channel_multiplier=1))
            c(pool.tensor_copy(identb[:, :], ident[:, :]))
            c(pool.memset(nhalf[:, :], -0.5))
            c(pool.memset(blk[:, :], 1.0))
            c(pool.affine_select(out=blk[:, :], in_=blk[:, :], compare_op=ALU.is_ge, fill=0.0,
                                 base=0, pattern=[[-DH1, H]], channel_multiplier=1))
            c(pool.affine_select(out=blk[:, :], in_=blk[:, :], compare_op=ALU.is_ge, fill=0.0,
                                 base=DH1 - 1, pattern=[[DH1, H]], channel_multiplier=-1))
            c(pool.memset(onesb[:, :], 1.0))
            c(pool.affine_select(out=lower[:, :], in_=onesb[:, :], compare_op=ALU.is_gt, fill=0.0,
                                 base=0, pattern=[[1, P]], channel_multiplier=-1))
            c(pool.iota(i32[:, :], pattern=[[1, 32]], base=0, channel_multiplier=0))
            c(pool.tensor_copy(kio[:, :], i32[:, :]))
            c(pool.tensor_scalar(iota[:, :], kio[:, 0:E], float(E), None, ALU.subtract))
            c(pool.tensor_scalar(thr[:, :], kio[:, 0:T], float(P), None, ALU.mult))
            c(pool.iota(i32[:, 0:T], pattern=[[P, T]], base=T * P, channel_multiplier=1))
            c(pool.tensor_copy(tok[:, :], i32[:, 0:T]))
            c(pool.memset(lowE[:, :, :], 1.0))
            c(pool.affine_select(out=lowE[:, :, :], in_=lowE[:, :, :], compare_op=ALU.is_gt, fill=0.0,
                                 base=0, pattern=[[1, E], [-1, E]], channel_multiplier=0))
            c(pool.memset(pre[:, :, :, :], 0.0))
            pool.wait_ge(*at("ld_later", 80))
            c(pool.tensor_copy(maskf[:, :, :].rearrange("p b m -> p (b m)"), maskw[:, :].bitcast(U8)))
            assert c.n == NCONST
            def pow_rstd(name):
                pool.wait_ge(*at(name + "_ve", 1))
                pool.tensor_tensor(rstd[:, :], ve[:, :], nhalf[:, :], ALU.pow).then_inc(sem(name + "_rstd"), 1)

            def attention(name, bias):
                def scale(g, j):
                    t = J * g + j
                    pool.wait_ge(*at(name + "_rs", t + 1))
                    pool.tensor_tensor(prb[:, j, :].rearrange("p (h m) -> p h m", h=H),
                                       prb[:, j, :].rearrange("p (h m) -> p h m", h=H),
                                       rs[:, j % 2, :].unsqueeze(2).to_broadcast([P, H, M]),
                                       ALU.mult).then_inc(sem(name + "_p"), 1)

                def group(g, first):
                    pool.wait_ge(*at(name + "_ln", G))
                    pool.tensor_tensor(X4(g), X4(g), boB[:, bias, :].unsqueeze(1).to_broadcast([P, J, D]),
                                       ALU.add).then_inc(sem(name + "_xb"), 1)
                    for j in range(J):
                        if not (first and j == 0):
                            scale(*((g, j - 1) if j else (g - 1, J - 1)))

                pow_rstd(name)
                group(0, True)
                with pool.Fori(1, G) as g:
                    group(g, False)
                scale(G - 1, J - 1)

            def X4(g):
                return X[:, :, :].rearrange("p (g j) d -> p g (j d)", g=G)[:, g, :].rearrange(
                    "p (j d) -> p j d", j=J)

            pool.wait_ge(*at("ld_bo", 48))
            attention("a0", 0)
            pow_rstd("f0")
            pool.wait_ge(*at("f0_ms", 1))
            pool.tensor_tensor(gs[:, 1, :], gs[:, 0, :], nhalf[:, :], ALU.pow).then_inc(sem("f0_rms"), 1)
            with pool.Fori(0, G) as g:
                for e in range(E):
                    n = E * g + e
                    pool.wait_ge(*at("f0_gl", n + 1))
                    pool.wait_ge(*at("f0_sg", n + 1))
                    pool.tensor_tensor(hid[:, e % 2, :], hid[:, e % 2, :], hid[:, 2 + e % 2, :],
                                       ALU.mult).then_inc(sem("f0_act"), 1)
            attention("a1", 1)

            def dispatch(name, rows, outs):
                pool.wait_ge(*at(name + "_idx", 1))
                pool.wait_ge(*at("zeroed", 16 * NZERO))
                for t in range(T):
                    pool.indirect_dma_start(out=rows, out_offset=bass.IndirectOffsetOnAxis(ap=idx[:, 0, t:t + 1], axis=0),
                                            in_=xn[:, t, :], in_offset=None).then_inc(sem(name + "_put"), 16)

            def collect(name, n, outs):
                pool.wait_ge(*at(name + "_yst", 16 * n))
                for t in range(T):
                    pool.indirect_dma_start(out=back[:, t, :], out_offset=None, in_=outs,
                                            in_offset=bass.IndirectOffsetOnAxis(ap=idx[:, 1, t:t + 1], axis=0)
                                            ).then_inc(sem(name + "_got"), 16)

            pow_rstd("f1")
            dispatch("f1", rows1, outs1)
            pool.wait_ge(*at("ld_b2", 16))
            pool.tensor_copy(b2first[:, :], b2pair[:, 0, :]).then_inc(sem("b2p"), 1)
            pool.wait_ge(*at("b2p", 1))
            for e in range(E):
                pool.tensor_tensor(b2pair[:, e, :], b2pair[:, e, :], b2pair[:, e + 1, :] if e + 1 < E else b2first[:, :],
                                   ALU.add).then_inc(sem("b2p"), 1)
                pool.wait_ge(*at("b2p", e + 2))

            collect("f1", E, outs1)
            pow_rstd("a2")
            pool.wait_ge(*at("a2_ln", G))
            with pool.Fori(0, G) as g:
                pool.tensor_tensor(X4(g), X4(g), rowc[:, g, :].unsqueeze(1).to_broadcast([P, J, D]),
                                   ALU.add).then_inc(sem("a2_xb"), 1)
            pow_rstd("f2")
            dispatch("f2", rows2, outs2)
            collect("f2", NBLK, outs2)
            pow_rstd("a3")
            pow_rstd("f3")

        @block.tensor
        def _(pe):
            job = [0]

            def begin(n):
                assert n == job[0]
                if n >= 8:
                    pe.wait_ge(*at("prep_ev", n - 7))
                return n % 8

            def end(ins):
                ins.then_inc(sem("prep_mm"), 1)
                job[0] += 1

            def mm(o, l, r, start=True, stop=True):
                return pe.matmul(o, l, r, start=start, stop=stop)

            pe.wait_ge(*at("consts", 4))
            pe.wait_ge(*at("ld_ctx", 16))
            k = begin(J_CTX)
            for b in range(B):
                i = pe.transpose(bank[k][:, b * M:(b + 1) * M], ctxr[:, b, :], ident[0:M, 0:M])
            end(i)
            pe.wait_ge(*at("ld_wq", 16))
            for a in range(2):
                k = begin(J_WQ + a)
                for c in range(4):
                    i = pe.transpose(b4(k)[:, c, :], wq[:, (4 * a + c) * P:(4 * a + c + 1) * P], ident[:, :])
                end(i)
            pe.wait_ge(*at("ld_wk", 16))
            pe.wait_ge(*at("prep_ev", J_CTX + 1))
            for c in range(8):
                k = begin(J_K + c)
                end(mm(bank[k][:, 0:B * M], wk[:, c * P:(c + 1) * P], ctxT[:, :]))
            for h in range(H):
                k = begin(J_A + h)
                o = DH0 * (h % 2)
                pe.wait_ge(*at("prep_ev", J_K + h // 2 + 1))
                end(mm(bank[k][:, 0:B * M], wqT[o:o + DH0, h // 2, :], kT[o:o + DH0, h // 2, :]))
            pe.wait_ge(*at("ld_wv", 16))
            for c in range(8):
                k = begin(J_V + c)
                end(mm(bank[k][:, 0:B * M], wv[:, c * P:(c + 1) * P], ctxT[:, :]))
            pe.wait_ge(*at("ld_wo", 16))
            pe.wait_ge(*at("prep_ev", J_V + 8))
            for b in range(B):
                for q in range(4):
                    k = begin(J_VW + 4 * b + q)
                    for a, h in enumerate(HORD[4 * q:4 * q + 4]):
                        o = DH0 * (h % 2)
                        i = mm(b4(k)[0:M, a, :], vT[o:o + DH0, h // 2, b * M:(b + 1) * M], wo[o:o + DH0, h // 2, :])
                    end(i)
            pe.wait_ge(*at("ld_w4", 64))
            k = begin(J_W4)
            for a in range(4):
                i = pe.transpose(b4(k)[:, a, :], w4r[:, a, :], ident[:, :])
            end(i)
            for a, jn in ((1, J_K1), (2, J_V1)):
                k = begin(jn)
                if a == 1:
                    pe.wait_ge(*at("prep_ev", J_W4 + 1))
                end(mm(bank[k][:, 0:B * M], w4T[:, a, :], ctxT[:, :]))
            for b in range(B):
                pe.wait_ge(*at("vblk", b + 1))
                for q in range(3):
                    k = begin(J_VB + 3 * b + q)
                    for kk in range(4 * q, min(4 * q + 4, NK)):
                        i = mm(b4(k)[0:CH[kk], kk % 4, :], vblk[:, b % 2, kk * P:kk * P + CH[kk]], w4T[:, 3, :])
                    end(i)
            pe.wait_ge(*at("ld_w3", 32))
            k = begin(J_W3)
            for a in range(3):
                i = pe.transpose(b4(k)[:, a, :], w3r[:, a, :], ident[:, :])
            end(i)
            pe.wait_ge(*at("ld_small", 64))
            k = begin(J_SM)
            pe.transpose(bank[k][:, 0:E], gw3r[:, :], ident[0:E, 0:E])
            end(pe.transpose(bank[k][:, E:E + E * FC], b1r[:, :], ident[0:E * FC, 0:E * FC]))
            pe.wait_ge(*at("ld_m", 32))
            for a in range(2):
                k = begin(J_M1 + a)
                for c in range(8):
                    n = 8 * a + c
                    i = pe.transpose(bb(k)[:, c, :], m1r[:, n // 2, (n % 2) * P:(n % 2 + 1) * P], identb[:, :])
                end(i)
            k = begin(J_M2)
            for c in range(E):
                i = pe.transpose(bb(k)[:, c, :], m2r[:, c, :], identb[:, :])
            end(i)
            k = begin(J_SMB)
            pe.transpose(bb(k)[:, 0, 0:E], gw0r[:, :], identb[0:E, 0:E])
            for a in range(2):
                i = pe.transpose(bb(k)[:, 0, E * (a + 1):E * (a + 2)], m1br[:, a:2 * P:2], identb[0:E, 0:E])
            end(i)
            k = begin(J_ROW)
            pe.wait_ge(*at("csum", 2))
            pe.wait_ge(*at("prep_ev", J_W3 + 1))
            for b in range(B):
                i = mm(b4(k)[:, b, :], csB[:, b, :], w3T[:, 1, :])
            end(i)
            k = begin(J_YP)
            end(mm(bank[k][:, 0:B * M], w3T[:, 2, :], ctxT[:, :]))
            pe.wait_ge(*at("prep_ev", J_END))

            pe.wait_ge(*at("consts", NCONST))

            def turn(name):
                for g in range(G):
                    if g >= 2:
                        pe.wait_ge(*at(name + "_xte", g - 1))
                    pe.wait_ge(*at(name + "_ln", g + 1))
                    for j in range(J):
                        i = pe.transpose(b4(6 + g % 2)[:, j, :], xn[:, J * g + j, :], ident[:, :])
                    i.then_inc(sem(name + "_xt"), 1)

            def attention(name, keys, vals, q_first):
                src = queT if q_first else grpT

                def scores(g, j, first):
                    t = J * g + j
                    for q, (h0, h1) in enumerate(HEADS):
                        if not (first and j == 0):
                            pe.wait_ge(*at(name + "_sub", 3 * t - 2 + q))
                        mm(bank[q][:, 0:(h1 - h0) * M], src[:, j, :], keys[:, g, h0 * M:h1 * M]
                           ).then_inc(sem(name + "_sc"), 1)

                def values(g, j, first):
                    t = J * g + j
                    pe.wait_ge(*at(name + "_p", t + 1))
                    for q in range(3):
                        if not first:
                            pe.wait_ge(*at(name + "_pte", 4 * t - 3 + (q if q < 2 else 3)))
                        for k in range(4 * q, min(4 * q + 4, NK)):
                            i = pe.transpose(b4(3 + q)[0:CH[k], k % 4, :], prb[:, j, k * P:k * P + CH[k]], ident[:, :])
                        i.then_inc(sem(name + "_pt"), 1)
                    if not first:
                        pe.wait_ge(*at(name + "_x", t))
                    for k in range(NK):
                        if k in (0, 4, 8, 9):
                            pe.wait_ge(*at(name + "_pte", 4 * t + {0: 1, 4: 2, 8: 3, 9: 4}[k]))
                        i = mm(bank[6][:, 0:D], prT[0:CH[k], j % 2, k * P:(k + 1) * P],
                               vals[0:CH[k], g, k, :], k == 0, k == NK - 1)
                    i.then_inc(sem(name + "_out"), 1)

                def group(g, first):
                    if q_first:
                        pe.wait_ge(*at(name + "_qe", g))
                        mm(bank[7][:, :], w4T[:, 0, :], xnT[:, g, :]).then_inc(sem(name + "_q"), 1)
                        pe.wait_ge(*at(name + "_qe", g + 1))
                    else:
                        pe.wait_ge(*at(name + "_gt", g + 1))
                    for j in range(J):
                        scores(g, j, first)
                        if j >= 2:
                            values(g, j - 2, first and j == 2)
                        elif not first:
                            values(g - 1, j + 2, False)

                turn(name)
                pe.wait_ge(*at(name + "_xte", G))
                group(0, True)
                with pe.Fori(1, G) as g:
                    group(g, False)
                values(G - 1, J - 2, False)
                values(G - 1, J - 1, False)

            pe.wait_ge(*at("vw_in", 32 * B))
            attention("a0", keys0, vals0, False)

            pe.wait_ge(*at("a0_x", T))
            for g in range(G):
                pe.wait_ge(*at("f0_nrm", g + 1))
                if g >= 2:
                    pe.wait_ge(*at("f0_xte", g - 1))
                for j in range(J):
                    i = pe.transpose(bb(6 + g % 2)[:, j, :], nrm[:, J * g + j, :], identb[:, :])
                i.then_inc(sem("f0_xt"), 1)
            for g in range(G):
                pe.wait_ge(*at("f0_xte", g + 1))
                for j in range(J):
                    i = mm(bank[5][:, (J * g + j) * E:(J * g + j + 1) * E], nT[:, g, j * P:(j + 1) * P], gw0T[:, :])
            i.then_inc(sem("f0_lg"), 1)
            pe.wait_ge(*at("f0_lge", 1))

            def f0_down(g, e):
                n = E * g + e
                pe.wait_ge(*at("f0_act", n + 1))
                if e >= 2:
                    pe.wait_ge(*at("f0_acc", n - 1))
                else:
                    pe.wait_ge(*at("f0_acc", E * g))
                for j in range(J):
                    mm(b4(4 + e % 2)[:, j, :], onesb[0:1, :], m2row[0:1, e, :], True, False)
                    i = mm(b4(4 + e % 2)[:, j, :], hid[:, e % 2, j * P:(j + 1) * P], m2T[:, e, :], False, True)
                i.then_inc(sem("f0_dn"), 1)

            with pe.Fori(0, G) as g:
                for e in range(E):
                    n = E * g + e
                    if e >= 2:
                        pe.wait_ge(*at("f0_gb", n - 1))
                        pe.wait_ge(*at("f0_lb", n - 1))
                    else:
                        pe.wait_ge(*at("f0_gb", E * g))
                        pe.wait_ge(*at("f0_lb", E * g))
                    mm(bank[e % 2][:, :], m1T[:, 2 * e, :], nT[:, g, :])
                    mm(bank[2 + e % 2][:, :], m1T[:, 2 * e + 1, :], nT[:, g, :]).then_inc(sem("f0_up"), 1)
                    if e:
                        f0_down(g, e - 1)
                f0_down(g, E - 1)

            pe.wait_ge(*at("f0_x", G))
            attention("a1", keys1, vals1, True)

            pe.wait_ge(*at("a1_x", T))
            def rank(name):
                pe.wait_ge(*at(name + "_pre", 1))
                o = bank[4][:, 0:T * E]
                mm(o, lower[:, :], ohb[:, 0, :, :].rearrange("p t e -> p (t e)"), True, False)
                mm(o, onesb[:, :], ohb[:, 1, :, :].rearrange("p t e -> p (t e)"), False, True)
                mm(bank[3][:, 0:E], onesb[:, :], ohb[:, 0, T - 1, :], True, False)
                mm(bank[3][:, 0:E], onesb[:, :], ohb[:, 1, T - 1, :], False, True).then_inc(sem(name + "_rk"), 1)

            def turn_rows(name, srt, n):
                pe.wait_ge(*at(name + "_xs", 16))
                for g in range(0, n, 4):
                    if g >= 8:
                        pe.wait_ge(*at(name + "_bte", g // 4 - 1))
                    for k in range(g, min(g + 4, n)):
                        i = pe.transpose(b4(6 + g // 4 % 2)[:, k - g, :], srt[:, k, :], ident[:, :])
                    i.then_inc(sem(name + "_bt"), 1)

            def experts1():
                def up(i, a):
                    pe.wait_ge(*at("f1_w1", 2 * i + a + 1))
                    for q in range(2):
                        if later(i):
                            pe.wait_ge(*at("f1_h", 4 * i + 2 * a + q - 3))
                        for c in range(2):
                            r = mm(bank[2 * a + q][:, c * CAP:(c + 1) * CAP],
                                   wsel1[:, a, (2 * q + c) * P:(2 * q + c + 1) * P],
                                   srtT[:, 0:T * P].rearrange("p (u n) -> p u n", n=CAP)[:, 2 * i + a, :])
                        r.then_inc(sem("f1_up"), 1)

                def down(i, a, last=False):
                    pe.wait_ge(*at("f1_w2", 2 * i + a + 1))
                    pe.wait_ge(*at("f1_h", 4 * i + 2 * a + 2))
                    if later(i):
                        pe.wait_ge(*at("f1_y", 2 * i + a - 1))
                    for r in range(2):
                        for c in range(FC):
                            x = mm(b4(4 + a)[:, r, :], hid1[:, a, c, r * P:(r + 1) * P], wsel2[:, a, c, :],
                                   c == 0, c == FC - 1)
                    x.then_inc(sem("f1_dn"), 1)

                up(0, 0)
                up(0, 1)
                down(0, 0)
                with pe.Fori(1, E // 2) as i:
                    up(i, 0)
                    down(i - 1, 1)
                    up(i, 1)
                    down(i, 0)
                down(E // 2 - 1, 1)

            def experts2():
                def up(k, a):
                    pe.wait_ge(*at("f2_w1", 2 * k + a + 1))
                    if later(k):
                        pe.wait_ge(*at("f2_h", 2 * k + a - 1))
                    for c in range(FC):
                        r = mm(b4(a)[:, c, :], wsel1[:, a, c * P:(c + 1) * P],
                               srtT[:, :].rearrange("p (k n) -> p k n", n=P)[:, k, :])
                    r.then_inc(sem("f2_up"), 1)

                def down(k, a):
                    pe.wait_ge(*at("f2_w2", 2 * k + a + 1))
                    pe.wait_ge(*at("f2_h", 2 * k + a + 1))
                    if a == 0 and later(k):
                        pe.wait_ge(*at("f2_y", k))
                    for c in range(FC):
                        x = mm(bank[4][:, 0:D], hid2[:, a, c, :], wsel2[:, a, c, :], a == 0 and c == 0,
                               a == 1 and c == FC - 1)
                    x.then_inc(sem("f2_dn"), 1)

                up(0, 0)
                up(0, 1)
                down(0, 0)
                with pe.Fori(1, NBLK) as k:
                    up(k, 0)
                    down(k - 1, 1)
                    up(k, 1)
                    down(k, 0)
                down(NBLK - 1, 1)

            turn("f1")
            for t in range(T):
                if t % J == 0:
                    pe.wait_ge(*at("f1_xte", t // J + 1))
                i = mm(bank[5][:, t * E:(t + 1) * E], xnT[:, t // J, (t % J) * P:(t % J + 1) * P], wr1[:, :])
            i.then_inc(sem("f1_lg"), 1)
            rank("f1")
            turn_rows("f1", srt1, T)
            pe.wait_ge(*at("f1_bte", 4))
            experts1()

            pe.wait_ge(*at("f1_y", E))
            turn("a2")
            for g in range(G):
                pe.wait_ge(*at("a2_xte", g + 1))
                for j in range(J):
                    i = mm(b4(g)[:, j, :], xnT[:, g, j * P:(j + 1) * P], w3T[:, 0, :])
                i.then_inc(sem("a2_out"), 1)

            pe.wait_ge(*at("a2_x", G))
            rank("f2")
            turn_rows("f2", srt2, NBLK)
            pe.wait_ge(*at("f2_bte", 6))
            experts2()

            pe.wait_ge(*at("f2_y", NBLK))
            turn("a3")
            pe.wait_ge(*at("a3_xte", G))
            with pe.Fori(0, G) as g:
                pe.wait_ge(*at("a3_qe", g))
                mm(bank[6][:, :], w3T[:, 2, :], xnT[:, g, :]).then_inc(sem("a3_q"), 1)
                pe.wait_ge(*at("a3_qe", g + 1))
                pe.wait_ge(*at("a3_sub", g))
                for j in range(J):
                    i = mm(bank[0][:, j * M:(j + 1) * M], queT[:, j, :],
                           ypT[:, :].rearrange("p (b m) -> p b m", b=B)[:, g, :])
                i.then_inc(sem("a3_sc"), 1)
                pe.wait_ge(*at("a3_exp", g + 1))
                pe.wait_ge(*at("a3_pte", g))
                for j in range(J):
                    i = pe.transpose(b4(1)[0:M, j, :], prb[:, 0, j * M:(j + 1) * M], ident[:, :])
                i.then_inc(sem("a3_pt"), 1)
                pe.wait_ge(*at("a3_pte", g + 1))
                pe.wait_ge(*at("a3_x", J * g))
                for j in range(J):
                    i = mm(b4(2)[:, j, :], prT[0:M, 0, j * P:(j + 1) * P], ctxr[:, g, :])
                i.then_inc(sem("a3_out"), 1)

            pe.wait_ge(*at("a3_x", T))
            turn("f3")
            for t in range(T):
                if t % J == 0:
                    pe.wait_ge(*at("f3_xte", t // J + 1))
                i = mm(bank[5][:, t * E:(t + 1) * E], xnT[:, t // J, (t % J) * P:(t % J + 1) * P], gw3T[:, :])
            i.then_inc(sem("f3_lg"), 1)
            pe.wait_ge(*at("f3_lge", 1))
            pe.wait_ge(*at("ld_w_l3", 16 * 6))
            with pe.Fori(0, G) as g:
                pe.wait_ge(*at("f3_gt", g + 1))


                def up(u):
                    j, pr = u // 5, u % 5
                    ne = 2 if pr < 4 else 1
                    n = NU * g + u
                    pe.wait_ge(*at("f3_prod", n - 1 if u >= 2 else NU * g))
                    for a in range(ne):
                        i = pe.matmul(bank[u % 2][:, a * 256:(a + 1) * 256], grpT[:, j, :],
                                      w13_l3[:, 2 * pr + a, :], start=True, stop=True)
                    i.then_inc(sem("f3_up"), 1)

                def back(u):
                    j, pr = u // 5, u % 5
                    ne = 2 if pr < 4 else 1
                    n = NU * g + u
                    pe.wait_ge(*at("f3_prod", n + 1))
                    pe.wait_ge(*at("f3_hte", n - 1 if u >= 2 else NU * g))
                    for a in range(ne):
                        i = pe.transpose(b4(2 + u % 2)[:, a, :], hid[:, u % 2, a * P:(a + 1) * P], ident[:, :])
                    i.then_inc(sem("f3_ht"), 1)

                def down(u):
                    j, pr = u // 5, u % 5
                    ne = 2 if pr < 4 else 1
                    n = NU * g + u
                    pe.wait_ge(*at("f3_hte", n + 1))
                    if pr == 0:
                        pe.wait_ge(*at("f3_x", J * g + j - 1 if j >= 2 else J * g))
                    for a in range(ne):
                        i = mm(bank[4 + j % 2][:, 0:D], hid[:, 2 + u % 2, a * P:(a + 1) * P],
                               w2_l3[:, 2 * pr + a, :], pr == 0 and a == 0, pr == 4)
                    i.then_inc(sem("f3_dn"), 1)

                for u in range(NU + 2):
                    if u < NU:
                        up(u)
                    if 1 <= u <= NU:
                        back(u - 1)
                    if u >= 2:
                        down(u - 2)

        @block.scalar
        def _(act):
            job = [0]

            def ready(n):
                assert n == job[0], (n, job)
                job[0] += 1
                act.wait_ge(*at("prep_mm", n + 1))
                return n % 8

            def ev(o, i, scale=1.0, inc=True):
                x = act.activation(o, i, ACT.Copy, scale=scale)
                if inc:
                    x.then_inc(sem("prep_ev"), 1)

            k = ready(J_CTX)
            ev(ctxT[:, :], bank[k][:, 0:B * M])
            for a in range(2):
                k = ready(J_WQ + a)
                ev(wqT[:, 4 * a:4 * a + 4, :], b4(k))
            for c in range(8):
                k = ready(J_K + c)
                ev(kT[:, c, :], bank[k][:, 0:B * M])
            for h in range(H):
                k = ready(J_A + h)
                ev(keys0[:, :, h * M:(h + 1) * M], bank[k][:, 0:B * M].rearrange("p (b m) -> p b m", b=B), DH0 ** -0.5)
            for c in range(8):
                k = ready(J_V + c)
                ev(vT[:, c, :], bank[k][:, 0:B * M])
            for b in range(B):
                for q in range(4):
                    k = ready(J_VW + 4 * b + q)
                    r = HORD[4 * q]
                    ev(vstage[:, b, r:r + 7:2, :], b4(k)[0:M, :, :])
            k = ready(J_W4)
            ev(w4T[:, :, :], b4(k))
            act.wait_ge(*at("vw_out", 16 * B))
            act.wait_ge(*at("ld_cols", 64))
            k = ready(J_K1)
            act.activation(kvT1[:, 0, :], bank[k][:, 0:B * M], ACT.Identity, bias=cols[:, 1:2]
                           ).then_inc(sem("prep_ev"), 1)
            k = ready(J_V1)
            act.activation(kvT1[:, 1, :], bank[k][:, 0:B * M], ACT.Identity, bias=cols[:, 2:3]
                           ).then_inc(sem("prep_ev"), 1)
            for b in range(B):
                for q in range(3):
                    k = ready(J_VB + 3 * b + q)
                    if q < 2:
                        ev(vals1[:, b, 4 * q:4 * q + 4, :], b4(k))
                    else:
                        ev(vals1[:, b, 8, :], b4(k)[:, 0, :], inc=False)
                        ev(vals1[0:CH[9], b, 9, :], b4(k)[0:CH[9], 1, :])
            k = ready(J_W3)
            ev(w3T[:, :, :], b4(k)[:, 0:3, :])
            k = ready(J_SM)
            ev(gw3T[:, :], bank[k][:, 0:E], inc=False)
            ev(b1T[:, :], bank[k][:, E:E + E * FC])
            for a in range(2):
                k = ready(J_M1 + a)
                ev(m1T[:, 8 * a:8 * a + 8, :], bb(k))
            k = ready(J_M2)
            ev(m2T[:, :, :], bb(k))
            k = ready(J_SMB)
            ev(gw0T[:, :], bb(k)[:, 0, 0:E], inc=False)
            ev(m1bT[:, :, :].rearrange("p a e -> p (a e)"), bb(k)[:, 0, E:3 * E])
            k = ready(J_ROW)
            ev(rowc[:, :, :], b4(k), 1.0 / M)
            k = ready(J_YP)
            act.activation(ypT[:, :], bank[k][:, 0:B * M], ACT.Relu, bias=cols[:, 3:4]).then_inc(sem("prep_ev"), 1)
            act.wait_ge(*at("prep_ev", J_END))

            def turned(name):
                for g in range(G):
                    act.wait_ge(*at(name + "_xt", g + 1))
                    act.activation(xnT[:, g, :], bank[6 + g % 2][:, :], ACT.Copy).then_inc(sem(name + "_xte"), 1)

            def group_buffer(name, g, used, n):
                act.wait_ge(*at(used, n))
                act.activation(grpT[:, :, :].rearrange("p j n -> p (j n)"), xnT[:, g, :], ACT.Copy
                               ).then_inc(sem(name + "_gt"), 1)

            def attention(name, q_first):
                def exps(g, j):
                    t = J * g + j
                    act.wait_ge(*at(name + "_sub", 3 * t + 3))
                    act.activation(prb[:, j, :], prb[:, j, :], ACT.Exp).then_inc(sem(name + "_exp"), 1)

                def evac(g, j, first):
                    t = J * g + j
                    if not first:
                        act.wait_ge(*at(name + "_out", t - 1))
                    for q in range(3):
                        act.wait_ge(*at(name + "_pt", 3 * t + q + 1))
                        if q < 2:
                            act.activation(prT[:, j % 2, 4 * q * P:(4 * q + 4) * P], bank[3 + q][:, :], ACT.Copy
                                           ).then_inc(sem(name + "_pte"), 1)
                        else:
                            act.activation(prT[:, j % 2, 8 * P:9 * P], b4(5)[:, 0, :], ACT.Copy
                                           ).then_inc(sem(name + "_pte"), 1)
                            act.activation(prT[0:CH[9], j % 2, 9 * P:10 * P], b4(5)[0:CH[9], 1, :], ACT.Copy
                                           ).then_inc(sem(name + "_pte"), 1)

                def group(g, first):
                    if q_first:
                        act.wait_ge(*at(name + "_q", g + 1))
                        act.wait_ge(*at(name + "_sc", 3 * J * g))
                        act.activation(queT[:, :, :].rearrange("p j n -> p (j n)"), bank[7][:, :], ACT.Identity,
                                       bias=cols[:, 0:1]).then_inc(sem(name + "_qe"), 1)
                    else:
                        group_buffer(name, g, name + "_sc", 3 * J * g)
                    for j in range(J):
                        if j >= 2:
                            evac(g, j - 2, first)
                        elif not first:
                            evac(g - 1, j + 2, False)
                        exps(g, j)

                turned(name)
                act.wait_ge(*at(name + "_xte", G))
                group(0, True)
                with act.Fori(1, G) as g:
                    group(g, False)
                evac(G - 1, J - 2, False)
                evac(G - 1, J - 1, False)

            attention("a0", False)

            for g in range(G):
                act.wait_ge(*at("f0_xt", g + 1))
                act.activation(nT[:, g, :], bb(6 + g % 2)[:, 0:4, :].rearrange("p j n -> p (j n)"), ACT.Copy
                               ).then_inc(sem("f0_xte"), 1)
            act.wait_ge(*at("f0_gap", 1))
            act.activation(gs[:, 3, :], gs[:, 2, :], ACT.Exp).then_inc(sem("f0_gexp"), 1)
            with act.Fori(0, G) as g:
                for e in range(E):
                    n = E * g + e
                    act.wait_ge(*at("f0_gb", n + 1))
                    act.wait_ge(*at("f0_act", n - 1 if e >= 2 else E * g))
                    act.activation(hid[:, 2 + e % 2, :], mlpg[:, e % 2, :], ACT.Sigmoid, scale=ALPHA
                                   ).then_inc(sem("f0_sg"), 1)

            attention("a1", True)

            def gates_exp(name):
                act.wait_ge(*at(name + "_gap", 1))
                act.activation(lg[:, :, :], lg[:, :, :], ACT.Exp).then_inc(sem(name + "_gexp"), 1)

            def rows_turned(name, n):
                for g in range(0, n, 4):
                    m = min(4, n - g)
                    act.wait_ge(*at(name + "_bt", g // 4 + 1))
                    act.activation(srtT[:, g * P:(g + m) * P], bank[6 + g // 4 % 2][:, 0:m * P], ACT.Copy
                                   ).then_inc(sem(name + "_bte"), 1)

            turned("f1")
            gates_exp("f1")
            rows_turned("f1", T)

            def relu1(i, a):
                for q in range(2):
                    act.wait_ge(*at("f1_up", 4 * i + 2 * a + q + 1))
                    if later(i):
                        act.wait_ge(*at("f1_dn", 2 * i + a - 1))
                    act.activation(hid1[:, a, 2 * q:2 * q + 2, :].rearrange("p c n -> p (c n)"),
                                   bank[2 * a + q][:, :], ACT.Relu).then_inc(sem("f1_h"), 1)

            relu1(0, 0)
            relu1(0, 1)
            with act.Fori(1, E // 2) as i:
                relu1(i, 0)
                relu1(i, 1)
            turned("a2")
            rows_turned("f2", NBLK)

            def relu2(k, a):
                e = act.value_load(tabi[0:1, k, a:a + 1], min_val=0, max_val=E - 1)
                act.wait_ge(*at("f2_up", 2 * k + a + 1))
                if later(k):
                    act.wait_ge(*at("f2_dn", 2 * k + a - 1))
                for c in range(FC):
                    i = act.activation(hid2[:, a, c, :], b4(a)[:, c, :], ACT.Relu,
                                       bias=b1T[:, :].rearrange("p (e c) -> p e c", c=FC)[:, e, c:c + 1])
                i.then_inc(sem("f2_h"), 1)

            act.wait_ge(*at("tabi", 1))
            relu2(0, 0)
            relu2(0, 1)
            with act.Fori(1, NBLK) as k:
                relu2(k, 0)
                relu2(k, 1)
            turned("a3")
            with act.Fori(0, G) as g:
                act.wait_ge(*at("a3_q", g + 1))
                act.wait_ge(*at("a3_sc", g))
                act.activation(queT[:, :, :].rearrange("p j n -> p (j n)"), bank[6][:, :], ACT.Relu,
                               bias=cols[:, 3:4]).then_inc(sem("a3_qe"), 1)
                act.wait_ge(*at("a3_gap", g + 1))
                act.activation(prb[:, 0, 0:J * M], prb[:, 0, 0:J * M], ACT.Exp).then_inc(sem("a3_exp"), 1)
                act.wait_ge(*at("a3_pt", g + 1))
                act.wait_ge(*at("a3_out", g))
                act.activation(prT[0:M, 0, 0:J * P], bank[1][0:M, :], ACT.Copy).then_inc(sem("a3_pte"), 1)
            turned("f3")
            gates_exp("f3")
            act.wait_ge(*at("f3_c", 1))
            act.wait_ge(*at("f3_xte", G))
            with act.Fori(0, G) as g:
                group_buffer("f3", g, "f3_up", NU * g)

                def silu(u):
                    j, pr = u // 5, u % 5
                    ne = 2 if pr < 4 else 1
                    act.wait_ge(*at("f3_up", NU * g + u + 1))
                    act.wait_ge(*at("f3_prod", NU * g + u - 1 if u >= 2 else NU * g))
                    for a in range(ne):
                        i = act.activation(mlpg[:, u % 2, a * P:(a + 1) * P], bank[u % 2][:, a * 256:a * 256 + P],
                                           ACT.Silu, scale=C9[:, J * g + j, 2 * pr + a:2 * pr + a + 1])
                    i.then_inc(sem("f3_silu"), 1)

                def hte(u):
                    j, pr = u // 5, u % 5
                    ne = 2 if pr < 4 else 1
                    act.wait_ge(*at("f3_ht", NU * g + u + 1))
                    act.wait_ge(*at("f3_dn", NU * g + u - 1 if u >= 2 else NU * g))
                    act.activation(hid[:, 2 + u % 2, 0:ne * P], bank[2 + u % 2][:, 0:ne * P], ACT.Copy
                                   ).then_inc(sem("f3_hte"), 1)

                for u in range(NU + 1):
                    if u < NU:
                        silu(u)
                    if u:
                        hte(u - 1)

        @block.vector
        def _(dve):
            def bc3(ap, shape, ax):
                return ap.unsqueeze(ax).to_broadcast(shape)

            def one(ap, t):
                return ap.unsqueeze(2)[:, t, :]

            def copy_at(o, i):
                return dve.tensor_scalar(o, i, 1.0, None, ALU.mult)

            dve.wait_ge(*at("consts", NCONST))
            dve.wait_ge(*at("prep_ev", J_CTX + 1))
            dve.tensor_reduce(csum[:, :], ctxT[:, :].rearrange("p (b m) -> p b m", b=B), AXX, ALU.add
                              ).then_inc(sem("csum"), 1)
            dve.wait_ge(*at("csum", 1))
            dve.tensor_copy(csB, bc3(csum[:, :], [P, B, P], 2)).then_inc(sem("csum"), 1)
            dve.wait_ge(*at("prep_ev", J_V1 + 1))
            i = dve.tensor_scalar(kvT1[:, 0, :], kvT1[:, 0, :], DH1 ** -0.5, None, ALU.mult)
            i.then_inc(sem("k1s"), 1)
            dve.wait_ge(*at("k1s", 1))

            def by_head(o, src, b):
                return dve.tensor_tensor(o.rearrange("p (h m) -> p h m", h=H),
                                         bc3(src[:, b * M:(b + 1) * M], [P, H, M], 1),
                                         bc3(blk[:, :], [P, H, M], 2), ALU.mult)

            for b in range(B):
                if b >= 2:
                    dve.wait_ge(*at("prep_mm", J_VB + 3 * (b - 1)))
                by_head(vblk[:, b % 2, :], kvT1[:, 1, :], b).then_inc(sem("vblk"), 1)
            for b in range(B):
                by_head(keys1[:, b, :], kvT1[:, 0, :], b).then_inc(sem("keys1"), 1)
            dve.wait_ge(*at("ld_bo", 48))
            dve.wait_ge(*at("prep_ev", J_END))
            dve.wait_ge(*at("keys1", B))
            dve.tensor_tensor(rowc[:, :, :], rowc[:, :, :], bc3(boB[:, 2, :], [P, B, D], 1), ALU.add
                              ).then_inc(sem("rowc"), 1)
            dve.tensor_scalar(maskf[:, :, :], maskf[:, :, :], MASKED, None, ALU.mult).then_inc(sem("rowc"), 1)
            dve.wait_ge(*at("rowc", 2))

            def norm(name, wait_x):
                with dve.Fori(0, G) as g:
                    wait_x(g)
                    for j in range(J):
                        i = dve.bn_stats(st[:, J * g + j, :], X[:, J * g + j, :])
                    i.then_inc(sem(name + "_st"), 1)
                dve.wait_ge(*at(name + "_st", G))
                dve.tensor_tensor(nv[:, 0, :], st[:, :, 1], st[:, :, 4], ALU.add)
                dve.tensor_tensor(nv[:, 1, :], st[:, :, 1], st[:, :, 4], ALU.subtract)
                dve.tensor_tensor(nv[:, 2, :], st[:, :, 2], st[:, :, 5], ALU.add).then_inc(sem(name + "_nv"), 1)
                dve.wait_ge(*at(name + "_nv", 1))
                dve.tensor_scalar(mean[:, :], nv[:, 0, :], 0.5, None, ALU.mult)
                dve.tensor_tensor(nv[:, 3, :], nv[:, 1, :], nv[:, 1, :], ALU.mult)
                dve.tensor_scalar(nv[:, 4, :], nv[:, 2, :], 1.0 / D, LN_EPS, ALU.mult, ALU.add
                                  ).then_inc(sem(name + "_nv"), 1)
                dve.wait_ge(*at(name + "_nv", 2))
                dve.scalar_tensor_tensor(ve[:, :], nv[:, 3, :], 0.25, nv[:, 4, :], ALU.mult, ALU.add
                                         ).then_inc(sem(name + "_ve"), 1)
                dve.wait_ge(*at(name + "_rstd", 1))
                if name == "a3":
                    dve.wait_ge(*at("f2_put", 16 * T))
                elif name == "f2":
                    dve.wait_ge(*at("a2_xt", G))
                elif name != "a0":
                    dve.wait_ge(*at(name + "_xt", 0))
                with dve.Fori(0, G) as g:
                    for j in range(J):
                        t = J * g + j
                        i = dve.tensor_scalar(xn[:, t, :], X[:, t, :], one(mean[:, :], t), one(rstd[:, :], t),
                                              ALU.subtract, ALU.mult)
                    i.then_inc(sem(name + "_ln"), 1)

            def attention(name, wait_x):
                def soft(g, j, first):
                    t = J * g + j
                    for q, (h0, h1) in enumerate(HEADS):
                        dve.wait_ge(*at(name + "_sc", 3 * t + q + 1))
                        dve.tensor_reduce(mx[:, j % 2, h0:h1],
                                          bank[q][:, 0:(h1 - h0) * M].rearrange("p (h m) -> p h m", m=M),
                                          AXX, ALU.max).then_inc(sem(name + "_mx"), 1)
                    if not first:
                        dve.wait_ge(*at(name + "_pt", 3 * (t - 3)))
                    for q, (h0, h1) in enumerate(HEADS):
                        dve.wait_ge(*at(name + "_mx", 3 * t + q + 1))
                        dve.tensor_tensor(prb[:, j, h0 * M:h1 * M].rearrange("p (h m) -> p h m", m=M),
                                          bank[q][:, 0:(h1 - h0) * M].rearrange("p (h m) -> p h m", m=M),
                                          bc3(mx[:, j % 2, h0:h1], [P, h1 - h0, M], 2),
                                          ALU.subtract).then_inc(sem(name + "_sub"), 1)

                def add(g, j):
                    t = J * g + j
                    dve.wait_ge(*at(name + "_out", t + 1))
                    if j == 0:
                        dve.wait_ge(*at(name + "_xb", g + 1))
                    dve.tensor_tensor(X[:, t, :], bank[6][:, 0:D], X[:, t, :], ALU.add).then_inc(sem(name + "_x"), 1)

                def sums(g, j, first):
                    t = J * g + j
                    dve.wait_ge(*at(name + "_exp", t + 1))
                    dve.tensor_reduce(sm[:, j % 2, :], prb[:, j, :].rearrange("p (h m) -> p h m", h=H),
                                      AXX, ALU.add).then_inc(sem(name + "_sm"), 1)
                    dve.wait_ge(*at(name + "_sm", t + 1))
                    if not (first and j < 2):
                        dve.wait_ge(*at(name + "_p", t - 1))
                    dve.reciprocal(rs[:, j % 2, :], sm[:, j % 2, :]).then_inc(sem(name + "_rs"), 1)

                def group(g, first):
                    for j in range(J):
                        soft(g, j, first)
                        if j == 3:
                            add(g, 0)
                        elif not first:
                            add(g - 1, j + 1)
                        if j:
                            sums(g, j - 1, first)
                        elif not first:
                            sums(g - 1, J - 1, False)

                norm(name, wait_x)
                group(0, True)
                with dve.Fori(1, G) as g:
                    group(g, False)
                sums(G - 1, J - 1, False)
                for j in range(1, J):
                    add(G - 1, j)

            dve.wait_ge(*at("ld_x", 16))
            attention("a0", lambda g: None)

            def grp(tile, g):
                return tile.rearrange("p (g j) d -> p g (j d)", g=G)[:, g, :].rearrange("p (j d) -> p j d", j=J)

            dve.wait_ge(*at("ld_later", 80))

            def top(c, src, dst, m):
                c(dve.tensor_reduce(gs[:, m, :], src, AXX, ALU.max))
                c(dve.tensor_tensor(tA[:, :, :], src, bc3(gs[:, m, :], [P, T, E], 2), ALU.is_equal))
                c(dve.tensor_tensor(tA[:, :, :], tA[:, :, :], bc3(iota[:, :], [P, T, E], 1), ALU.mult))
                c(dve.tensor_reduce(gs[:, 11, :], tA[:, :, :], AXX, ALU.min))
                c(dve.tensor_tensor(dst, bc3(iota[:, :], [P, T, E], 1), bc3(gs[:, 11, :], [P, T, E], 2), ALU.is_equal))

            def top_two(c, src, m):
                top(c, src, oh[:, 0, :, :], m)
                c(dve.scalar_tensor_tensor(lg2[:, :, :], oh[:, 0, :, :], MASKED, src, ALU.mult, ALU.add))
                top(c, lg2[:, :, :], oh[:, 1, :, :], m + 1)

            norm("f0", lambda g: dve.wait_ge(*at("a0_x", T)))
            c = Steps(dve, sem("f0_c"))
            dve.wait_ge(*at("f0_ln", G))
            c(dve.tensor_copy(xc[:, :, :], xn[:, :, :]))
            for t in range(T):
                i = dve.tensor_tensor_reduce(nrm[:, t, :], xc[:, t, :], xc[:, t, :], 1.0, 0.0,
                                             ALU.mult, ALU.add, gs[:, 4, t:t + 1])
            c(i)
            dve.tensor_scalar(gs[:, 0, :], gs[:, 4, :], 1.0 / D, LN_EPS, ALU.mult, ALU.add).then_inc(sem("f0_ms"), 1)
            dve.wait_ge(*at("f0_rms", 1))
            with dve.Fori(0, G) as g:
                for j in range(J):
                    t = J * g + j
                    i = dve.scalar_tensor_tensor(nrm[:, t, :], xc[:, t, :], one(gs[:, 1, :], t), nwB[:, :],
                                                 ALU.mult, ALU.mult)
                i.then_inc(sem("f0_nrm"), 1)
            dve.wait_ge(*at("f0_lg", 1))
            c(dve.tensor_tensor(lgb[:, :, :], bank[5][:, 0:T * E].rearrange("p (t e) -> p t e", t=T),
                                bc3(gbB[:, :], [P, T, E], 1), ALU.add))
            dve.tensor_copy(lg[:, :, :], lgb[:, :, :]).then_inc(sem("f0_lge"), 1)
            dve.wait_ge(*at("f0_lge", 1))
            top_two(c, lg[:, :, :], 5)
            dve.tensor_tensor(gs[:, 2, :], gs[:, 6, :], gs[:, 5, :], ALU.subtract).then_inc(sem("f0_gap"), 1)
            dve.wait_ge(*at("f0_gexp", 1))
            c(dve.tensor_scalar(gs[:, 7, :], gs[:, 3, :], 1.0, None, ALU.add))
            c(dve.reciprocal(gs[:, 8, :], gs[:, 7, :]))
            c(dve.tensor_tensor(gs[:, 9, :], gs[:, 8, :], gs[:, 3, :], ALU.mult))
            for a in range(2):
                i = dve.tensor_tensor(oh[:, a, :, :], oh[:, a, :, :], bc3(gs[:, 8 + a, :], [P, T, E], 2), ALU.mult)
            c(i)
            c(dve.tensor_tensor(C[:, :, :], oh[:, 0, :, :], oh[:, 1, :, :], ALU.add))
            dve.memset(acc, 0.0).then_inc(sem("acc0"), 1)
            dve.wait_ge(*at("acc0", 1))

            def accumulate(name, g, e, n, dst, upto):
                dve.wait_ge(*at(name + "_dn", upto))
                dve.wait_ge(*at(name + "_acc", n))
                for j in range(J):
                    i = dve.scalar_tensor_tensor(dst[:, J * g + j, :], b4(4 + e % 2)[:, j, :], C[:, J * g + j, e:e + 1],
                                                 dst[:, J * g + j, :], ALU.mult, ALU.add)
                i.then_inc(sem(name + "_acc"), 1)

            with dve.Fori(0, G) as g:
                for e in range(E):
                    n = E * g + e
                    s = e % 2
                    dve.wait_ge(*at("f0_up", n + 1))
                    dve.wait_ge(*at("f0_sg", n - 1 if e >= 2 else E * g))
                    dve.wait_ge(*at("f0_gl", n))
                    dve.tensor_scalar(mlpg[:, s, :], bank[s][:, :], m1bT[:, 0, e:e + 1], LIMIT, ALU.add, ALU.min
                                      ).then_inc(sem("f0_gb"), 1)
                    dve.tensor_scalar(mlpl[:, s, :], bank[2 + s][:, :], m1bT[:, 1, e:e + 1], -LIMIT, ALU.add, ALU.max
                                      ).then_inc(sem("f0_lb"), 1)
                    dve.wait_ge(*at("f0_lb", n + 1))
                    dve.tensor_scalar(mlpl[:, s, :], mlpl[:, s, :], LIMIT, 1.0, ALU.min, ALU.add
                                      ).then_inc(sem("f0_l1"), 1)
                    dve.wait_ge(*at("f0_l1", n + 1))
                    dve.wait_ge(*at("f0_dn", n - 1 if e >= 2 else E * g))
                    dve.tensor_tensor(hid[:, s, :], mlpl[:, s, :], mlpg[:, s, :], ALU.mult).then_inc(sem("f0_gl"), 1)
                    if e:
                        accumulate("f0", g, e - 1, n - 1, acc, n)
                accumulate("f0", g, E - 1, E * g + E - 1, acc, E * g + E)
                dve.wait_ge(*at("f0_acc", E * (g + 1)))
                c = Steps(dve, sem("f0_fin"), 2 * g)
                c(copy_at(accb[:, :, :], grp(acc, g)))
                c(dve.tensor_tensor(accb[:, :, :], accb[:, :, :], grp(xc[:, :, :], g), ALU.add))
                dve.tensor_tensor(grp(X[:, :, :], g), accb[:, :, :], grp(X[:, :, :], g), ALU.add
                                  ).then_inc(sem("f0_x"), 1)

            attention("a1", lambda g: dve.wait_ge(*at("f0_x", g + 1)))

            def gates(name, c):
                dve.wait_ge(*at(name + "_lg", 1))
                dve.tensor_copy(lg[:, :, :], bank[5][:, 0:T * E].rearrange("p (t e) -> p t e", t=T)
                                ).then_inc(sem(name + "_lge"), 1)
                dve.wait_ge(*at(name + "_lge", 1))
                c(dve.tensor_reduce(gs[:, 0, :], lg[:, :, :], AXX, ALU.max))
                dve.tensor_tensor(lg[:, :, :], lg[:, :, :], bc3(gs[:, 0, :], [P, T, E], 2), ALU.subtract
                                  ).then_inc(sem(name + "_gap"), 1)
                dve.wait_ge(*at(name + "_gexp", 1))
                c(dve.tensor_reduce(gs[:, 0, :], lg[:, :, :], AXX, ALU.add))
                c(dve.reciprocal(gs[:, 1, :], gs[:, 0, :]))
                c(dve.tensor_tensor(lg[:, :, :], lg[:, :, :], bc3(gs[:, 1, :], [P, T, E], 2), ALU.mult))

            def ranks(name, c):
                c(dve.tensor_copy(pre[:, 0, E:, :], oh[:, 0, :, :]))
                for n, shift in enumerate((1, 2, 4, 8)):
                    a, b = n % 2, (n + 1) % 2
                    c(dve.tensor_tensor(pre[:, b, E:, :], pre[:, a, E:, :], pre[:, a, E - shift:E + T - shift, :],
                                        ALU.add))
                dve.tensor_copy(ohb[:, 0, :, :], oh[:, 0, :, :])
                dve.tensor_tensor(ohb[:, 1, :, :], pre[:, 0, E:, :], oh[:, 0, :, :], ALU.subtract
                                  ).then_inc(sem(name + "_pre"), 1)
                dve.wait_ge(*at(name + "_rk", 1))
                dve.tensor_copy(tot[:, :], bank[3][:, 0:E])
                c(dve.tensor_copy(tA[:, :, :], bank[4][:, 0:T * E].rearrange("p (t e) -> p t e", t=T)))

            def chosen(c, m):
                c(dve.tensor_tensor(tA[:, :, :], tA[:, :, :], oh[:, 0, :, :], ALU.mult))
                c(dve.tensor_reduce(gs[:, m, :], tA[:, :, :], AXX, ALU.add))

            def summed(name, weight):
                dve.wait_ge(*at(name + "_got", 16 * T))
                with dve.Fori(0, G) as g:
                    for j in range(J):
                        t = J * g + j
                        i = dve.scalar_tensor_tensor(X[:, t, :], back[:, t, :], weight(t), X[:, t, :],
                                                     ALU.mult, ALU.add)
                    i.then_inc(sem(name + "_add"), 1)

            norm("f1", lambda g: dve.wait_ge(*at("a1_x", T)))
            c = Steps(dve, sem("f1_c"))
            gates("f1", c)
            top(c, lg[:, :, :], oh[:, 0, :, :], 2)
            ranks("f1", c)
            chosen(c, 3)
            c(dve.tensor_scalar(gs[:, 4, :], gs[:, 3, :], float(CAP), None, ALU.is_lt))
            c(dve.tensor_scalar(gs[:, 5, :], gs[:, 11, :], float(E), float(CAP), ALU.add, ALU.mult))
            c(dve.tensor_tensor(gs[:, 6, :], gs[:, 5, :], gs[:, 3, :], ALU.add))
            c(dve.tensor_tensor(gs[:, 9, :], gs[:, 4, :], gs[:, 2, :], ALU.mult))
            c(dve.tensor_scalar(idx[:, 1, :], gs[:, 6, :], T * P - 1.0, None, ALU.min))
            c(dve.tensor_tensor(gs[:, 6, :], gs[:, 6, :], tok[:, :], ALU.subtract))
            c(dve.tensor_tensor(gs[:, 6, :], gs[:, 6, :], gs[:, 4, :], ALU.mult))
            dve.tensor_tensor(idx[:, 0, :], gs[:, 6, :], tok[:, :], ALU.add).then_inc(sem("f1_idx"), 1)

            dve.wait_ge(*at("ld_w1_l1", 16))
            dve.wait_ge(*at("ld_w2_l1", 16))

            def weights1(i, a):
                if later(i):
                    dve.wait_ge(*at("f1_up", 4 * i + 2 * a - 2))
                copy_at(wsel1[:, a, :], w1_l1[:, 2 * i + a, :]).then_inc(sem("f1_w1"), 1)
                if later(i):
                    dve.wait_ge(*at("f1_dn", 2 * i + a - 1))
                copy_at(wsel2[:, a, :, :], w2_l1[:, 2 * i + a, :, :]).then_inc(sem("f1_w2"), 1)

            def result1(i, a):
                dve.wait_ge(*at("f1_dn", 2 * i + a + 1))
                copy_at(res1.rearrange("p (u r) d -> p u r d", r=2)[:, 2 * i + a, :, :], b4(4 + a)[:, 0:2, :]
                        ).then_inc(sem("f1_y"), 1)

            weights1(0, 0)
            weights1(0, 1)
            with dve.Fori(1, E // 2) as i:
                weights1(i, 0)
                result1(i - 1, 0)
                weights1(i, 1)
                result1(i - 1, 1)
            result1(E // 2 - 1, 0)
            result1(E // 2 - 1, 1)
            summed("f1", lambda t: one(gs[:, 9, :], t))
            norm("a2", lambda g: dve.wait_ge(*at("f1_add", g + 1)))
            for g in range(G):
                dve.wait_ge(*at("a2_out", g + 1))
                dve.wait_ge(*at("a2_xb", g + 1))
                dve.tensor_tensor(grp(X[:, :, :], g), b4(g), grp(X[:, :, :], g), ALU.add).then_inc(sem("a2_x"), 1)
            norm("f2", lambda g: dve.wait_ge(*at("a2_x", g + 1)))
            dve.wait_ge(*at("f2_ln", G))
            c = Steps(dve, sem("f2_c"))
            c(dve.tensor_tensor(gs[:, 0, :], xn[:, :, 0], xn[:, :, 1], ALU.add))
            c(dve.tensor_scalar(gs[:, 1, :], gs[:, 0, :], -1.0, None, ALU.mult))
            c(dve.tensor_tensor(gs[:, 1, :], gs[:, 0, :], gs[:, 1, :], ALU.max))
            c(dve.tensor_copy(gi[:, :], gs[:, 1, :]))
            c(dve.tensor_copy(gs[:, 2, :], gi[:, :]))
            c(dve.tensor_tensor(gs[:, 3, :], gs[:, 2, :], gs[:, 1, :], ALU.is_gt))
            c(dve.tensor_tensor(gs[:, 2, :], gs[:, 2, :], gs[:, 3, :], ALU.subtract))
            c(dve.tensor_scalar(gs[:, 3, :], gs[:, 0, :], 0.0, 2.0, ALU.is_ge, ALU.mult))
            c(dve.tensor_scalar(gs[:, 3, :], gs[:, 3, :], -1.0, None, ALU.add))
            c(dve.tensor_tensor(gs[:, 2, :], gs[:, 2, :], gs[:, 3, :], ALU.mult))
            c(dve.tensor_scalar(gs[:, 2, :], gs[:, 2, :], 3.0 * E, None, ALU.add))
            for k in (4, 2, 1):
                c(dve.tensor_scalar(gs[:, 3, :], gs[:, 2, :], float(k * E), -float(k * E), ALU.is_ge, ALU.mult))
                c(dve.tensor_tensor(gs[:, 2, :], gs[:, 2, :], gs[:, 3, :], ALU.add))
            c(dve.tensor_scalar(gs[:, 2, :], gs[:, 2, :], -float(E), None, ALU.add))
            c(dve.tensor_tensor(oh[:, 0, :, :], bc3(iota[:, :], [P, T, E], 1), bc3(gs[:, 2, :], [P, T, E], 2),
                                ALU.is_equal))
            ranks("f2", c)
            c(dve.tensor_tensor(cmp[:, :, 0:T], bc3(tot[:, :], [P, E, T], 2), bc3(thr[:, :], [P, E, T], 1), ALU.is_gt))
            c(dve.tensor_reduce(nblk[:, 0, :], cmp[:, :, 0:T], AXX, ALU.add))
            c(dve.tensor_tensor(cmp[:, :, 0:E], lowE[:, :, :], bc3(nblk[:, 0, :], [P, E, E], 1), ALU.mult))
            c(dve.tensor_reduce(nblk[:, 1, :], cmp[:, :, 0:E], AXX, ALU.add))
            c(dve.tensor_tensor(nblk[:, 2, :], nblk[:, 1, :], nblk[:, 0, :], ALU.add))
            c(dve.tensor_scalar(nblk[:, 1, :], nblk[:, 1, :], float(P), None, ALU.mult))
            c(dve.tensor_tensor(tA[:, :, :], tA[:, :, :], bc3(nblk[:, 1, :], [P, T, E], 1), ALU.add))
            chosen(c, 4)
            dve.tensor_copy(idx[:, 1, :], gs[:, 4, :])
            dve.tensor_copy(idx[:, 0, :], gs[:, 4, :]).then_inc(sem("f2_idx"), 1)
            c(dve.tensor_tensor(blkc[:, :, :], bc3(kio[:, 0:NBLK], [P, NBLK, E], 2),
                                bc3(nblk[:, 2, :], [P, NBLK, E], 1), ALU.is_ge))
            c(dve.tensor_reduce(tab[:, 0, :], blkc[:, :, :], AXX, ALU.add))
            c(dve.tensor_scalar(tab[:, 0, :], tab[:, 0, :], E - 1.0, None, ALU.min))
            c(dve.tensor_scalar(tab[:, 1, :], tab[:, 0, :], E - 1.0, -float(E), ALU.is_equal, ALU.mult))
            c(dve.scalar_tensor_tensor(tab[:, 1, :], tab[:, 0, :], 1.0, tab[:, 1, :], ALU.add, ALU.add))
            dve.tensor_copy(tabi[:, :, 0], tab[:, 0, :])
            dve.tensor_copy(tabi[:, :, 1], tab[:, 1, :]).then_inc(sem("tabi"), 1)
            dve.wait_ge(*at("tabi", 1))

            dve.wait_ge(*at("ld_w1_l2", 16))
            dve.wait_ge(*at("ld_w2_l2", 16))
            dve.wait_ge(*at("b2p", E + 1))

            def weights2(k, a):
                e = dve.value_load(tabi[0:1, k, a:a + 1], min_val=0, max_val=E - 1)
                if later(k):
                    dve.wait_ge(*at("f2_up", 2 * k + a - 1))
                copy_at(wsel1[:, a, :], w1_l2[:, e, :]).then_inc(sem("f2_w1"), 1)
                if later(k):
                    dve.wait_ge(*at("f2_dn", 2 * k + a - 1))
                copy_at(wsel2[:, a, :, :], w2_l2[:, e, :, :]).then_inc(sem("f2_w2"), 1)

            def result2(k):
                e = dve.value_load(tabi[0:1, k, 0:1], min_val=0, max_val=E - 1)
                dve.wait_ge(*at("f2_dn", 2 * k + 2))
                dve.tensor_tensor(res2[:, k, :], bank[4][:, 0:D], b2pair[:, e, :], ALU.add).then_inc(sem("f2_y"), 1)

            weights2(0, 0)
            weights2(0, 1)
            with dve.Fori(1, NBLK) as k:
                weights2(k, 0)
                result2(k - 1)
                weights2(k, 1)
            result2(NBLK - 1)
            summed("f2", lambda t: 0.5)

            norm("a3", lambda g: dve.wait_ge(*at("f2_add", g + 1)))
            with dve.Fori(0, G) as g:
                dve.wait_ge(*at("a3_sc", g + 1))
                dve.wait_ge(*at("a3_pt", g))
                p3 = prb[:, 0, 0:J * M].rearrange("p (j m) -> p j m", j=J)
                c = Steps(dve, sem("a3_c"), 3 * g)
                dve.tensor_tensor(p3, bank[0][:, 0:J * M].rearrange("p (j m) -> p j m", j=J),
                                  bc3(maskf[:, g, :], [P, J, M], 1), ALU.add).then_inc(sem("a3_sub"), 1)
                dve.wait_ge(*at("a3_sub", g + 1))
                c(dve.tensor_reduce(gs[:, 0, 0:J], p3, AXX, ALU.max))
                dve.tensor_tensor(p3, p3, bc3(gs[:, 0, 0:J], [P, J, M], 2), ALU.subtract).then_inc(sem("a3_gap"), 1)
                dve.wait_ge(*at("a3_exp", g + 1))
                c(dve.tensor_reduce(gs[:, 1, 0:J], p3, AXX, ALU.add))
                c(dve.reciprocal(gs[:, 2, 0:J], gs[:, 1, 0:J]))
                dve.wait_ge(*at("a3_out", g + 1))
                for j in range(J):
                    dve.scalar_tensor_tensor(X[:, J * g + j, :], b4(2)[:, j, :], gs[:, 2, j:j + 1],
                                             X[:, J * g + j, :], ALU.mult, ALU.add).then_inc(sem("a3_x"), 1)

            norm("f3", lambda g: dve.wait_ge(*at("a3_x", T)))
            c = Steps(dve, sem("f3_ch"))
            gates("f3", c)
            top_two(c, lg[:, :, :], 2)
            c(dve.tensor_tensor(oh[:, 0, :, :], oh[:, 0, :, :], oh[:, 1, :, :], ALU.add))
            dve.memset(C9[:, :, E:E + 1], 1.0)
            dve.tensor_tensor(C9[:, :, 0:E], oh[:, 0, :, :], lg[:, :, :], ALU.mult).then_inc(sem("f3_c"), 1)
            dve.wait_ge(*at("f3_c", 1))
            with dve.Fori(0, G) as g:
                for u in range(NU + 3):
                    if u < NU:
                        j, pr = u // 5, u % 5
                        ne = 2 if pr < 4 else 1
                        dve.wait_ge(*at("f3_silu", NU * g + u + 1))
                        dve.wait_ge(*at("f3_ht", NU * g + u - 1 if u >= 2 else NU * g))
                        for a in range(ne):
                            i = dve.scalar_tensor_tensor(hid[:, u % 2, a * P:(a + 1) * P],
                                                         bank[u % 2][:, a * 256 + P:(a + 1) * 256],
                                                         C9[:, J * g + j, 2 * pr + a:2 * pr + a + 1],
                                                         mlpg[:, u % 2, a * P:(a + 1) * P], ALU.mult, ALU.mult)
                        i.then_inc(sem("f3_prod"), 1)
                    if u >= 7 and (u - 7) % 5 == 0:
                        j = (u - 7) // 5
                        dve.wait_ge(*at("f3_dn", NU * g + 5 * (j + 1)))
                        t = J * g + j
                        dve.tensor_tensor(X[:, t, :], bank[4 + j % 2][:, 0:D], X[:, t, :], ALU.add
                                          ).then_inc(sem("f3_x"), 1)


_INS = ['x', 'ctx_1024', 'mask_BxS2_bk0', 'L0_xattn_Wq', 'L0_xattn_Wk', 'L0_xattn_Wv', 'L0_xattn_Wo', 'L0_xattn_bo',
        'L0_ffn_norm_weight', 'L0_ffn_gate_weight', 'L0_ffn_gate_bias', 'L0_ffn_mlp1_weight', 'L0_ffn_mlp1_bias',
        'L0_ffn_mlp2_weight', 'L0_ffn_mlp2_bias', 'L1_xattn_wq_w', 'L1_xattn_wq_b', 'L1_xattn_wk_w', 'L1_xattn_wk_b',
        'L1_xattn_wv_w', 'L1_xattn_wv_b', 'L1_xattn_dense_w', 'L1_xattn_dense_b', 'L1_ffn_Wr', 'L1_ffn_W1',
        'L1_ffn_W2', 'L2_xattn_W', 'L2_xattn_b', 'L2_ffn_W1', 'L2_ffn_b1', 'L2_ffn_W2', 'L2_ffn_b2', 'L3_xattn_W',
        'L3_xattn_b', 'L3_ffn_gate_w', 'L3_ffn_w1', 'L3_ffn_w2', 'L3_ffn_w3', 'L3_ffn_w1s', 'L3_ffn_w2s', 'L3_ffn_w3s']


def kernel(**inputs):
    import concourse.bacc as _bacc
    from concourse.bass_utils import run_bass_kernel_spmd as _run

    nc = _bacc.Bacc("TRN2", target_bir_lowering=False, num_devices=1)
    arrays, args = {}, {}
    for name in _INS:
        a = np.ascontiguousarray(inputs[name])
        if a.dtype == np.bool_:
            a = a.reshape(-1).view(np.int32)
        arrays["in_" + name] = a
        args[name] = nc.dram_tensor("in_" + name, a.shape, mybir.dt.from_np(a.dtype), kind="ExternalInput").ap()
    out = nc.dram_tensor("out_0", (B, SEQ, D), F32, kind="ExternalOutput").ap()
    build(nc, args, out)
    r = _run(nc, [arrays], core_ids=[0])
    return r.results[0]["out_0"]
```

```python
import numpy as np
import concourse.bass as bass
from concourse import mybir
from contextlib import ExitStack

F32 = mybir.dt.float32
BF16 = mybir.dt.bfloat16
U8 = mybir.dt.uint8
I32 = mybir.dt.int32
ALU = mybir.AluOpType
ACT = mybir.ActivationFunctionType
AXX = mybir.AxisListType.X

P = 128
B, SEQ, D = 4, 512, 128
G, J = B, SEQ // P
T = G * J
M = 77
H = 16
DH0, DH1 = 64, D // H
HM = H * M
NK = -(-HM // P)
CH = [min(P, HM - P * k) for k in range(NK)]
HEADS = [(0, 5), (5, 10), (10, 16)]
E = 8
F = 512
FC = F // P
CAP = T * P // E
LN_EPS = 1e-5
LIMIT, ALPHA = 7.0, 1.702
MASKED = -1e30
NZERO = T // 4 + 6
NCONST = 25
NBLK = (T * P + E * (P - 1)) // P
NU = G + E * G
C3 = 3 * E

STAGES = ["a0", "f0", "a1", "f1", "a2", "f2", "a3", "f3"]
HEADED = ["a0", "a1"]
SIGNALS = {k: [(s, G) for s in STAGES] for k in ("st", "ln")}
SIGNALS |= {k: [(s, G) for s in STAGES if s != "f2"] for k in ("xt", "xte")}
SIGNALS |= {"ve": [(s, 1) for s in STAGES], "rstd": [(s, G) for s in STAGES]}
SIGNALS |= {"nv": [(s, 2) for s in STAGES]}
SIGNALS |= {k: [(s, 3 * T) for s in HEADED] + [("a3", G)] for k in ("sc", "sub", "pt")}
SIGNALS |= {"out": [(s, T) for s in HEADED] + [("a2", G), ("a3", G)]}
SIGNALS |= {k: [(s, T) for s in HEADED] for k in ("sm", "rs")}
SIGNALS |= {"p": [(s, T - 1) for s in HEADED], "last": [(s, 1) for s in HEADED]}
SIGNALS |= {"mx": [(s, 3 * T) for s in HEADED], "exp": [("a0", T), ("a1", T), ("a3", G)],
            "pte": [("a0", 4 * T), ("a1", 4 * T), ("a3", G)], "xb": [("a0", G), ("a1", G), ("a2", G)],
            "x": [("a0", T), ("f0", G), ("a1", T), ("a2", G), ("a3", T), ("f3", 2 * G)],
            "q": [("a1", G), ("a3", G)], "qe": [("a1", G), ("a3", G)],
            "lg": [("f0", 1), ("f1", 1), ("f3", 1)], "lge": [("f0", 1), ("f1", 1), ("f3", 1)],
            "gap": [("f0", 1), ("f1", 1), ("a3", G), ("f3", 1)], "gexp": [("f0", 1), ("f1", 1), ("f3", 1)],
            "cs": [("f0", 1), ("f3", 1)], "ct": [("f0", 2), ("f3", 2)], "cte": [("f0", 2), ("f3", 2)],
            "dn": [("f0", E * G), ("f1", E), ("f2", 2 * NBLK), ("f3", NU)],
            "up": [("f0", E * G), ("f1", 2 * E), ("f2", 2 * NBLK), ("f3", NU)],
            "h": [("f1", 2 * E), ("f2", 2 * NBLK)]}
SIGNALS |= {k: [("f1", E), ("f2", 2 * NBLK)] for k in ("w1", "w2")}
SIGNALS |= {"y": [("f1", E), ("f2", 2 * NBLK)]}
SIGNALS |= {"yst": [("f1", 16 * E), ("f2", 16 * NBLK)], "put": [("f1", 16 * T), ("f2", 16 * T)]}
SIGNALS |= {f"got{g}": [("f1", 16 * J), ("f2", 16 * J)] for g in range(G)}
SIGNALS |= {"idx": [("f1", 1), ("f2", 1)], "rk": [("f1", 1), ("f2", 1)], "pre": [("f1", 1), ("f2", 1)],
            "bt": [("f1", 4), ("f2", 6)], "bte": [("f1", 4), ("f2", 6)],
            "add": [("f1", G), ("f2", G)]}
SIGNALS |= {f"xs{k}": [("f1", 16), ("f2", 16)] if k < T // 4 else [("f2", 16)] for k in range(-(-NBLK // 4))}


FROM_ONE = ["h", "out"]


HORD = [0, 2, 4, 6, 1, 3, 5, 7, 8, 10, 12, 14, 9, 11, 13, 15]


def later(n):
    return not isinstance(n, int) or n > 0


class Steps:

    def __init__(self, eng, sem, base=0):
        self.eng, self.sem, self.base, self.n = eng, sem, base, 0

    def __call__(self, ins):
        self.n += 1
        ins.then_inc(self.sem, 1)
        self.eng.wait_ge(self.sem, self.base + self.n)


def build(nc, A, out):
    ctx = ExitStack()
    with ctx:
        def sb(name, shape, dt=F32):
            return ctx.enter_context(nc.sbuf_tensor(name, shape, dt))

        sems = {}

        def sem(name):
            stage, _, signal = name.partition("_")
            if stage in STAGES and signal in SIGNALS:
                name = signal
            if name not in sems:
                sems[name] = ctx.enter_context(nc.semaphore(name))
            return sems[name]

        def at(name, n):
            stage, _, signal = name.partition("_")
            base = 1 if name in FROM_ONE or (stage in STAGES and signal in FROM_ONE) else 0
            for s, count in SIGNALS.get(signal, ()) if stage in STAGES else ():
                if s == stage:
                    return sem(name), n + base
                base += count
            assert stage not in STAGES or signal not in SIGNALS, name
            return sem(name), n + base

        def wait_for(eng, name, n):
            if not isinstance(n, int) or n > 0:
                eng.wait_ge(*at(name, n))

        X = sb("X", [P, T, D])
        xn = sb("xn", [P, T, D])
        xnT = sb("xnT", [P, G, SEQ])
        grpque = sb("grpque", [P, 2, J, P])
        grpT = grpque[:, 0, :, :]
        queT = grpque[:, 1, :, :]
        xc = grpque[:, :, :, :].rearrange("p a j n -> p (a j n)").bitcast(BF16).rearrange("p (t d) -> p t d", t=T)
        nrm = xnT[:, 0:2, :].rearrange("p a n -> p (a n)").bitcast(BF16).rearrange("p (t d) -> p t d", t=T)
        nT = xnT[:, 2:4, :].rearrange("p a n -> p (a n)").bitcast(BF16).rearrange("p (g n) -> p g n", g=G)
        ident = sb("ident", [P, P])
        identb = sb("identb", [P, P], BF16)
        ctxr = sb("ctxr", [M, B, D])
        ctxT = sb("ctxT", [P, B * M])
        prb = sb("prb", [P, 4, HM])
        prT = sb("prT", [P, 2, NK * P])
        R1 = sb("R1", [P, B * HM + B * NK * P])
        R2 = sb("R2", [P, B * HM + B * NK * P])
        R3 = sb("R3", [P, 2 * E * F])
        keys0 = R1[:, 0:B * HM].rearrange("p (b n) -> p b n", b=B)
        vals0 = R1[:, B * HM:].rearrange("p (b k n) -> p b k n", b=B, k=NK)
        keys1 = R2[:, 0:B * HM].rearrange("p (b n) -> p b n", b=B)
        vals1 = R2[:, B * HM:].rearrange("p (b k n) -> p b k n", b=B, k=NK)
        w1_l1 = R3[:, 0:E * F].rearrange("p (e n) -> p e n", e=E)
        w2_l1 = R3[:, E * F:].rearrange("p (e c n) -> p e c n", e=E, c=FC)
        w1_l2 = R1[:, 0:E * F].rearrange("p (e n) -> p e n", e=E)
        w2_l2 = R1[:, B * HM:B * HM + E * F].rearrange("p (e c n) -> p e c n", e=E, c=FC)
        w13_l3 = R2[:, 0:9 * 256].rearrange("p (e n) -> p e n", e=9)
        w2_l3 = R2[:, 9 * 256:9 * 384].rearrange("p (e n) -> p e n", e=9)
        wq = R3[:, 0:1024]
        wk = R3[:, 1024:2048]
        wv = R3[:, 2048:3072]
        wo = R3[:, 3072:4096].rearrange("p (c n) -> p c n", c=8)
        wqT = R3[:, 4096:5120].rearrange("p (c n) -> p c n", c=8)
        w4r = R3[:, 7584:8096].rearrange("p (a n) -> p a n", a=4)
        kT = R3[:, 5120:5120 + 8 * B * M].rearrange("p (c n) -> p c n", c=8)
        vT = prT[:, :, :].rearrange("p a n -> p (a n)")[:, 0:8 * B * M].rearrange("p (c n) -> p c n", c=8)
        vstage = R2[0:M, 0:B * H * D].rearrange("p (b h n) -> p b h n", b=B, h=H)
        prbf = prb[:, :, :].rearrange("p a n -> p (a n)")
        kvT1 = prbf[:, 0:2 * B * M].rearrange("p (a n) -> p a n", a=2)
        vblk = prbf[:, 640:640 + 2 * HM].rearrange("p (a n) -> p a n", a=2)
        w3r = prbf[:, 3712:4096].rearrange("p (a n) -> p a n", a=3)
        zero = R1[:, B * HM:B * HM + F]
        csB = prbf[:, 3200:3200 + B * P].rearrange("p (b n) -> p b n", b=B)
        CT = prbf[0:C3, 0:T * P // 2].bitcast(BF16)
        Csp = prbf[:, 1024:1024 + T * C3 // 2].bitcast(BF16).rearrange("p (t c) -> p t c", t=T)
        hid = prbf[:, 2048:2048 + 4 * SEQ].rearrange("p (a n) -> p a n", a=4)
        sig = xn[:, :, :].rearrange("p t d -> p (t d)").rearrange("p (a n) -> p a n", a=4)
        mlpg = prT[:, 0, 0:2 * SEQ].rearrange("p (a n) -> p a n", a=2)
        mlpl = prT[:, 1, 0:2 * SEQ].rearrange("p (a n) -> p a n", a=2)
        srt1 = R2[:, 3456:3456 + T * D].rearrange("p (k n) -> p k n", k=T)
        res1 = R2[:, 5504:5504 + T * D].rearrange("p (k n) -> p k n", k=T)
        srt2 = R3[:, 0:NBLK * D].rearrange("p (k n) -> p k n", k=NBLK)
        res2 = R3[:, NBLK * D:2 * NBLK * D].rearrange("p (k n) -> p k n", k=NBLK)
        srtT = prbf[:, 0:NBLK * P]
        hid1 = prbf[:, 2048:2048 + 2 * FC * 256].rearrange("p (a c n) -> p a c n", a=2, c=FC)
        hid2 = prbf[:, NBLK * P:NBLK * P + 2 * FC * P].rearrange("p (a c n) -> p a c n", a=2, c=FC)
        back = prbf[:, 0:T * D].rearrange("p (t n) -> p t n", t=T)
        p3 = prbf[:, 2048:2048 + G * J * M].rearrange("p (g j m) -> p g j m", g=G, j=J)
        que2 = grpque[:, :, :, :].rearrange("p a j n -> p a (j n)")

        w4T = sb("w4T", [P, 4, D])
        w3T = sb("w3T", [P, 3, D])
        gw3r = sb("gw3r", [E, D])
        gw3T = sb("gw3T", [P, E])
        wr1 = sb("wr1", [P, E])
        gw0r = sb("gw0r", [E, D], BF16)
        gw0T = sb("gw0T", [P, E], BF16)
        m1r = R1[:, B * HM + F:B * HM + F + 1024].bitcast(BF16).rearrange("p (e n) -> p e n", e=E)
        m1T = sb("m1T", [P, E * 2, P], BF16)
        m2r = R1[:, B * HM + F + 1024:B * HM + F + 1536].bitcast(BF16).rearrange("p (e n) -> p e n", e=E)
        m2T = sb("m2T", [P, E, P])
        wsel1 = m1T[:, :, :].rearrange("p a n -> p (a n)").bitcast(F32).rearrange("p (a n) -> p a n", a=2)
        wsel2 = m2T[:, :, :].rearrange("p (a c) n -> p a c n", a=2)
        b2pair = R2[:, 7552:7552 + E * D].rearrange("p (e n) -> p e n", e=E)
        m1br = sb("m1br", [E, 2 * P], BF16)
        m1bT = sb("m1bT", [P, 2, E])
        b1r = sb("b1r", [E * FC, P])
        b1T = sb("b1T", [P, E * FC])
        nwB = sb("nwB", [P, D])
        gbB = sb("gbB", [P, E], BF16)
        boB = sb("boB", [P, 3, D])
        cols = sb("cols", [P, 4])
        rowc = sb("rowc", [P, B, D])
        ypT = sb("ypT", [P, B * M])
        maskw = sb("maskw", [P, M], I32)
        maskf = sb("maskf", [P, B, M])
        blk = sb("blk", [P, H])
        lower = sb("lower", [P, P], BF16)
        onesb = sb("onesb", [P, P], BF16)
        iota = sb("iota", [P, E])
        nhalf = sb("nhalf", [P, T])
        pad = sb("pad", [P, 1])
        ones1 = sb("ones1", [P, 1])
        st = sb("st", [P, T, 6])
        nv = sb("nv", [P, 5, T])
        mean = sb("mean", [P, T])
        ve = sb("ve", [P, T])
        rstd = sb("rstd", [P, T])
        mx = sb("mx", [P, 2, H])
        sm = sb("sm", [P, 2, H])
        rs = sb("rs", [P, 2, H])
        csum = sb("csum", [P, B])
        C = sb("C", [P, T, E])
        Cr = sb("Cr", [P, T, E])
        lg = sb("lg", [P, T, E])
        lg2 = sb("lg2", [P, T, E])
        lgb = sb("lgb", [P, T, E], BF16)
        tA = sb("tA", [P, T, E])
        gs = sb("gs", [P, 12, T])
        gi = sb("gi", [P, T], I32)
        oh = sb("oh", [P, 2, T, E])
        ohb = sb("ohb", [P, 2, T, E], BF16)
        pre = sb("pre", [P, 2, E + T, E])
        blkc = sb("blkc", [P, NBLK, E])
        tot = sb("tot", [P, E])
        nblk = sb("nblk", [P, 3, E])
        cmp = sb("cmp", [P, E, T])
        thr = sb("thr", [P, T])
        kio = sb("kio", [P, 32])
        lowE = sb("lowE", [P, E, E])
        tab = sb("tab", [P, 2, NBLK])
        tabi = sb("tabi", [P, NBLK, 2], I32)
        idx = sb("idx", [P, 2, T], I32)
        tok = sb("tok", [P, T])
        accb = sb("accb", [P, J, D], BF16)
        m2row = sb("m2row", [C3, D], BF16)
        sel = sb("sel", [C3, E, P], BF16)
        b2first = sb("b2first", [P, D])
        i32 = sb("i32", [P, 32], I32)
        rows1 = nc.dram_tensor("rows1", [2 * T * P, D], F32, kind="Internal").ap()
        outs1 = nc.dram_tensor("outs1", [T * P, D], F32, kind="Internal").ap()
        rows2 = nc.dram_tensor("rows2", [NBLK * P, D], F32, kind="Internal").ap()
        outs2 = nc.dram_tensor("outs2", [NBLK * P, D], F32, kind="Internal").ap()
        vwd = nc.dram_tensor("vwd", [B, HM, D], F32, kind="Internal").ap()

        bank = [ctx.enter_context(nc.psum_tensor(f"bank{i}", [P, 512], F32)) for i in range(8)]

        def b4(i):
            return bank[i][:, :].rearrange("p (j n) -> p j n", j=4)

        def bb(i):
            return bank[i][:, :].bitcast(BF16).rearrange("p (j n) -> p j n", j=8)

        block = ctx.enter_context(nc.Block())

        J_CTX, J_WQ, J_K, J_A, J_W4, J_V = 0, 1, 3, 11, 27, 28
        J_K1, J_V1 = J_V + 8, J_V + 9
        J_VW = J_V1 + 1
        J_VB = J_VW + 16
        J_W3 = J_VB + 3 * B
        J_SM = J_W3 + 1
        J_M1 = J_SM + 1
        J_M2 = J_M1 + 2
        J_SMB = J_M2 + 1
        J_ROW = J_SMB + 1
        J_YP = J_ROW + 1
        J_END = J_YP + 1

        @block.sync
        def _(sp):
            sp.dma_start(ctxr[:, :, :], A["ctx_1024"].rearrange("b m d -> m b d")).then_inc(sem("ld_ctx"), 16)
            sp.dma_start(wq, A["L0_xattn_Wq"]).then_inc(sem("ld_wq"), 16)
            sp.dma_start(wk, A["L0_xattn_Wk"]).then_inc(sem("ld_wk"), 16)
            sp.dma_start(X[:, :, :], A["x"].rearrange("b (j p) d -> p (b j) d", p=P)).then_inc(sem("ld_x"), 16)
            sp.dma_start(wv, A["L0_xattn_Wv"]).then_inc(sem("ld_wv"), 16)
            sp.dma_start(wo, A["L0_xattn_Wo"].rearrange("(c p) n -> p c n", p=P)).then_inc(sem("ld_wo"), 16)
            sp.dma_start(m1r, A["L0_ffn_mlp1_weight"].rearrange("e (i two) h -> i e (two h)", two=2)
                         ).then_inc(sem("ld_m"), 16)
            sp.dma_start(m2r, A["L0_ffn_mlp2_weight"].rearrange("e h i -> h e i")).then_inc(sem("ld_m"), 16)
            for n, w in enumerate(["wq_w", "wk_w", "wv_w", "dense_w"]):
                sp.dma_start(w4r[:, n, :], A["L1_xattn_" + w]).then_inc(sem("ld_w4"), 16)
            for n, w in enumerate(["L1_xattn_wq_b", "L1_xattn_wk_b", "L1_xattn_wv_b", "L3_xattn_b"]):
                sp.dma_start(cols[:, n:n + 1], A[w].rearrange("(p a) -> p a", a=1)).then_inc(sem("ld_cols"), 16)
            for n, w in enumerate(["L0_xattn_bo", "L1_xattn_dense_b", "L2_xattn_b"]):
                sp.dma_start(boB[:, n, :], A[w].rearrange("(a n) -> a n", a=1).partition_broadcast(P)
                             ).then_inc(sem("ld_bo"), 16)
            sp.dma_start(w3r[:, 0:2, :], A["L2_xattn_W"].rearrange("p (a n) -> p a n", a=2)).then_inc(sem("ld_w3"), 16)
            sp.dma_start(w3r[:, 2, :], A["L3_xattn_W"]).then_inc(sem("ld_w3"), 16)
            sp.dma_start(gw3r[:, :], A["L3_ffn_gate_w"]).then_inc(sem("ld_small"), 16)
            sp.dma_start(b1r[:, :], A["L2_ffn_b1"].rearrange("e (c p) -> (e c) p", p=P)).then_inc(sem("ld_small"), 16)
            sp.dma_start(gw0r[:, :], A["L0_ffn_gate_weight"]).then_inc(sem("ld_small"), 16)
            sp.dma_start(m1br[:, :], A["L0_ffn_mlp1_bias"]).then_inc(sem("ld_small"), 16)
            for a in range(3):
                sp.dma_start(m2row[a * E:(a + 1) * E, :], A["L0_ffn_mlp2_bias"]).then_inc(sem("ld_later"), 16)
            sp.dma_start(wr1[:, :], A["L1_ffn_Wr"]).then_inc(sem("ld_later"), 16)
            sp.dma_start(nwB[:, :], A["L0_ffn_norm_weight"].rearrange("(a n) -> a n", a=1).partition_broadcast(P)
                         ).then_inc(sem("ld_later"), 16)
            sp.dma_start(gbB[:, :], A["L0_ffn_gate_bias"].rearrange("(a n) -> a n", a=1).partition_broadcast(P)
                         ).then_inc(sem("ld_later"), 16)
            sp.dma_start(maskw[:, :], A["mask_BxS2_bk0"].rearrange("(a n) -> a n", a=1).partition_broadcast(P)
                         ).then_inc(sem("ld_later"), 16)
            sp.wait_ge(*at("consts", 2))
            z = zero[:, :].rearrange("p (k d) -> p k d", d=D)
            for rows, n in ((rows1, T), (rows2, NBLK)):
                for k in range(0, n, 4):
                    m = min(4, n - k)
                    sp.dma_start(rows[k * P:(k + m) * P, :].rearrange("(k p) d -> p k d", p=P), z[:, 0:m, :]
                                 ).then_inc(sem("zeroed"), 16)
            for b in range(B):
                sp.wait_ge(*at("prep_ev", J_VW + 4 * (b + 1)))
                sp.dma_start(vwd[b, :, :].rearrange("(h m) n -> m h n", h=H), vstage[:, b, :, :]
                             ).then_inc(sem("vw_out"), 16)
            sp.wait_ge(*at("vw_out", 16 * B))
            sp.wait_ge(*at("zeroed", 16 * NZERO))
            sp.wait_ge(*at("prep_mm", J_M2 + 1))
            for b in range(B):
                sp.dma_start(vals0[:, b, 0:NK - 1, :], vwd[b, 0:(NK - 1) * P, :].rearrange("(k p) n -> p k n", p=P)
                             ).then_inc(sem("vw_in"), 16)
                sp.dma_start(vals0[0:CH[-1], b, NK - 1, :], vwd[b, (NK - 1) * P:HM, :]).then_inc(sem("vw_in"), 16)
            sp.wait_ge(*at("prep_mm", J_VW + 16))
            sp.dma_start(w1_l1, A["L1_ffn_W1"].rearrange("e d f -> d e f")).then_inc(sem("ld_w1_l1"), 16)
            sp.dma_start(w2_l1, A["L1_ffn_W2"].rearrange("e (c p) n -> p e c n", p=P)).then_inc(sem("ld_w2_l1"), 16)
            sp.wait_ge(*at("a0_out", T))
            sp.dma_start(w1_l2, A["L2_ffn_W1"].rearrange("e d f -> d e f")).then_inc(sem("ld_w1_l2"), 16)
            sp.dma_start(w2_l2, A["L2_ffn_W2"].rearrange("e (c p) n -> p e c n", p=P)).then_inc(sem("ld_w2_l2"), 16)
            sp.wait_ge(*at("a1_out", T))
            sp.dma_start(b2pair, A["L2_ffn_b2"].rearrange("(a e) d -> a e d", a=1).partition_broadcast(P)
                         ).then_inc(sem("ld_b2"), 16)
            for n, (w1, w3, w2) in enumerate([("w1", "w3", "w2"), ("w1s", "w3s", "w2s")]):
                e0, ne = (0, E) if n == 0 else (E, 1)
                sp.dma_start(w13_l3[:, e0:e0 + ne, 0:P], A["L3_ffn_" + w1].rearrange("e d n -> d e n")
                             ).then_inc(sem("ld_w_l3"), 16)
                sp.dma_start(w13_l3[:, e0:e0 + ne, P:2 * P], A["L3_ffn_" + w3].rearrange("e d n -> d e n")
                             ).then_inc(sem("ld_w_l3"), 16)
                sp.dma_start(w2_l3[:, e0:e0 + ne, :], A["L3_ffn_" + w2].rearrange("e d n -> d e n")
                             ).then_inc(sem("ld_w_l3"), 16)
            def sorted_rows(name, n_it, rows, srt, res, outs, per):
                sp.wait_ge(*at(name + "_put", 16 * T))
                n = n_it * per
                for k in range(0, n, 4):
                    m = min(k + 4, n)
                    sp.dma_start(srt[:, k:m, :], rows[k * P:m * P, :].rearrange("(k p) d -> p k d", p=P)
                                 ).then_inc(sem(f"{name}_xs{k // 4}"), 16)
                y = 1 if name == "f1" else 2
                with sp.Fori(0, n_it) as k:
                    sp.wait_ge(*at(name + "_y", y * k + y))
                    sp.dma_start(outs.rearrange("(k r p) d -> p k r d", p=P, r=per)[:, k, :, :],
                                 res.rearrange("p (k r) d -> p k r d", r=per)[:, k, :, :]
                                 ).then_inc(sem(name + "_yst"), 16)

            sorted_rows("f1", E, rows1, srt1, res1, outs1, 2)
            sorted_rows("f2", NBLK, rows2, srt2, res2, outs2, 1)
            with sp.Fori(0, G) as g:
                sp.wait_ge(*at("f3_x", G + g + 1))
                sp.dma_start(out.rearrange("b (j p) d -> p b j d", p=P)[:, g, :, :], X[:, :, :].rearrange(
                    "p (b j) d -> p b j d", b=B)[:, g, :, :]).then_inc(sem("stored"), 16)
            sp.wait_ge(*at("stored", 16 * G))

        @block.gpsimd
        def _(pool):
            for name in FROM_ONE:
                pool.sem_inc(sem(name), 1)
            c = Steps(pool, sem("consts"))
            c(pool.memset(ident[:, :], 0.0))
            c(pool.memset(zero[:, :], 0.0))
            c(pool.affine_select(out=ident[:, :], in_=ident[:, :], compare_op=ALU.not_equal, fill=1.0,
                                 base=0, pattern=[[-1, P]], channel_multiplier=1))
            c(pool.tensor_copy(identb[:, :], ident[:, :]))
            c(pool.memset(nhalf[:, :], -0.5))
            c(pool.memset(ones1[:, :], 1.0))
            c(pool.memset(blk[:, :], 1.0))
            c(pool.affine_select(out=blk[:, :], in_=blk[:, :], compare_op=ALU.is_ge, fill=0.0,
                                 base=0, pattern=[[-DH1, H]], channel_multiplier=1))
            c(pool.affine_select(out=blk[:, :], in_=blk[:, :], compare_op=ALU.is_ge, fill=0.0,
                                 base=DH1 - 1, pattern=[[DH1, H]], channel_multiplier=-1))
            c(pool.memset(onesb[:, :], 1.0))
            c(pool.affine_select(out=lower[:, :], in_=onesb[:, :], compare_op=ALU.is_gt, fill=0.0,
                                 base=0, pattern=[[1, P]], channel_multiplier=-1))
            c(pool.iota(i32[:, :], pattern=[[1, 32]], base=0, channel_multiplier=0))
            c(pool.tensor_copy(kio[:, :], i32[:, :]))
            c(pool.tensor_scalar(iota[:, :], kio[:, 0:E], float(E), None, ALU.subtract))
            c(pool.tensor_scalar(thr[:, :], kio[:, 0:T], float(P), None, ALU.mult))
            c(pool.iota(i32[:, 0:T], pattern=[[P, T]], base=T * P, channel_multiplier=1))
            c(pool.tensor_copy(tok[:, :], i32[:, 0:T]))
            c(pool.memset(lowE[:, :, :], 1.0))
            c(pool.affine_select(out=lowE[:, :, :], in_=lowE[:, :, :], compare_op=ALU.is_gt, fill=0.0,
                                 base=0, pattern=[[1, E], [-1, E]], channel_multiplier=0))
            c(pool.memset(sel[:, :, :], 0.0))
            for a in range(3):
                c(pool.affine_select(out=sel[:, :, :], in_=sel[:, :, :], compare_op=ALU.not_equal, fill=1.0,
                                     base=-E * a, pattern=[[-1, E], [0, P]], channel_multiplier=1))
            c(pool.memset(pre[:, :, :, :], 0.0))

            def pow_rstd(name):
                pool.wait_ge(*at(name + "_ve", 1))
                for g in range(G):
                    pool.tensor_tensor(rstd[:, J * g:J * (g + 1)], ve[:, J * g:J * (g + 1)],
                                       nhalf[:, J * g:J * (g + 1)], ALU.pow).then_inc(sem(name + "_rstd"), 1)

            def attention(name, bias):
                def scale(g, j):
                    t = J * g + j
                    pool.wait_ge(*at(name + "_rs", t + 1))
                    pool.tensor_tensor(prb[:, j, :].rearrange("p (h m) -> p h m", h=H),
                                       prb[:, j, :].rearrange("p (h m) -> p h m", h=H),
                                       rs[:, j % 2, :].unsqueeze(2).to_broadcast([P, H, M]),
                                       ALU.mult).then_inc(sem(name + "_p"), 1)

                def group(g, first):
                    pool.wait_ge(*at(name + "_ln", G))
                    pool.tensor_tensor(X4(g), X4(g), boB[:, bias, :].unsqueeze(1).to_broadcast([P, J, D]),
                                       ALU.add).then_inc(sem(name + "_xb"), 1)
                    for j in range(J):
                        if not (first and j == 0):
                            scale(*((g, j - 1) if j else (g - 1, J - 1)))

                group(0, True)
                with pool.Fori(1, G) as g:
                    group(g, False)

            def X4(g):
                return X[:, :, :].rearrange("p (g j) d -> p g (j d)", g=G)[:, g, :].rearrange(
                    "p (j d) -> p j d", j=J)

            pow_rstd("a0")
            pool.wait_ge(*at("ld_later", 112))
            c(pool.tensor_copy(maskf[:, :, :].rearrange("p b m -> p (b m)"), maskw[:, :].bitcast(U8)))
            assert c.n == NCONST
            pool.wait_ge(*at("ld_bo", 48))
            attention("a0", 0)
            pow_rstd("f0")
            for g in range(G):
                pool.wait_ge(*at("f0_ms", g + 1))
                pool.tensor_tensor(gs[:, 1, J * g:J * (g + 1)], gs[:, 0, J * g:J * (g + 1)],
                                   nhalf[:, J * g:J * (g + 1)], ALU.pow).then_inc(sem("f0_rms"), 1)
            with pool.Fori(0, G) as g:
                for e in range(E):
                    n = E * g + e
                    pool.wait_ge(*at("f0_sg", n + 1))
                    pool.wait_ge(*at("f0_wl", n + 1))
                    pool.tensor_tensor(hid[:, e % 4, :], hid[:, e % 4, :], sig[:, e % 4, :],
                                       ALU.mult).then_inc(sem("f0_act"), 1)
            pow_rstd("a1")
            attention("a1", 1)

            def dispatch(name, rows):
                pool.wait_ge(*at(name + "_idx", 1))
                pool.wait_ge(*at("zeroed", 16 * NZERO))
                for t in range(T):
                    pool.indirect_dma_start(out=rows, out_offset=bass.IndirectOffsetOnAxis(ap=idx[:, 0, t:t + 1], axis=0),
                                            in_=xn[:, t, :], in_offset=None).then_inc(sem(name + "_put"), 16)

            def collect(name, n, outs):
                pool.wait_ge(*at(name + "_yst", 16 * n))
                for t in range(T):
                    pool.indirect_dma_start(out=back[:, t, :], out_offset=None, in_=outs,
                                            in_offset=bass.IndirectOffsetOnAxis(ap=idx[:, 1, t:t + 1], axis=0)
                                            ).then_inc(sem(f"{name}_got{t // J}"), 16)

            pow_rstd("f1")
            dispatch("f1", rows1)
            pool.wait_ge(*at("ld_b2", 16))
            pool.tensor_copy(b2first[:, :], b2pair[:, 0, :]).then_inc(sem("b2p"), 1)
            pool.wait_ge(*at("b2p", 1))
            for e in range(E):
                pool.tensor_tensor(b2pair[:, e, :], b2pair[:, e, :], b2pair[:, e + 1, :] if e + 1 < E else b2first[:, :],
                                   ALU.add).then_inc(sem("b2p"), 1)
                pool.wait_ge(*at("b2p", e + 2))

            collect("f1", E, outs1)
            pow_rstd("a2")
            for g in range(G):
                pool.wait_ge(*at("a2_ln", g + 1))
                pool.tensor_tensor(X4(g), X4(g), rowc[:, g, :].unsqueeze(1).to_broadcast([P, J, D]),
                                   ALU.add).then_inc(sem("a2_xb"), 1)
            pow_rstd("f2")
            dispatch("f2", rows2)

            one_bc = ones1[:, :].to_broadcast([P, F])

            def first2(k, a):
                e = pool.value_load(tabi[0:1, k, a:a + 1], min_val=0, max_val=E - 1)
                if later(k):
                    pool.wait_ge(*at("f2_up", 2 * k + a - 1))
                pool.tensor_tensor(wsel1[:, a, :], w1_l2[:, e, :], one_bc, ALU.mult).then_inc(sem("f2_w1"), 1)

            pool.wait_ge(*at("tabi", 1))
            pool.wait_ge(*at("ld_w1_l2", 16))
            first2(0, 0)
            first2(0, 1)
            with pool.Fori(1, NBLK) as k:
                first2(k, 0)
                first2(k, 1)
            collect("f2", NBLK, outs2)
            pow_rstd("a3")
            pow_rstd("f3")

        @block.tensor
        def _(pe):
            job = [0]

            def begin(n):
                assert n == job[0]
                if n >= 8:
                    pe.wait_ge(*at("prep_ev", n - 7))
                return n % 8

            def end(ins):
                ins.then_inc(sem("prep_mm"), 1)
                job[0] += 1

            def mm(o, l, r, start=True, stop=True):
                return pe.matmul(o, l, r, start=start, stop=stop)

            pe.wait_ge(*at("consts", 4))
            pe.wait_ge(*at("ld_ctx", 16))
            k = begin(J_CTX)
            for b in range(B):
                i = pe.transpose(bank[k][:, b * M:(b + 1) * M], ctxr[:, b, :], ident[0:M, 0:M])
            end(i)
            pe.wait_ge(*at("ld_wq", 16))
            for a in range(2):
                k = begin(J_WQ + a)
                for c in range(4):
                    i = pe.transpose(b4(k)[:, c, :], wq[:, (4 * a + c) * P:(4 * a + c + 1) * P], ident[:, :])
                end(i)
            pe.wait_ge(*at("ld_wk", 16))
            pe.wait_ge(*at("prep_ev", J_CTX + 1))
            for c in range(8):
                k = begin(J_K + c)
                end(mm(bank[k][:, 0:B * M], wk[:, c * P:(c + 1) * P], ctxT[:, :]))
            for h in range(H):
                k = begin(J_A + h)
                o = DH0 * (h % 2)
                pe.wait_ge(*at("prep_ev", J_K + h // 2 + 1))
                end(mm(bank[k][:, 0:B * M], wqT[o:o + DH0, h // 2, :], kT[o:o + DH0, h // 2, :]))
            pe.wait_ge(*at("ld_w4", 64))
            k = begin(J_W4)
            for a in range(4):
                i = pe.transpose(b4(k)[:, a, :], w4r[:, a, :], ident[:, :])
            end(i)
            pe.wait_ge(*at("ld_wv", 16))
            for c in range(8):
                k = begin(J_V + c)
                end(mm(bank[k][:, 0:B * M], wv[:, c * P:(c + 1) * P], ctxT[:, :]))
            for a, jn in ((1, J_K1), (2, J_V1)):
                k = begin(jn)
                if a == 1:
                    pe.wait_ge(*at("prep_ev", J_W4 + 1))
                end(mm(bank[k][:, 0:B * M], w4T[:, a, :], ctxT[:, :]))
            pe.wait_ge(*at("ld_wo", 16))
            pe.wait_ge(*at("prep_ev", J_V + 8))
            for b in range(B):
                for q in range(4):
                    k = begin(J_VW + 4 * b + q)
                    for a, h in enumerate(HORD[4 * q:4 * q + 4]):
                        o = DH0 * (h % 2)
                        i = mm(b4(k)[0:M, a, :], vT[o:o + DH0, h // 2, b * M:(b + 1) * M], wo[o:o + DH0, h // 2, :])
                    end(i)
            for b in range(B):
                pe.wait_ge(*at("vblk", b + 1))
                for q in range(3):
                    k = begin(J_VB + 3 * b + q)
                    for kk in range(4 * q, min(4 * q + 4, NK)):
                        i = mm(b4(k)[0:CH[kk], kk % 4, :], vblk[:, b % 2, kk * P:kk * P + CH[kk]], w4T[:, 3, :])
                    end(i)
            pe.wait_ge(*at("ld_w3", 32))
            k = begin(J_W3)
            for a in range(3):
                i = pe.transpose(b4(k)[:, a, :], w3r[:, a, :], ident[:, :])
            end(i)
            pe.wait_ge(*at("ld_small", 64))
            k = begin(J_SM)
            pe.transpose(bank[k][:, 0:E], gw3r[:, :], ident[0:E, 0:E])
            end(pe.transpose(bank[k][:, E:E + E * FC], b1r[:, :], ident[0:E * FC, 0:E * FC]))
            pe.wait_ge(*at("ld_m", 32))
            for a in range(2):
                k = begin(J_M1 + a)
                for c in range(8):
                    n = 8 * a + c
                    i = pe.transpose(bb(k)[:, c, :], m1r[:, n // 2, (n % 2) * P:(n % 2 + 1) * P], identb[:, :])
                end(i)
            k = begin(J_M2)
            for c in range(E):
                i = pe.transpose(bb(k)[:, c, :], m2r[:, c, :], identb[:, :])
            end(i)
            k = begin(J_SMB)
            pe.transpose(bb(k)[:, 0, 0:E], gw0r[:, :], identb[0:E, 0:E])
            for a in range(2):
                i = pe.transpose(bb(k)[:, 0, E * (a + 1):E * (a + 2)], m1br[:, a:2 * P:2], identb[0:E, 0:E])
            end(i)
            k = begin(J_ROW)
            pe.wait_ge(*at("csum", 2))
            pe.wait_ge(*at("prep_ev", J_W3 + 1))
            for b in range(B):
                i = mm(b4(k)[:, b, :], csB[:, b, :], w3T[:, 1, :])
            end(i)
            k = begin(J_YP)
            end(mm(bank[k][:, 0:B * M], w3T[:, 2, :], ctxT[:, :]))
            pe.wait_ge(*at("prep_ev", J_END))

            pe.wait_ge(*at("consts", NCONST))

            def turn(name):
                for g in range(G):
                    if g >= 2:
                        pe.wait_ge(*at(name + "_xte", g - 1))
                    pe.wait_ge(*at(name + "_ln", g + 1))
                    for j in range(J):
                        i = pe.transpose(b4(6 + g % 2)[:, j, :], xn[:, J * g + j, :], ident[:, :])
                    i.then_inc(sem(name + "_xt"), 1)

            def attention(name, keys, vals, q_first):
                src = queT if q_first else grpT

                def scores(g, j, first):
                    t = J * g + j
                    for q, (h0, h1) in enumerate(HEADS):
                        if not (first and j == 0):
                            pe.wait_ge(*at(name + "_sub", 3 * t - 2 + q))
                        mm(bank[q][:, 0:(h1 - h0) * M], src[:, j, :], keys[:, g, h0 * M:h1 * M]
                           ).then_inc(sem(name + "_sc"), 1)

                def turned(g, j, first, last=False):
                    t = J * g + j
                    pe.wait_ge(*(at(name + "_last", 1) if last else at(name + "_p", t + 1)))
                    for q in range(3):
                        if not first:
                            pe.wait_ge(*at(name + "_pte", 4 * t - 3 + (q if q < 2 else 3)))
                        for k in range(4 * q, min(4 * q + 4, NK)):
                            i = pe.transpose(b4(3 + q)[0:CH[k], k % 4, :], prb[:, j, k * P:k * P + CH[k]], ident[:, :])
                        i.then_inc(sem(name + "_pt"), 1)

                def values(g, j, first):
                    t = J * g + j
                    if not first:
                        pe.wait_ge(*at(name + "_x", t))
                    elif name == "a0":
                        pe.wait_ge(*at("vw_in", 32 * B))
                    for k in range(NK):
                        if k in (0, 4, 8, 9):
                            pe.wait_ge(*at(name + "_pte", 4 * t + {0: 1, 4: 2, 8: 3, 9: 4}[k]))
                        i = mm(bank[6][:, 0:D], prT[0:CH[k], j % 2, k * P:(k + 1) * P],
                               vals[0:CH[k], g, k, :], k == 0, k == NK - 1)
                    i.then_inc(sem(name + "_out"), 1)

                def group(g, first):
                    if q_first:
                        pe.wait_ge(*at(name + "_qe", g))
                        mm(bank[7][:, :], w4T[:, 0, :], xnT[:, g, :]).then_inc(sem(name + "_q"), 1)
                    for j in range(J):
                        before = (g, 0, first) if j == J - 1 else None if first else (g - 1, j + 1, False)
                        if before:
                            turned(*before)
                        if j == 0:
                            pe.wait_ge(*at(name + ("_qe" if q_first else "_gt"), g + 1))
                        scores(g, j, first)
                        if before:
                            values(*before)

                turn(name)
                pe.wait_ge(*at(name + "_xte", G))
                group(0, True)
                with pe.Fori(1, G) as g:
                    group(g, False)
                turned(G - 1, 1, False)
                values(G - 1, 1, False)
                turned(G - 1, 2, False)
                turned(G - 1, 3, False, last=True)
                values(G - 1, 2, False)
                values(G - 1, 3, False)

            attention("a0", keys0, vals0, False)

            pe.wait_ge(*at("a0_x", T))
            for g in range(G):
                pe.wait_ge(*at("f0_nrm", g + 1))
                if g >= 2:
                    pe.wait_ge(*at("f0_xte", g - 1))
                for j in range(J):
                    i = pe.transpose(bb(6 + g % 2)[:, j, :], nrm[:, J * g + j, :], identb[:, :])
                i.then_inc(sem("f0_xt"), 1)
            for g in range(G):
                pe.wait_ge(*at("f0_xte", g + 1))
                for j in range(J):
                    i = mm(bank[5][:, (J * g + j) * E:(J * g + j + 1) * E], nT[:, g, j * P:(j + 1) * P], gw0T[:, :])
            i.then_inc(sem("f0_lg"), 1)
            pe.wait_ge(*at("f0_lge", 1))

            def weight_rows(name):
                pe.wait_ge(*at(name + "_cs", 1))
                for a in range(2):
                    for t in range(8):
                        i = pe.transpose(bb(4 + a)[0:C3, t, :], Csp[:, 8 * a + t, :], identb[:, :])
                    i.then_inc(sem(name + "_ct"), 1)
                pe.wait_ge(*at(name + "_cte", 2))

            def spread(k, g, e):
                return mm(bank[k][:, :], sel[:, e, :], CT.rearrange("p (g n) -> p g n", g=G)[:, g, :])

            weight_rows("f0")

            def f0_up(g, e):
                n = E * g + e
                wait_for(pe, "f0_gv", n - 1)
                mm(bank[e % 2][:, :], m1T[:, 2 * e, :], nT[:, g, :])
                wait_for(pe, "f0_lv", n - 1)
                mm(bank[2 + e % 2][:, :], m1T[:, 2 * e + 1, :], nT[:, g, :]).then_inc(sem("f0_up"), 1)

            def f0_down(g, e):
                if e == 0:
                    wait_for(pe, "f0_ob", g)
                pe.wait_ge(*at("f0_act", E * g + e + 1))
                for j in range(J):
                    i = mm(b4(6)[:, j, :], hid[:, e % 4, j * P:(j + 1) * P], m2T[:, e, :], e == 0 and j == 0,
                           e == E - 1 and j == J - 1)
                i.then_inc(sem("f0_dn"), 1)
                if e == 0:
                    for j in range(J):
                        mm(b4(6)[:, j, :], CT.rearrange("p (t n) -> p t n", t=T)[:, J * g + j, :], m2row[:, :],
                           False, False)

            def f0_spread(g, e):
                spread(4 + e % 2, g, e).then_inc(sem("f0_sp"), 1)

            def f0_group(g, first):
                for e in range(E):
                    f0_up(g, e)
                    if e >= 3:
                        f0_down(g, e - 3)
                    elif not first:
                        f0_down(g - 1, E - 3 + e)
                    if e >= 1:
                        f0_spread(g, e - 1)
                    elif not first:
                        f0_spread(g - 1, E - 1)

            f0_group(0, True)
            with pe.Fori(1, G) as g:
                f0_group(g, False)
            f0_down(G - 1, E - 3)
            f0_spread(G - 1, E - 1)
            f0_down(G - 1, E - 2)
            f0_down(G - 1, E - 1)

            pe.wait_ge(*at("f0_x", G))
            attention("a1", keys1, vals1, True)

            pe.wait_ge(*at("a1_x", T))
            def rank(name):
                pe.wait_ge(*at(name + "_pre", 1))
                o = bank[4][:, 0:T * E]
                mm(o, lower[:, :], ohb[:, 0, :, :].rearrange("p t e -> p (t e)"), True, False)
                mm(o, onesb[:, :], ohb[:, 1, :, :].rearrange("p t e -> p (t e)"), False, True)
                mm(bank[3][:, 0:E], onesb[:, :], ohb[:, 0, T - 1, :], True, False)
                mm(bank[3][:, 0:E], onesb[:, :], ohb[:, 1, T - 1, :], False, True).then_inc(sem(name + "_rk"), 1)

            def turn_rows(name, srt, n):
                for g in range(0, n, 4):
                    pe.wait_ge(*at(f"{name}_xs{g // 4}", 16))
                    if g >= 8:
                        pe.wait_ge(*at(name + "_bte", g // 4 - 1))
                    for k in range(g, min(g + 4, n)):
                        i = pe.transpose(b4(6 + g // 4 % 2)[:, k - g, :], srt[:, k, :], ident[:, :])
                    i.then_inc(sem(name + "_bt"), 1)

            def experts1():
                def up(i, a):
                    pe.wait_ge(*at("f1_w1", 2 * i + a + 1))
                    for q in range(2):
                        if later(i):
                            pe.wait_ge(*at("f1_h", 4 * i + 2 * a + q - 3))
                        for c in range(2):
                            r = mm(bank[2 * a + q][:, c * CAP:(c + 1) * CAP],
                                   wsel1[:, a, (2 * q + c) * P:(2 * q + c + 1) * P],
                                   srtT[:, 0:T * P].rearrange("p (u n) -> p u n", n=CAP)[:, 2 * i + a, :])
                        r.then_inc(sem("f1_up"), 1)

                def down(i, a, last=False):
                    pe.wait_ge(*at("f1_w2", 2 * i + a + 1))
                    pe.wait_ge(*at("f1_h", 4 * i + 2 * a + 2))
                    if later(i):
                        pe.wait_ge(*at("f1_y", 2 * i + a - 1))
                    for r in range(2):
                        for c in range(FC):
                            x = mm(b4(4 + a)[:, r, :], hid1[:, a, c, r * P:(r + 1) * P], wsel2[:, a, c, :],
                                   c == 0, c == FC - 1)
                    x.then_inc(sem("f1_dn"), 1)

                up(0, 0)
                up(0, 1)
                down(0, 0)
                with pe.Fori(1, E // 2) as i:
                    up(i, 0)
                    down(i - 1, 1)
                    up(i, 1)
                    down(i, 0)
                down(E // 2 - 1, 1)

            def experts2():
                def up(k, a):
                    pe.wait_ge(*at("f2_w1", 2 * k + a + 1))
                    if later(k):
                        pe.wait_ge(*at("f2_h", 2 * k + a - 1))
                    for c in range(FC):
                        r = mm(b4(a)[:, c, :], wsel1[:, a, c * P:(c + 1) * P],
                               srtT[:, :].rearrange("p (k n) -> p k n", n=P)[:, k, :])
                    r.then_inc(sem("f2_up"), 1)

                def down(k, a):
                    pe.wait_ge(*at("f2_w2", 2 * k + a + 1))
                    pe.wait_ge(*at("f2_h", 2 * k + a + 1))
                    if later(k):
                        pe.wait_ge(*at("f2_y", 2 * k + a - 1))
                    for c in range(FC):
                        x = mm(bank[4 + a][:, 0:D], hid2[:, a, c, :], wsel2[:, a, c, :], c == 0, c == FC - 1)
                    x.then_inc(sem("f2_dn"), 1)

                up(0, 0)
                up(0, 1)
                down(0, 0)
                with pe.Fori(1, NBLK) as k:
                    up(k, 0)
                    down(k - 1, 1)
                    up(k, 1)
                    down(k, 0)
                down(NBLK - 1, 1)

            turn("f1")
            for t in range(T):
                if t % J == 0:
                    pe.wait_ge(*at("f1_xte", t // J + 1))
                i = mm(bank[5][:, t * E:(t + 1) * E], xnT[:, t // J, (t % J) * P:(t % J + 1) * P], wr1[:, :])
            i.then_inc(sem("f1_lg"), 1)
            rank("f1")
            turn_rows("f1", srt1, T)
            pe.wait_ge(*at("f1_bte", 4))
            experts1()

            pe.wait_ge(*at("f1_y", E))
            turn("a2")
            for g in range(G):
                pe.wait_ge(*at("a2_xte", g + 1))
                for j in range(J):
                    i = mm(b4(g)[:, j, :], xnT[:, g, j * P:(j + 1) * P], w3T[:, 0, :])
                i.then_inc(sem("a2_out"), 1)

            pe.wait_ge(*at("a2_x", G))
            rank("f2")
            turn_rows("f2", srt2, NBLK)
            pe.wait_ge(*at("f2_bte", 6))
            experts2()

            pe.wait_ge(*at("f2_y", 2 * NBLK))
            turn("a3")

            def a3_queries(g):
                pe.wait_ge(*at("a3_xte", g + 1))
                if g == G - 2:
                    pe.wait_ge(*at("a3_xte", G))
                if g >= 2:
                    pe.wait_ge(*at("a3_qe", g - 1))
                mm(bank[4 + g % 2][:, :], w3T[:, 2, :], xnT[:, g, :]).then_inc(sem("a3_q"), 1)

            def a3_scores(g):
                pe.wait_ge(*at("a3_qe", g + 1))
                if g >= 2:
                    pe.wait_ge(*at("a3_sub", g - 1))
                for j in range(J):
                    i = mm(bank[2 + g % 2][:, j * M:(j + 1) * M], que2[:, g % 2, j * P:(j + 1) * P],
                           ypT[:, g * M:(g + 1) * M])
                i.then_inc(sem("a3_sc"), 1)

            def a3_turned(g):
                pe.wait_ge(*at("a3_exp", g + 1))
                if g >= 2:
                    pe.wait_ge(*at("a3_pte", g - 1))
                for j in range(J):
                    i = pe.transpose(b4(6 + g % 2)[0:M, j, :], p3[:, g, j, :], ident[:, :])
                i.then_inc(sem("a3_pt"), 1)

            def a3_values(g):
                pe.wait_ge(*at("a3_pte", g + 1))
                if g >= 2:
                    pe.wait_ge(*at("a3_x", J * (g - 1)))
                for j in range(J):
                    i = mm(b4(g % 2)[:, j, :], prT[0:M, g % 2, j * P:(j + 1) * P], ctxr[:, g, :])
                i.then_inc(sem("a3_out"), 1)

            for s in range(G + 3):
                if s < G:
                    a3_queries(s)
                if 1 <= s <= G:
                    a3_scores(s - 1)
                if 2 <= s <= G + 1:
                    a3_turned(s - 2)
                if s >= 3:
                    a3_values(s - 3)

            pe.wait_ge(*at("a3_x", T))
            turn("f3")
            for t in range(T):
                if t % J == 0:
                    pe.wait_ge(*at("f3_xte", t // J + 1))
                i = mm(bank[5][:, t * E:(t + 1) * E], xnT[:, t // J, (t % J) * P:(t % J + 1) * P], gw3T[:, :])
            i.then_inc(sem("f3_lg"), 1)
            pe.wait_ge(*at("ld_w_l3", 16 * 6))

            def f3_up(n, s, e, g):
                if e < E:
                    pe.wait_ge(*at("f3_sx", n - G + 1))
                    src = mlpl[:, s, :]
                else:
                    src = xnT[:, g, :]
                wait_for(pe, "f3_silu", n - 1)
                mm(bank[s][:, :], w13_l3[:, e, 0:P], src)
                wait_for(pe, "f3_hd", n - 1)
                mm(bank[2 + s][:, :], w13_l3[:, e, P:2 * P], src).then_inc(sem("f3_up"), 1)

            def f3_down(n, s, e, g):
                pe.wait_ge(*at("f3_hd", n + 1))
                if e in (0, E):
                    wait_for(pe, "f3_x", g + (G if e == 0 else 0))
                for j in range(J):
                    i = mm(b4(6)[:, j, :], hid[:, s, j * P:(j + 1) * P], w2_l3[:, e, :], e in (0, E) and j == 0,
                           e >= E - 1 and j == J - 1)
                i.then_inc(sem("f3_dn"), 1)

            def f3_spread(n, s, e, g):
                spread(4 + s, g, e).then_inc(sem("f3_bc"), 1)

            f3_up(0, 0, E, 0)
            f3_up(1, 1, E, 1)
            weight_rows("f3")
            f3_spread(G, 0, 0, 0)
            f3_spread(G + 1, 1, 1, 0)
            for g in range(G):
                f3_down(g, g % 2, E, g)
                if g + 2 < G:
                    f3_up(g + 2, g % 2, E, g + 2)

            def f3_group(g, first, last):
                n = G + E * g
                for e in range(E):
                    f3_up(n + e, e % 2, e, g)
                    if e < E - 2:
                        f3_spread(n + e + 2, e % 2, e + 2, g)
                    elif not last:
                        f3_spread(n + e + 2, e % 2, e + 2 - E, g + 1)
                    if e:
                        f3_down(n + e - 1, (e - 1) % 2, e - 1, g)
                    elif not first:
                        f3_down(n - 1, (E - 1) % 2, E - 1, g - 1)

            f3_group(0, True, False)
            with pe.Fori(1, G - 1) as g:
                f3_group(g, False, False)
            f3_group(G - 1, False, True)
            f3_down(NU - 1, (E - 1) % 2, E - 1, G - 1)

        @block.scalar
        def _(act):
            job = [0]

            def ready(n):
                assert n == job[0], (n, job)
                job[0] += 1
                act.wait_ge(*at("prep_mm", n + 1))
                return n % 8

            def ev(o, i, scale=1.0, inc=True):
                x = act.activation(o, i, ACT.Copy, scale=scale)
                if inc:
                    x.then_inc(sem("prep_ev"), 1)

            k = ready(J_CTX)
            ev(ctxT[:, :], bank[k][:, 0:B * M])
            for a in range(2):
                k = ready(J_WQ + a)
                ev(wqT[:, 4 * a:4 * a + 4, :], b4(k))
            for c in range(8):
                k = ready(J_K + c)
                ev(kT[:, c, :], bank[k][:, 0:B * M])
            for h in range(H):
                k = ready(J_A + h)
                ev(keys0[:, :, h * M:(h + 1) * M], bank[k][:, 0:B * M].rearrange("p (b m) -> p b m", b=B), DH0 ** -0.5)
            k = ready(J_W4)
            ev(w4T[:, :, :], b4(k))
            for c in range(8):
                k = ready(J_V + c)
                ev(vT[:, c, :], bank[k][:, 0:B * M])
            act.wait_ge(*at("ld_cols", 64))
            k = ready(J_K1)
            act.activation(kvT1[:, 0, :], bank[k][:, 0:B * M], ACT.Identity, bias=cols[:, 1:2]
                           ).then_inc(sem("prep_ev"), 1)
            k = ready(J_V1)
            act.activation(kvT1[:, 1, :], bank[k][:, 0:B * M], ACT.Identity, bias=cols[:, 2:3]
                           ).then_inc(sem("prep_ev"), 1)
            for b in range(B):
                for q in range(4):
                    k = ready(J_VW + 4 * b + q)
                    r = HORD[4 * q]
                    ev(vstage[:, b, r:r + 7:2, :], b4(k)[0:M, :, :])
            act.wait_ge(*at("vw_out", 16 * B))
            for b in range(B):
                for q in range(3):
                    k = ready(J_VB + 3 * b + q)
                    if q < 2:
                        ev(vals1[:, b, 4 * q:4 * q + 4, :], b4(k))
                    else:
                        ev(vals1[:, b, 8, :], b4(k)[:, 0, :], inc=False)
                        ev(vals1[0:CH[9], b, 9, :], b4(k)[0:CH[9], 1, :])
            k = ready(J_W3)
            ev(w3T[:, :, :], b4(k)[:, 0:3, :])
            k = ready(J_SM)
            ev(gw3T[:, :], bank[k][:, 0:E], inc=False)
            ev(b1T[:, :], bank[k][:, E:E + E * FC])
            for a in range(2):
                k = ready(J_M1 + a)
                ev(m1T[:, 8 * a:8 * a + 8, :], bb(k))
            k = ready(J_M2)
            ev(m2T[:, :, :], bb(k))
            k = ready(J_SMB)
            ev(gw0T[:, :], bb(k)[:, 0, 0:E], inc=False)
            ev(m1bT[:, :, :].rearrange("p a e -> p (a e)"), bb(k)[:, 0, E:3 * E])
            k = ready(J_ROW)
            ev(rowc[:, :, :], b4(k), 1.0 / M)
            k = ready(J_YP)
            act.activation(ypT[:, :], bank[k][:, 0:B * M], ACT.Relu, bias=cols[:, 3:4]).then_inc(sem("prep_ev"), 1)
            act.wait_ge(*at("prep_ev", J_END))

            def turned(name):
                for g in range(G):
                    act.wait_ge(*at(name + "_xt", g + 1))
                    act.activation(xnT[:, g, :], bank[6 + g % 2][:, :], ACT.Copy).then_inc(sem(name + "_xte"), 1)

            def group_buffer(name, g, used, n):
                act.wait_ge(*at(used, n))
                act.activation(grpT[:, :, :].rearrange("p j n -> p (j n)"), xnT[:, g, :], ACT.Copy
                               ).then_inc(sem(name + "_gt"), 1)

            def attention(name, q_first):
                def exps(g, j):
                    t = J * g + j
                    act.wait_ge(*at(name + "_sub", 3 * t + 3))
                    act.activation(prb[:, j, :], prb[:, j, :], ACT.Exp).then_inc(sem(name + "_exp"), 1)

                def evac(g, j, first):
                    t = J * g + j
                    if not first:
                        act.wait_ge(*at(name + "_out", t - 1))
                    for q in range(3):
                        act.wait_ge(*at(name + "_pt", 3 * t + q + 1))
                        if q < 2:
                            act.activation(prT[:, j % 2, 4 * q * P:(4 * q + 4) * P], bank[3 + q][:, :], ACT.Copy
                                           ).then_inc(sem(name + "_pte"), 1)
                        else:
                            act.activation(prT[:, j % 2, 8 * P:9 * P], b4(5)[:, 0, :], ACT.Copy
                                           ).then_inc(sem(name + "_pte"), 1)
                            act.activation(prT[0:CH[9], j % 2, 9 * P:10 * P], b4(5)[0:CH[9], 1, :], ACT.Copy
                                           ).then_inc(sem(name + "_pte"), 1)

                def group(g, first):
                    if q_first:
                        act.wait_ge(*at(name + "_q", g + 1))
                        act.wait_ge(*at(name + "_sc", 3 * J * g))
                        act.activation(queT[:, :, :].rearrange("p j n -> p (j n)"), bank[7][:, :], ACT.Identity,
                                       bias=cols[:, 0:1]).then_inc(sem(name + "_qe"), 1)
                    else:
                        group_buffer(name, g, name + "_sc", 3 * J * g)
                    for j in range(J):
                        if j == J - 1:
                            evac(g, 0, first)
                        elif not first:
                            evac(g - 1, j + 1, False)
                        exps(g, j)

                turned(name)
                act.wait_ge(*at(name + "_xte", G))
                group(0, True)
                with act.Fori(1, G) as g:
                    group(g, False)
                for j in range(1, J):
                    evac(G - 1, j, False)

            attention("a0", False)

            for g in range(G):
                act.wait_ge(*at("f0_ln", g + 1))
                for t in range(J * g, J * (g + 1)):
                    i = act.activation(nrm[:, t, :], xc[:, t, :], ACT.Square, accum_out=gs[:, 4, t:t + 1])
                i.then_inc(sem("f0_sq"), 1)
            for g in range(G):
                act.wait_ge(*at("f0_xt", g + 1))
                act.activation(nT[:, g, :], bb(6 + g % 2)[:, 0:4, :].rearrange("p j n -> p (j n)"), ACT.Copy
                               ).then_inc(sem("f0_xte"), 1)
            act.wait_ge(*at("f0_gap", 1))
            act.activation(gs[:, 3, :], gs[:, 2, :], ACT.Exp).then_inc(sem("f0_gexp"), 1)
            act.activation(pad[:, :], ident[:, 0:1], ACT.Sigmoid)

            def weight_rows(name):
                for a in range(2):
                    act.wait_ge(*at(name + "_ct", a + 1))
                    act.activation(CT[:, 8 * P * a:8 * P * (a + 1)],
                                   bb(4 + a)[0:C3, :, :].rearrange("p j n -> p (j n)"), ACT.Copy
                                   ).then_inc(sem(name + "_cte"), 1)

            weight_rows("f0")

            def f0_unit(g, e):
                n, s = E * g + e, e % 2
                act.wait_ge(*at("f0_up", n + 1))
                wait_for(act, "f0_sg", n - 1)
                wait_for(act, "f0_gl", n - 1)
                act.activation(mlpg[:, s, :], bank[s][:, :], ACT.Identity, bias=m1bT[:, 0, e:e + 1]
                               ).then_inc(sem("f0_gv"), 1)
                wait_for(act, "f0_wl", n - 1)
                act.activation(mlpl[:, s, :], bank[2 + s][:, :], ACT.Identity, bias=m1bT[:, 1, e:e + 1]
                               ).then_inc(sem("f0_lv"), 1)
                act.wait_ge(*at("f0_gb", n + 1))
                wait_for(act, "f0_act", n - 3)
                act.activation(sig[:, e % 4, :], mlpg[:, s, :], ACT.Sigmoid, scale=ALPHA).then_inc(sem("f0_sg"), 1)

            for e in range(E):
                f0_unit(0, e)
            with act.Fori(1, G) as g:
                for e in range(E):
                    f0_unit(g, e)

            act.activation(pad[:, :], ident[:, 0:1], ACT.Exp)
            attention("a1", True)

            def gates_exp(name):
                act.wait_ge(*at(name + "_gap", 1))
                act.activation(lg[:, :, :], lg[:, :, :], ACT.Exp).then_inc(sem(name + "_gexp"), 1)

            def rows_turned(name, n):
                for g in range(0, n, 4):
                    m = min(4, n - g)
                    act.wait_ge(*at(name + "_bt", g // 4 + 1))
                    act.activation(srtT[:, g * P:(g + m) * P], bank[6 + g // 4 % 2][:, 0:m * P], ACT.Copy
                                   ).then_inc(sem(name + "_bte"), 1)

            turned("f1")
            gates_exp("f1")
            rows_turned("f1", T)

            def relu1(i, a):
                for q in range(2):
                    act.wait_ge(*at("f1_up", 4 * i + 2 * a + q + 1))
                    if later(i):
                        act.wait_ge(*at("f1_dn", 2 * i + a - 1))
                    act.activation(hid1[:, a, 2 * q:2 * q + 2, :].rearrange("p c n -> p (c n)"),
                                   bank[2 * a + q][:, :], ACT.Relu).then_inc(sem("f1_h"), 1)

            relu1(0, 0)
            relu1(0, 1)
            with act.Fori(1, E // 2) as i:
                relu1(i, 0)
                relu1(i, 1)
            turned("a2")
            rows_turned("f2", NBLK)

            def relu2(k, a):
                e = act.value_load(tabi[0:1, k, a:a + 1], min_val=0, max_val=E - 1)
                act.wait_ge(*at("f2_up", 2 * k + a + 1))
                if later(k):
                    act.wait_ge(*at("f2_dn", 2 * k + a - 1))
                for c in range(FC):
                    i = act.activation(hid2[:, a, c, :], b4(a)[:, c, :], ACT.Relu,
                                       bias=b1T[:, :].rearrange("p (e c) -> p e c", c=FC)[:, e, c:c + 1])
                i.then_inc(sem("f2_h"), 1)

            act.wait_ge(*at("tabi", 1))
            relu2(0, 0)
            relu2(0, 1)
            with act.Fori(1, NBLK) as k:
                relu2(k, 0)
                relu2(k, 1)
            turned("a3")
            for s in range(G + 3):
                if s < G:
                    g = s
                    act.wait_ge(*at("a3_q", g + 1))
                    if g >= 2:
                        act.wait_ge(*at("a3_sc", g - 1))
                    act.activation(que2[:, g % 2, :], bank[4 + g % 2][:, :], ACT.Relu,
                                   bias=cols[:, 3:4]).then_inc(sem("a3_qe"), 1)
                if 1 <= s <= G:
                    g = s - 1
                    act.wait_ge(*at("a3_gap", g + 1))
                    act.activation(p3[:, g, :, :], p3[:, g, :, :], ACT.Exp).then_inc(sem("a3_exp"), 1)
                if 2 <= s <= G + 1:
                    g = s - 2
                    act.wait_ge(*at("a3_pt", g + 1))
                    if g >= 2:
                        act.wait_ge(*at("a3_out", g - 1))
                    act.activation(prT[0:M, g % 2, 0:J * P], bank[6 + g % 2][0:M, :], ACT.Copy
                                   ).then_inc(sem("a3_pte"), 1)
            turned("f3")
            gates_exp("f3")

            def silu(n, s):
                act.wait_ge(*at("f3_up", n + 1))
                wait_for(act, "f3_hd", n - 1)
                act.activation(mlpg[:, s, :], bank[s][:, :], ACT.Silu).then_inc(sem("f3_silu"), 1)

            silu(0, 0)
            silu(1, 1)
            weight_rows("f3")
            for g in range(2, G):
                silu(g, g % 2)
            with act.Fori(0, G) as g:
                for e in range(E):
                    silu(G + E * g + e, e % 2)

        @block.vector
        def _(dve):
            def bc3(ap, shape, ax):
                return ap.unsqueeze(ax).to_broadcast(shape)

            def copy_at(o, i):
                return dve.tensor_scalar(o, i, 1.0, None, ALU.mult)

            def stats(name, g):
                for j in range(J):
                    i = dve.bn_stats(st[:, J * g + j, :], X[:, J * g + j, :])
                i.then_inc(sem(name + "_st"), 1)

            def norm(name, dst=xn):
                dve.wait_ge(*at(name + "_st", G))
                dve.tensor_tensor(nv[:, 0, :], st[:, :, 1], st[:, :, 4], ALU.add)
                dve.tensor_tensor(nv[:, 1, :], st[:, :, 1], st[:, :, 4], ALU.subtract)
                dve.tensor_tensor(nv[:, 2, :], st[:, :, 2], st[:, :, 5], ALU.add).then_inc(sem(name + "_nv"), 1)
                dve.wait_ge(*at(name + "_nv", 1))
                dve.tensor_scalar(mean[:, :], nv[:, 0, :], 0.5, None, ALU.mult)
                dve.tensor_tensor(nv[:, 3, :], nv[:, 1, :], nv[:, 1, :], ALU.mult)
                dve.tensor_scalar(nv[:, 4, :], nv[:, 2, :], 1.0 / D, LN_EPS, ALU.mult, ALU.add
                                  ).then_inc(sem(name + "_nv"), 1)
                dve.wait_ge(*at(name + "_nv", 2))
                dve.scalar_tensor_tensor(ve[:, :], nv[:, 3, :], 0.25, nv[:, 4, :], ALU.mult, ALU.add
                                         ).then_inc(sem(name + "_ve"), 1)
                if name == "a3":
                    dve.wait_ge(*at("f2_put", 16 * T))
                elif name == "f2":
                    dve.wait_ge(*at("a2_xt", G))
                elif name != "a0":
                    dve.wait_ge(*at(name + "_xt", 0))
                for g in range(G):
                    dve.wait_ge(*at(name + "_rstd", g + 1))
                    for j in range(J):
                        t = J * g + j
                        i = dve.tensor_scalar(dst[:, t, :], X[:, t, :], mean[:, t:t + 1], rstd[:, t:t + 1],
                                              ALU.subtract, ALU.mult)
                    i.then_inc(sem(name + "_ln"), 1)
            dve.wait_ge(*at("ld_x", 16))
            for g in range(G):
                stats("a0", g)
            norm("a0")

            dve.wait_ge(*at("consts", NCONST))
            dve.wait_ge(*at("prep_ev", J_CTX + 1))
            dve.tensor_reduce(csum[:, :], ctxT[:, :].rearrange("p (b m) -> p b m", b=B), AXX, ALU.add
                              ).then_inc(sem("csum"), 1)
            dve.wait_ge(*at("csum", 1))
            dve.tensor_copy(csB, bc3(csum[:, :], [P, B, P], 2)).then_inc(sem("csum"), 1)
            dve.wait_ge(*at("prep_ev", J_V1 + 1))
            dve.tensor_scalar(kvT1[:, 0, :], kvT1[:, 0, :], DH1 ** -0.5, None, ALU.mult).then_inc(sem("k1s"), 1)

            def by_head(o, src, b):
                return dve.tensor_tensor(o.rearrange("p (h m) -> p h m", h=H),
                                         bc3(src[:, b * M:(b + 1) * M], [P, H, M], 1),
                                         bc3(blk[:, :], [P, H, M], 2), ALU.mult)

            for b in range(B):
                if b >= 2:
                    dve.wait_ge(*at("prep_mm", J_VB + 3 * (b - 1)))
                by_head(vblk[:, b % 2, :], kvT1[:, 1, :], b).then_inc(sem("vblk"), 1)
            dve.wait_ge(*at("k1s", 1))
            dve.wait_ge(*at("vw_out", 16 * B))
            for b in range(B):
                by_head(keys1[:, b, :], kvT1[:, 0, :], b).then_inc(sem("keys1"), 1)
            dve.wait_ge(*at("ld_bo", 48))
            dve.wait_ge(*at("prep_ev", J_END))
            dve.wait_ge(*at("keys1", B))
            dve.tensor_tensor(rowc[:, :, :], rowc[:, :, :], bc3(boB[:, 2, :], [P, B, D], 1), ALU.add
                              ).then_inc(sem("rowc"), 1)
            dve.tensor_scalar(maskf[:, :, :], maskf[:, :, :], MASKED, None, ALU.mult).then_inc(sem("rowc"), 1)
            dve.wait_ge(*at("rowc", 2))

            def attention(name, following):
                def soft(g, j, first):
                    t = J * g + j
                    for q, (h0, h1) in enumerate(HEADS):
                        dve.wait_ge(*at(name + "_sc", 3 * t + q + 1))
                        dve.tensor_reduce(mx[:, j % 2, h0:h1],
                                          bank[q][:, 0:(h1 - h0) * M].rearrange("p (h m) -> p h m", m=M),
                                          AXX, ALU.max).then_inc(sem(name + "_mx"), 1)
                    if not first:
                        dve.wait_ge(*at(name + "_pt", 3 * (t - 3)))
                    for q, (h0, h1) in enumerate(HEADS):
                        dve.wait_ge(*at(name + "_mx", 3 * t + q + 1))
                        dve.tensor_tensor(prb[:, j, h0 * M:h1 * M].rearrange("p (h m) -> p h m", m=M),
                                          bank[q][:, 0:(h1 - h0) * M].rearrange("p (h m) -> p h m", m=M),
                                          bc3(mx[:, j % 2, h0:h1], [P, h1 - h0, M], 2),
                                          ALU.subtract).then_inc(sem(name + "_sub"), 1)

                def add(g, j):
                    t = J * g + j
                    dve.wait_ge(*at(name + "_out", t + 1))
                    if j == 0:
                        dve.wait_ge(*at(name + "_xb", g + 1))
                    dve.tensor_tensor(X[:, t, :], bank[6][:, 0:D], X[:, t, :], ALU.add).then_inc(sem(name + "_x"), 1)

                def sums(g, j, first):
                    t = J * g + j
                    dve.wait_ge(*at(name + "_exp", t + 1))
                    dve.tensor_reduce(sm[:, j % 2, :], prb[:, j, :].rearrange("p (h m) -> p h m", h=H),
                                      AXX, ALU.add).then_inc(sem(name + "_sm"), 1)
                    dve.wait_ge(*at(name + "_sm", t + 1))
                    if not (first and j < 2):
                        dve.wait_ge(*at(name + "_p", t - 1))
                    dve.reciprocal(rs[:, j % 2, :], sm[:, j % 2, :]).then_inc(sem(name + "_rs"), 1)

                def group(g, first):
                    for j in range(J):
                        if not first:
                            add(g - 1, j)
                        soft(g, j, first)
                        if j:
                            sums(g, j - 1, first)
                        elif not first:
                            sums(g - 1, J - 1, False)
                        if not first and j == J - 1:
                            dve.wait_ge(*at(name + "_x", J * g))
                            stats(following, g - 1)

                group(0, True)
                with dve.Fori(1, G) as g:
                    group(g, False)
                add(G - 1, 0)
                sums(G - 1, J - 1, False)
                dve.wait_ge(*at(name + "_rs", T))
                dve.tensor_tensor(prb[:, J - 1, :].rearrange("p (h m) -> p h m", h=H),
                                  prb[:, J - 1, :].rearrange("p (h m) -> p h m", h=H),
                                  bc3(rs[:, (J - 1) % 2, :], [P, H, M], 2), ALU.mult).then_inc(sem(name + "_last"), 1)
                for j in range(1, J):
                    add(G - 1, j)
                dve.wait_ge(*at(name + "_x", T))
                stats(following, G - 1)

            attention("a0", "f0")

            def grp(tile, g):
                return tile.rearrange("p (g j) d -> p g (j d)", g=G)[:, g, :].rearrange("p (j d) -> p j d", j=J)

            dve.wait_ge(*at("ld_later", 112))

            def top(c, src, dst, m):
                c(dve.tensor_reduce(gs[:, m, :], src, AXX, ALU.max))
                c(dve.tensor_tensor(tA[:, :, :], src, bc3(gs[:, m, :], [P, T, E], 2), ALU.is_equal))
                c(dve.tensor_tensor(tA[:, :, :], tA[:, :, :], bc3(iota[:, :], [P, T, E], 1), ALU.mult))
                c(dve.tensor_reduce(gs[:, 11, :], tA[:, :, :], AXX, ALU.min))
                c(dve.tensor_tensor(dst, bc3(iota[:, :], [P, T, E], 1), bc3(gs[:, 11, :], [P, T, E], 2), ALU.is_equal))

            def top_two(c, src, m):
                top(c, src, oh[:, 0, :, :], m)
                c(dve.scalar_tensor_tensor(lg2[:, :, :], oh[:, 0, :, :], MASKED, src, ALU.mult, ALU.add))
                top(c, lg2[:, :, :], oh[:, 1, :, :], m + 1)

            c = Steps(dve, sem("f0_c"))

            norm("f0", xc)
            for g in range(G):
                dve.wait_ge(*at("f0_sq", g + 1))
                dve.tensor_scalar(gs[:, 0, J * g:J * (g + 1)], gs[:, 4, J * g:J * (g + 1)], 1.0 / D, LN_EPS,
                                  ALU.mult, ALU.add).then_inc(sem("f0_ms"), 1)
            for g in range(G):
                dve.wait_ge(*at("f0_rms", g + 1))
                for j in range(J):
                    t = J * g + j
                    i = dve.scalar_tensor_tensor(nrm[:, t, :], xc[:, t, :], gs[:, 1, t:t + 1], nwB[:, :],
                                                 ALU.mult, ALU.mult)
                i.then_inc(sem("f0_nrm"), 1)
            dve.wait_ge(*at("f0_lg", 1))
            c(dve.tensor_tensor(lgb[:, :, :], bank[5][:, 0:T * E].rearrange("p (t e) -> p t e", t=T),
                                bc3(gbB[:, :], [P, T, E], 1), ALU.add))
            dve.tensor_copy(lg[:, :, :], lgb[:, :, :]).then_inc(sem("f0_lge"), 1)
            dve.wait_ge(*at("f0_lge", 1))
            top_two(c, lg[:, :, :], 5)
            dve.tensor_tensor(gs[:, 2, :], gs[:, 6, :], gs[:, 5, :], ALU.subtract).then_inc(sem("f0_gap"), 1)
            dve.wait_ge(*at("f0_gexp", 1))
            c(dve.tensor_scalar(gs[:, 7, :], gs[:, 3, :], 1.0, None, ALU.add))
            c(dve.reciprocal(gs[:, 8, :], gs[:, 7, :]))
            c(dve.tensor_tensor(gs[:, 9, :], gs[:, 8, :], gs[:, 3, :], ALU.mult))
            for a in range(2):
                i = dve.tensor_tensor(oh[:, a, :, :], oh[:, a, :, :], bc3(gs[:, 8 + a, :], [P, T, E], 2), ALU.mult)
            c(i)
            c(dve.tensor_tensor(C[:, :, :], oh[:, 0, :, :], oh[:, 1, :, :], ALU.add))

            def split(name, c):
                c(dve.tensor_copy(Csp[:, :, 0:E], C[:, :, :]))
                c(dve.tensor_tensor(Cr[:, :, :], C[:, :, :], Csp[:, :, 0:E], ALU.subtract))
                c(dve.tensor_copy(Csp[:, :, E:2 * E], Cr[:, :, :]))
                c(dve.tensor_tensor(Cr[:, :, :], Cr[:, :, :], Csp[:, :, E:2 * E], ALU.subtract))
                dve.tensor_copy(Csp[:, :, 2 * E:3 * E], Cr[:, :, :]).then_inc(sem(name + "_cs"), 1)

            split("f0", c)

            def f0_clamped(g, e):
                n, s = E * g + e, e % 2
                dve.wait_ge(*at("f0_gv", n + 1))
                dve.tensor_scalar(mlpg[:, s, :], mlpg[:, s, :], LIMIT, None, ALU.min).then_inc(sem("f0_gb"), 1)
                dve.wait_ge(*at("f0_lv", n + 1))
                dve.tensor_scalar(mlpl[:, s, :], mlpl[:, s, :], -LIMIT, LIMIT, ALU.max, ALU.min
                                  ).then_inc(sem("f0_lb"), 1)

            def f0_product(g, e):
                n, s = E * g + e, e % 2
                dve.wait_ge(*at("f0_gb", n + 1))
                dve.wait_ge(*at("f0_lb", n + 1))
                dve.scalar_tensor_tensor(mlpl[:, s, :], mlpl[:, s, :], 1.0, mlpg[:, s, :], ALU.add, ALU.mult
                                         ).then_inc(sem("f0_gl"), 1)

            def f0_weighted(g, e):
                n, s = E * g + e, e % 2
                dve.wait_ge(*at("f0_sp", n + 1))
                dve.wait_ge(*at("f0_gl", n + 1))
                wait_for(dve, "f0_dn", n - 3)
                dve.tensor_tensor(hid[:, e % 4, :], mlpl[:, s, :], bank[4 + s][:, :], ALU.mult
                                  ).then_inc(sem("f0_wl"), 1)

            def f0_sum(g):
                dve.wait_ge(*at("f0_dn", E * (g + 1)))
                c = Steps(dve, sem("f0_fin"), g)
                dve.tensor_scalar(accb[:, :, :], b4(6), 1.0, None, ALU.mult).then_inc(sem("f0_ob"), 1)
                dve.wait_ge(*at("f0_ob", g + 1))
                c(dve.tensor_tensor(accb[:, :, :], accb[:, :, :], grp(xc[:, :, :], g), ALU.add))
                dve.tensor_tensor(grp(X[:, :, :], g), accb[:, :, :], grp(X[:, :, :], g), ALU.add
                                  ).then_inc(sem("f0_x"), 1)

            def f0_group(g, first):
                for e in range(E):
                    if e == 3 and not first:
                        f0_sum(g - 1)
                    f0_clamped(g, e)
                    if e:
                        f0_weighted(g, e - 1)
                    elif not first:
                        f0_weighted(g - 1, E - 1)
                    f0_product(g, e)

            f0_group(0, True)
            with dve.Fori(1, G) as g:
                f0_group(g, False)
            f0_weighted(G - 1, E - 1)
            f0_sum(G - 1)

            for g in range(G):
                dve.wait_ge(*at("f0_x", g + 1))
                stats("a1", g)
            norm("a1")
            attention("a1", "f1")

            def gates(name, c):
                dve.wait_ge(*at(name + "_lg", 1))
                dve.tensor_copy(lg[:, :, :], bank[5][:, 0:T * E].rearrange("p (t e) -> p t e", t=T)
                                ).then_inc(sem(name + "_lge"), 1)
                dve.wait_ge(*at(name + "_lge", 1))
                c(dve.tensor_reduce(gs[:, 0, :], lg[:, :, :], AXX, ALU.max))
                dve.tensor_tensor(lg[:, :, :], lg[:, :, :], bc3(gs[:, 0, :], [P, T, E], 2), ALU.subtract
                                  ).then_inc(sem(name + "_gap"), 1)
                dve.wait_ge(*at(name + "_gexp", 1))
                c(dve.tensor_reduce(gs[:, 0, :], lg[:, :, :], AXX, ALU.add))
                c(dve.reciprocal(gs[:, 1, :], gs[:, 0, :]))
                c(dve.tensor_tensor(lg[:, :, :], lg[:, :, :], bc3(gs[:, 1, :], [P, T, E], 2), ALU.mult))

            def ranks(name, c):
                c(dve.tensor_copy(pre[:, 0, E:, :], oh[:, 0, :, :]))
                for n, shift in enumerate((1, 2, 4, 8)):
                    a, b = n % 2, (n + 1) % 2
                    c(dve.tensor_tensor(pre[:, b, E:, :], pre[:, a, E:, :], pre[:, a, E - shift:E + T - shift, :],
                                        ALU.add))
                dve.tensor_copy(ohb[:, 0, :, :], oh[:, 0, :, :])
                dve.tensor_tensor(ohb[:, 1, :, :], pre[:, 0, E:, :], oh[:, 0, :, :], ALU.subtract
                                  ).then_inc(sem(name + "_pre"), 1)
                dve.wait_ge(*at(name + "_rk", 1))
                dve.tensor_copy(tot[:, :], bank[3][:, 0:E])
                c(dve.tensor_copy(tA[:, :, :], bank[4][:, 0:T * E].rearrange("p (t e) -> p t e", t=T)))

            def chosen(c, m):
                c(dve.tensor_tensor(tA[:, :, :], tA[:, :, :], oh[:, 0, :, :], ALU.mult))
                c(dve.tensor_reduce(gs[:, m, :], tA[:, :, :], AXX, ALU.add))

            def summed(name, g, weight):
                dve.wait_ge(*at(f"{name}_got{g}", 16 * J))
                for j in range(J):
                    t = J * g + j
                    i = dve.scalar_tensor_tensor(X[:, t, :], back[:, t, :], weight(t), X[:, t, :], ALU.mult, ALU.add)
                i.then_inc(sem(name + "_add"), 1)
                dve.wait_ge(*at(name + "_add", g + 1))

            norm("f1")
            c = Steps(dve, sem("f1_c"))
            gates("f1", c)
            top(c, lg[:, :, :], oh[:, 0, :, :], 2)
            ranks("f1", c)
            chosen(c, 3)
            c(dve.tensor_scalar(gs[:, 4, :], gs[:, 3, :], float(CAP), None, ALU.is_lt))
            c(dve.tensor_scalar(gs[:, 5, :], gs[:, 11, :], float(E), float(CAP), ALU.add, ALU.mult))
            c(dve.tensor_tensor(gs[:, 6, :], gs[:, 5, :], gs[:, 3, :], ALU.add))
            c(dve.tensor_tensor(gs[:, 9, :], gs[:, 4, :], gs[:, 2, :], ALU.mult))
            c(dve.tensor_scalar(idx[:, 1, :], gs[:, 6, :], T * P - 1.0, None, ALU.min))
            c(dve.tensor_tensor(gs[:, 6, :], gs[:, 6, :], tok[:, :], ALU.subtract))
            c(dve.tensor_tensor(gs[:, 6, :], gs[:, 6, :], gs[:, 4, :], ALU.mult))
            dve.tensor_tensor(idx[:, 0, :], gs[:, 6, :], tok[:, :], ALU.add).then_inc(sem("f1_idx"), 1)

            dve.wait_ge(*at("ld_w1_l1", 16))
            dve.wait_ge(*at("ld_w2_l1", 16))

            def weights1(i, a):
                if later(i):
                    dve.wait_ge(*at("f1_up", 4 * i + 2 * a - 2))
                copy_at(wsel1[:, a, :], w1_l1[:, 2 * i + a, :]).then_inc(sem("f1_w1"), 1)
                if later(i):
                    dve.wait_ge(*at("f1_dn", 2 * i + a - 1))
                copy_at(wsel2[:, a, :, :], w2_l1[:, 2 * i + a, :, :]).then_inc(sem("f1_w2"), 1)

            def result1(i, a):
                dve.wait_ge(*at("f1_dn", 2 * i + a + 1))
                copy_at(res1.rearrange("p (u r) d -> p u r d", r=2)[:, 2 * i + a, :, :], b4(4 + a)[:, 0:2, :]
                        ).then_inc(sem("f1_y"), 1)

            weights1(0, 0)
            weights1(0, 1)
            with dve.Fori(1, E // 2) as i:
                weights1(i, 0)
                result1(i - 1, 0)
                weights1(i, 1)
                result1(i - 1, 1)
            result1(E // 2 - 1, 0)
            result1(E // 2 - 1, 1)
            for g in range(G):
                summed("f1", g, lambda t: gs[:, 9, t:t + 1])
                stats("a2", g)
            norm("a2")
            for g in range(G):
                dve.wait_ge(*at("a2_out", g + 1))
                dve.wait_ge(*at("a2_xb", g + 1))
                dve.tensor_tensor(grp(X[:, :, :], g), b4(g), grp(X[:, :, :], g), ALU.add).then_inc(sem("a2_x"), 1)
                dve.wait_ge(*at("a2_x", g + 1))
                stats("f2", g)
            norm("f2")
            dve.wait_ge(*at("f2_ln", G))
            c = Steps(dve, sem("f2_c"))
            c(dve.tensor_tensor(gs[:, 0, :], xn[:, :, 0], xn[:, :, 1], ALU.add))
            c(dve.tensor_scalar(gs[:, 1, :], gs[:, 0, :], -1.0, None, ALU.mult))
            c(dve.tensor_tensor(gs[:, 1, :], gs[:, 0, :], gs[:, 1, :], ALU.max))
            c(dve.tensor_copy(gi[:, :], gs[:, 1, :]))
            c(dve.tensor_copy(gs[:, 2, :], gi[:, :]))
            c(dve.tensor_tensor(gs[:, 3, :], gs[:, 2, :], gs[:, 1, :], ALU.is_gt))
            c(dve.tensor_tensor(gs[:, 2, :], gs[:, 2, :], gs[:, 3, :], ALU.subtract))
            c(dve.tensor_scalar(gs[:, 3, :], gs[:, 0, :], 0.0, 2.0, ALU.is_ge, ALU.mult))
            c(dve.tensor_scalar(gs[:, 3, :], gs[:, 3, :], -1.0, None, ALU.add))
            c(dve.tensor_tensor(gs[:, 2, :], gs[:, 2, :], gs[:, 3, :], ALU.mult))
            assert E & (E - 1) == 0
            c(dve.tensor_copy(gi[:, :], gs[:, 2, :]))
            c(dve.tensor_scalar(gi[:, :], gi[:, :], E - 1, None, ALU.bitwise_and))
            c(dve.tensor_scalar(gs[:, 2, :], gi[:, :], -float(E), None, ALU.add))
            c(dve.tensor_tensor(oh[:, 0, :, :], bc3(iota[:, :], [P, T, E], 1), bc3(gs[:, 2, :], [P, T, E], 2),
                                ALU.is_equal))
            ranks("f2", c)
            c(dve.tensor_tensor(cmp[:, :, 0:T], bc3(tot[:, :], [P, E, T], 2), bc3(thr[:, :], [P, E, T], 1), ALU.is_gt))
            c(dve.tensor_reduce(nblk[:, 0, :], cmp[:, :, 0:T], AXX, ALU.add))
            c(dve.tensor_tensor(cmp[:, :, 0:E], lowE[:, :, :], bc3(nblk[:, 0, :], [P, E, E], 1), ALU.mult))
            c(dve.tensor_reduce(nblk[:, 1, :], cmp[:, :, 0:E], AXX, ALU.add))
            c(dve.tensor_tensor(nblk[:, 2, :], nblk[:, 1, :], nblk[:, 0, :], ALU.add))
            c(dve.tensor_scalar(nblk[:, 1, :], nblk[:, 1, :], float(P), None, ALU.mult))
            c(dve.tensor_tensor(tA[:, :, :], tA[:, :, :], bc3(nblk[:, 1, :], [P, T, E], 1), ALU.add))
            chosen(c, 4)
            dve.tensor_copy(idx[:, 1, :], gs[:, 4, :])
            dve.tensor_copy(idx[:, 0, :], gs[:, 4, :]).then_inc(sem("f2_idx"), 1)
            c(dve.tensor_tensor(blkc[:, :, :], bc3(kio[:, 0:NBLK], [P, NBLK, E], 2),
                                bc3(nblk[:, 2, :], [P, NBLK, E], 1), ALU.is_ge))
            c(dve.tensor_reduce(tab[:, 0, :], blkc[:, :, :], AXX, ALU.add))
            c(dve.tensor_scalar(tab[:, 0, :], tab[:, 0, :], E - 1.0, None, ALU.min))
            c(dve.tensor_scalar(tab[:, 1, :], tab[:, 0, :], E - 1.0, -float(E), ALU.is_equal, ALU.mult))
            c(dve.scalar_tensor_tensor(tab[:, 1, :], tab[:, 0, :], 1.0, tab[:, 1, :], ALU.add, ALU.add))
            dve.tensor_copy(tabi[:, :, 0], tab[:, 0, :])
            dve.tensor_copy(tabi[:, :, 1], tab[:, 1, :]).then_inc(sem("tabi"), 1)
            dve.wait_ge(*at("tabi", 1))

            dve.wait_ge(*at("ld_w2_l2", 16))
            dve.wait_ge(*at("b2p", E + 1))

            def second2(k, a):
                e = dve.value_load(tabi[0:1, k, a:a + 1], min_val=0, max_val=E - 1)
                if later(k):
                    dve.wait_ge(*at("f2_dn", 2 * k + a - 1))
                copy_at(wsel2[:, a, :, :], w2_l2[:, e, :, :]).then_inc(sem("f2_w2"), 1)
                if a == 0:
                    copy_at(res2[:, k, :], b2pair[:, e, :]).then_inc(sem("f2_bi"), 1)

            def result2(k, a):
                dve.wait_ge(*at("f2_dn", 2 * k + a + 1))
                if a == 0:
                    dve.wait_ge(*at("f2_bi", k + 1))
                else:
                    dve.wait_ge(*at("f2_y", 2 * k + 1))
                dve.tensor_tensor(res2[:, k, :], bank[4 + a][:, 0:D], res2[:, k, :], ALU.add
                                  ).then_inc(sem("f2_y"), 1)

            second2(0, 0)
            second2(0, 1)
            with dve.Fori(1, NBLK) as k:
                second2(k, 0)
                result2(k - 1, 0)
                second2(k, 1)
                result2(k - 1, 1)
            result2(NBLK - 1, 0)
            result2(NBLK - 1, 1)

            for g in range(G):
                summed("f2", g, lambda t: 0.5)
                stats("a3", g)
            norm("a3")
            def a3_gaps(g):
                p, m = p3[:, g, :, :], 3 * (g % 2)
                dve.wait_ge(*at("a3_sc", g + 1))
                dve.tensor_tensor(p, bank[2 + g % 2][:, 0:J * M].rearrange("p (j m) -> p j m", j=J),
                                  bc3(maskf[:, g, :], [P, J, M], 1), ALU.add).then_inc(sem("a3_sub"), 1)
                dve.wait_ge(*at("a3_sub", g + 1))
                c(dve.tensor_reduce(gs[:, m, 0:J], p, AXX, ALU.max))
                dve.tensor_tensor(p, p, bc3(gs[:, m, 0:J], [P, J, M], 2), ALU.subtract).then_inc(sem("a3_gap"), 1)

            def a3_sums(g):
                m = 3 * (g % 2)
                dve.wait_ge(*at("a3_exp", g + 1))
                c(dve.tensor_reduce(gs[:, m + 1, 0:J], p3[:, g, :, :], AXX, ALU.add))
                c(dve.reciprocal(gs[:, m + 2, 0:J], gs[:, m + 1, 0:J]))

            def a3_add(g):
                dve.wait_ge(*at("a3_out", g + 1))
                for j in range(J):
                    dve.scalar_tensor_tensor(X[:, J * g + j, :], b4(g % 2)[:, j, :],
                                             gs[:, 3 * (g % 2) + 2, j:j + 1], X[:, J * g + j, :],
                                             ALU.mult, ALU.add).then_inc(sem("a3_x"), 1)
                dve.wait_ge(*at("a3_x", J * (g + 1)))
                stats("f3", g)

            c = Steps(dve, sem("a3_c"))
            for g in range(G + 2):
                if g < G:
                    a3_gaps(g)
                if 1 <= g <= G:
                    a3_sums(g - 1)
                if g >= 2:
                    a3_add(g - 2)

            norm("f3")
            c = Steps(dve, sem("f3_ch"))
            gates("f3", c)
            top_two(c, lg[:, :, :], 2)
            c(dve.tensor_tensor(oh[:, 0, :, :], oh[:, 0, :, :], oh[:, 1, :, :], ALU.add))
            c(dve.tensor_tensor(C[:, :, :], oh[:, 0, :, :], lg[:, :, :], ALU.mult))
            split("f3", c)

            def f3_hidden(n, s):
                dve.wait_ge(*at("f3_silu", n + 1))
                wait_for(dve, "f3_dn", n - 1)
                dve.tensor_tensor(hid[:, s, :], mlpg[:, s, :], bank[2 + s][:, :], ALU.mult
                                  ).then_inc(sem("f3_hd"), 1)

            def f3_sum(n, g, k):
                dve.wait_ge(*at("f3_dn", n))
                if k >= G or not isinstance(k, int):
                    dve.wait_ge(*at("f3_x", G))
                dve.tensor_tensor(grp(X[:, :, :], g), b4(6), grp(X[:, :, :], g), ALU.add
                                  ).then_inc(sem("f3_x"), 1)

            def f3_scaled(n, s, g):
                dve.wait_ge(*at("f3_bc", n - G + 1))
                wait_for(dve, "f3_up", n - 1)
                dve.tensor_tensor(mlpl[:, s, :], xnT[:, g, :], bank[4 + s][:, :], ALU.mult
                                  ).then_inc(sem("f3_sx"), 1)

            for g in range(G):
                f3_hidden(g, g % 2)
                if g:
                    f3_sum(g, g - 1, 0)
            f3_scaled(G, 0, 0)
            f3_scaled(G + 1, 1, 0)
            f3_sum(G, G - 1, 0)

            def f3_group(g, first, last):
                n = G + E * g
                for e in range(E):
                    f3_hidden(n + e, e % 2)
                    if e < E - 2:
                        f3_scaled(n + e + 2, e % 2, g)
                    elif not last:
                        f3_scaled(n + e + 2, e % 2, g + 1)
                    if e == 0 and not first:
                        f3_sum(n, g - 1, G)

            f3_group(0, True, False)
            with dve.Fori(1, G - 1) as g:
                f3_group(g, False, False)
            f3_group(G - 1, False, True)
            f3_sum(NU, G - 1, G)


_INS = ['x', 'ctx_1024', 'mask_BxS2_bk0', 'L0_xattn_Wq', 'L0_xattn_Wk', 'L0_xattn_Wv', 'L0_xattn_Wo', 'L0_xattn_bo',
        'L0_ffn_norm_weight', 'L0_ffn_gate_weight', 'L0_ffn_gate_bias', 'L0_ffn_mlp1_weight', 'L0_ffn_mlp1_bias',
        'L0_ffn_mlp2_weight', 'L0_ffn_mlp2_bias', 'L1_xattn_wq_w', 'L1_xattn_wq_b', 'L1_xattn_wk_w', 'L1_xattn_wk_b',
        'L1_xattn_wv_w', 'L1_xattn_wv_b', 'L1_xattn_dense_w', 'L1_xattn_dense_b', 'L1_ffn_Wr', 'L1_ffn_W1',
        'L1_ffn_W2', 'L2_xattn_W', 'L2_xattn_b', 'L2_ffn_W1', 'L2_ffn_b1', 'L2_ffn_W2', 'L2_ffn_b2', 'L3_xattn_W',
        'L3_xattn_b', 'L3_ffn_gate_w', 'L3_ffn_w1', 'L3_ffn_w2', 'L3_ffn_w3', 'L3_ffn_w1s', 'L3_ffn_w2s', 'L3_ffn_w3s']


def kernel(**inputs):
    import concourse.bacc as _bacc
    from concourse.bass_utils import run_bass_kernel_spmd as _run

    nc = _bacc.Bacc("TRN2", target_bir_lowering=False, num_devices=1)
    arrays, args = {}, {}
    for name in _INS:
        a = np.ascontiguousarray(inputs[name])
        if a.dtype == np.bool_:
            a = a.reshape(-1).view(np.int32)
        arrays["in_" + name] = a
        args[name] = nc.dram_tensor("in_" + name, a.shape, mybir.dt.from_np(a.dtype), kind="ExternalInput").ap()
    out = nc.dram_tensor("out_0", (B, SEQ, D), F32, kind="ExternalOutput").ap()
    build(nc, args, out)
    r = _run(nc, [arrays], core_ids=[0])
    return r.results[0]["out_0"]
```
